# Optimizing a Trainium2 kernel written in Bass

```python
import numpy as np
import jax
import jax.numpy as jnp

def _softmax(x, axis=-1):
    return jax.nn.softmax(x, axis=axis)

def _gelu(x):
    return jax.nn.gelu(x, approximate=True)

def _silu(x):
    return jax.nn.silu(x)

def _sigmoid(x):
    return jax.nn.sigmoid(x)

def _layernorm(x, axis=-1, eps=1e-05):
    m = jnp.mean(x, axis=axis, keepdims=True)
    v = jnp.var(x, axis=axis, keepdims=True)
    return (x - m) / jnp.sqrt(v + eps)

def _scatter_add(tgt, idx, src, axis=0):
    return tgt.at[idx].add(src)

def _segment_sum(src, seg, n):
    return jax.ops.segment_sum(src, seg, n)
kernel_name = 'mk_gnn_ffn_d1_gnn_r8_df8bc1'

def setup_inputs(seed: int=0):
    np.random.seed(seed)
    _w = jnp.asarray

    def _rec_inputs():
        import jax
        import jax.numpy as jnp
        _gk = jax.random.key(seed)
        x = -0.0001126 + 1 * jax.random.normal(jax.random.fold_in(_gk, 1), (1250, 768), jnp.float32)
        src = jax.random.randint(jax.random.fold_in(_gk, 2), (40000,), 0, 1250, jnp.int32)
        dst = jnp.minimum((1250 * jax.random.uniform(jax.random.fold_in(_gk, 3), (40000,)) ** 2.0).astype(jnp.int32), 9999)
        _o = jnp.argsort(dst, stable=True)
        src = src[_o]
        dst = dst[_o]
        return (x, src, dst)
    x, src, dst = _rec_inputs()

    def _L0_gnn_setup():
        import jax, jax.numpy as jnp
        import numpy as np
        N = 1250
        E = 20000
        D = 768
        H1, C1 = (4, 192)
        H2, C2 = (2, 96)
        EPS = 1e-05
        NEG_SLOPE = 0.2

        def layer_norm(x, g, b):
            mu = x.mean(-1, keepdims=True)
            var = ((x - mu) ** 2).mean(-1, keepdims=True)
            return (x - mu) * jax.lax.rsqrt(var + EPS) * g + b

        def gat_conv(x, src, dst, W, a_src, a_dst, bias, H, C, n):
            h = (x @ W).reshape(n, H, C)
            s_src = (h * a_src).sum(-1)
            s_dst = (h * a_dst).sum(-1)
            e = jax.nn.leaky_relu(s_src[src] + s_dst[dst], NEG_SLOPE)
            emax = jax.ops.segment_max(e, dst, num_segments=n)
            ee = jnp.exp(e - emax[dst])
            denom = jax.ops.segment_sum(ee, dst, num_segments=n)
            alpha = ee / denom[dst]
            out = jax.ops.segment_sum(alpha[:, :, None] * h[src], dst, num_segments=n)
            return out.reshape(n, H * C) + bias
        key = jax.random.key(seed)
        ks = jax.random.split(key, 16)
        sd = 1.0 / np.sqrt(D)
        inp = {'x': jax.random.normal(ks[0], (N, D), jnp.float32), 'edge_index': jax.random.randint(ks[1], (2, E), 0, N, jnp.int64), 'norm_g': jnp.ones((D,), jnp.float32), 'norm_b': jnp.zeros((D,), jnp.float32), 'W1': jax.random.normal(ks[2], (D, H1 * C1), jnp.float32) * sd, 'a_src1': jax.random.normal(ks[3], (H1, C1), jnp.float32) * sd, 'a_dst1': jax.random.normal(ks[4], (H1, C1), jnp.float32) * sd, 'b1': jnp.zeros((H1 * C1,), jnp.float32), 'W2': jax.random.normal(ks[5], (H1 * C1, H2 * C2), jnp.float32) * sd, 'a_src2': jax.random.normal(ks[6], (H2, C2), jnp.float32) * sd, 'a_dst2': jax.random.normal(ks[7], (H2, C2), jnp.float32) * sd, 'b2': jnp.zeros((H2 * C2,), jnp.float32), 'Wu': jax.random.normal(ks[8], (D + H2 * C2, D), jnp.float32) / np.sqrt(D + H2 * C2), 'bu': jnp.zeros((D,), jnp.float32)}
        return inp
    _L0_gnn_all = _L0_gnn_setup()
    _L0_gnn_in = {k: v for k, v in _L0_gnn_all.items() if k in ('norm_g', 'norm_b', 'W1', 'a_src1', 'a_dst1', 'b1', 'W2', 'a_src2', 'a_dst2', 'b2', 'Wu', 'bu')}
    del _L0_gnn_all

    def _L0_ffn_setup():
        import jax, jax.numpy as jnp
        import numpy as np
        H = 768
        I = 384
        E = 16
        G = 4
        TOPK_GROUP = 2
        TOP_K = 4
        SCALE = 2.5
        N_SHARED = 2
        IS = I * N_SHARED
        B, S = (1, 256)

        def _route(x, router_w, router_b, corr_bias):
            logits = x.astype(jnp.float32) @ router_w.T + router_b
            scores = jax.nn.sigmoid(logits)
            sfc = scores + corr_bias[None, :]
            grp = sfc.reshape(-1, G, E // G)
            group_scores = jax.lax.top_k(grp, 2)[0].sum(-1)
            _, gidx = jax.lax.top_k(group_scores, TOPK_GROUP)
            gmask = jax.nn.one_hot(gidx, G, dtype=sfc.dtype).sum(axis=1)
            score_mask = jnp.repeat(gmask, E // G, axis=-1)
            sfc = jnp.where(score_mask > 0, sfc, 0.0)
            _, idx = jax.lax.top_k(sfc, TOP_K)
            w = jnp.take_along_axis(scores, idx, axis=1)
            w = w / (w.sum(-1, keepdims=True) + 1e-20)
            return (idx, w * SCALE)

        def _forward(x3, router_w, router_b, corr_bias, gWg, gbg, gWu, gbu, gWd, gbd, sWg, sbg, sWu, sbu, sWd, sbd):
            orig_shape = x3.shape
            x = x3.reshape(-1, H)
            idx, w = _route(x, router_w, router_b, corr_bias)
            c = (jax.nn.one_hot(idx, E, dtype=w.dtype) * w[..., None]).sum(1)
            h = jax.nn.silu(jnp.einsum('th,ehi->tei', x, gWg) + gbg) * (jnp.einsum('th,ehi->tei', x, gWu) + gbu)
            out_e = jnp.einsum('tei,eih->teh', h, gWd) + gbd
            moe_out = jnp.einsum('te,teh->th', c, out_e)
            hs = jax.nn.silu(x @ sWg + sbg) * (x @ sWu + sbu)
            shared = hs @ sWd + sbd
            return (moe_out + shared).reshape(orig_shape)
        key = jax.random.key(seed)
        ks = jax.random.split(key, 16)
        s = lambda k, shape, fan: jax.random.normal(k, shape, jnp.float32) * fan ** (-0.5)
        return {'hidden_states': jax.random.normal(ks[0], (B, S, H), jnp.float32), 'router_w': s(ks[1], (E, H), H), 'router_b': jnp.zeros((E,), jnp.float32), 'corr_bias': jnp.zeros((E,), jnp.float32), 'gWg': s(ks[2], (E, H, I), H), 'gbg': jnp.zeros((E, I), jnp.float32), 'gWu': s(ks[3], (E, H, I), H), 'gbu': jnp.zeros((E, I), jnp.float32), 'gWd': s(ks[4], (E, I, H), I), 'gbd': jnp.zeros((E, H), jnp.float32), 'sWg': s(ks[5], (H, IS), H), 'sbg': jnp.zeros((IS,), jnp.float32), 'sWu': s(ks[6], (H, IS), H), 'sbu': jnp.zeros((IS,), jnp.float32), 'sWd': s(ks[7], (IS, H), IS), 'sbd': jnp.zeros((H,), jnp.float32)}
    _L0_ffn_all = _L0_ffn_setup()
    _L0_ffn_in = {k: v for k, v in _L0_ffn_all.items() if k in ('router_w', 'router_b', 'corr_bias', 'gWg', 'gbg', 'gWu', 'gbu', 'gWd', 'gbd', 'sWg', 'sbg', 'sWu', 'sbu', 'sWd', 'sbd')}
    del _L0_ffn_all
    return {'x': x, 'src': src, 'dst': dst, 'L0_gnn_norm_g': _L0_gnn_in['norm_g'], 'L0_gnn_norm_b': _L0_gnn_in['norm_b'], 'L0_gnn_W1': _L0_gnn_in['W1'], 'L0_gnn_a_src1': _L0_gnn_in['a_src1'], 'L0_gnn_a_dst1': _L0_gnn_in['a_dst1'], 'L0_gnn_b1': _L0_gnn_in['b1'], 'L0_gnn_W2': _L0_gnn_in['W2'], 'L0_gnn_a_src2': _L0_gnn_in['a_src2'], 'L0_gnn_a_dst2': _L0_gnn_in['a_dst2'], 'L0_gnn_b2': _L0_gnn_in['b2'], 'L0_gnn_Wu': _L0_gnn_in['Wu'], 'L0_gnn_bu': _L0_gnn_in['bu'], 'L0_ffn_router_w': _L0_ffn_in['router_w'], 'L0_ffn_router_b': _L0_ffn_in['router_b'], 'L0_ffn_corr_bias': _L0_ffn_in['corr_bias'], 'L0_ffn_gWg': _L0_ffn_in['gWg'], 'L0_ffn_gbg': _L0_ffn_in['gbg'], 'L0_ffn_gWu': _L0_ffn_in['gWu'], 'L0_ffn_gbu': _L0_ffn_in['gbu'], 'L0_ffn_gWd': _L0_ffn_in['gWd'], 'L0_ffn_gbd': _L0_ffn_in['gbd'], 'L0_ffn_sWg': _L0_ffn_in['sWg'], 'L0_ffn_sbg': _L0_ffn_in['sbg'], 'L0_ffn_sWu': _L0_ffn_in['sWu'], 'L0_ffn_sbu': _L0_ffn_in['sbu'], 'L0_ffn_sWd': _L0_ffn_in['sWd'], 'L0_ffn_sbd': _L0_ffn_in['sbd']}

def reference(x, src, dst, L0_gnn_norm_g, L0_gnn_norm_b, L0_gnn_W1, L0_gnn_a_src1, L0_gnn_a_dst1, L0_gnn_b1, L0_gnn_W2, L0_gnn_a_src2, L0_gnn_a_dst2, L0_gnn_b2, L0_gnn_Wu, L0_gnn_bu, L0_ffn_router_w, L0_ffn_router_b, L0_ffn_corr_bias, L0_ffn_gWg, L0_ffn_gbg, L0_ffn_gWu, L0_ffn_gbu, L0_ffn_gWd, L0_ffn_gbd, L0_ffn_sWg, L0_ffn_sbg, L0_ffn_sWu, L0_ffn_sbu, L0_ffn_sWd, L0_ffn_sbd):
    import jax
    import jax.numpy as jnp

    def _L0_gnn_ref(x, edge_index, norm_g, norm_b, W1, a_src1, a_dst1, b1, W2, a_src2, a_dst2, b2, Wu, bu):
        import jax, jax.numpy as jnp
        import numpy as np
        N = 1250
        E = 20000
        D = 768
        H1, C1 = (4, 192)
        H2, C2 = (2, 96)
        EPS = 1e-05
        NEG_SLOPE = 0.2

        def layer_norm(x, g, b):
            mu = x.mean(-1, keepdims=True)
            var = ((x - mu) ** 2).mean(-1, keepdims=True)
            return (x - mu) * jax.lax.rsqrt(var + EPS) * g + b

        def gat_conv(x, src, dst, W, a_src, a_dst, bias, H, C, n):
            h = (x @ W).reshape(n, H, C)
            s_src = (h * a_src).sum(-1)
            s_dst = (h * a_dst).sum(-1)
            e = jax.nn.leaky_relu(s_src[src] + s_dst[dst], NEG_SLOPE)
            emax = jax.ops.segment_max(e, dst, num_segments=n)
            ee = jnp.exp(e - emax[dst])
            denom = jax.ops.segment_sum(ee, dst, num_segments=n)
            alpha = ee / denom[dst]
            out = jax.ops.segment_sum(alpha[:, :, None] * h[src], dst, num_segments=n)
            return out.reshape(n, H * C) + bias
        loops = jnp.arange(N, dtype=edge_index.dtype)
        src = jnp.concatenate([edge_index[0], loops])
        dst = jnp.concatenate([edge_index[1], loops])
        x_norm = layer_norm(x, norm_g, norm_b)
        out1 = gat_conv(x_norm, src, dst, W1, a_src1, a_dst1, b1, H1, C1, N)
        out2 = gat_conv(out1, src, dst, W2, a_src2, a_dst2, b2, H2, C2, N)
        combined = jnp.concatenate([x, out2], axis=-1)
        return combined @ Wu + bu

    def _L0_ffn_ref(hidden_states, router_w, router_b, corr_bias, gWg, gbg, gWu, gbu, gWd, gbd, sWg, sbg, sWu, sbu, sWd, sbd):
        import jax, jax.numpy as jnp
        import numpy as np
        H = 768
        I = 384
        E = 16
        G = 4
        TOPK_GROUP = 2
        TOP_K = 4
        SCALE = 2.5
        N_SHARED = 2
        IS = I * N_SHARED
        B, S = (1, 256)

        def _route(x, router_w, router_b, corr_bias):
            logits = x.astype(jnp.float32) @ router_w.T + router_b
            scores = jax.nn.sigmoid(logits)
            sfc = scores + corr_bias[None, :]
            grp = sfc.reshape(-1, G, E // G)
            group_scores = jax.lax.top_k(grp, 2)[0].sum(-1)
            _, gidx = jax.lax.top_k(group_scores, TOPK_GROUP)
            gmask = jax.nn.one_hot(gidx, G, dtype=sfc.dtype).sum(axis=1)
            score_mask = jnp.repeat(gmask, E // G, axis=-1)
            sfc = jnp.where(score_mask > 0, sfc, 0.0)
            _, idx = jax.lax.top_k(sfc, TOP_K)
            w = jnp.take_along_axis(scores, idx, axis=1)
            w = w / (w.sum(-1, keepdims=True) + 1e-20)
            return (idx, w * SCALE)

        def _forward(x3, router_w, router_b, corr_bias, gWg, gbg, gWu, gbu, gWd, gbd, sWg, sbg, sWu, sbu, sWd, sbd):
            orig_shape = x3.shape
            x = x3.reshape(-1, H)
            idx, w = _route(x, router_w, router_b, corr_bias)
            c = (jax.nn.one_hot(idx, E, dtype=w.dtype) * w[..., None]).sum(1)
            h = jax.nn.silu(jnp.einsum('th,ehi->tei', x, gWg) + gbg) * (jnp.einsum('th,ehi->tei', x, gWu) + gbu)
            out_e = jnp.einsum('tei,eih->teh', h, gWd) + gbd
            moe_out = jnp.einsum('te,teh->th', c, out_e)
            hs = jax.nn.silu(x @ sWg + sbg) * (x @ sWu + sbu)
            shared = hs @ sWd + sbd
            return (moe_out + shared).reshape(orig_shape)
        return _forward(hidden_states, router_w, router_b, corr_bias, gWg, gbg, gWu, gbu, gWd, gbd, sWg, sbg, sWu, sbu, sWd, sbd)
    edge_index = jnp.stack([src, dst])
    x = x + _L0_gnn_ref(_layernorm(x, axis=-1), edge_index, L0_gnn_norm_g, L0_gnn_norm_b, L0_gnn_W1, L0_gnn_a_src1, L0_gnn_a_dst1, L0_gnn_b1, L0_gnn_W2, L0_gnn_a_src2, L0_gnn_a_dst2, L0_gnn_b2, L0_gnn_Wu, L0_gnn_bu)
    x = x + _L0_ffn_ref(_layernorm(x, axis=-1)[None], L0_ffn_router_w, L0_ffn_router_b, L0_ffn_corr_bias, L0_ffn_gWg, L0_ffn_gbg, L0_ffn_gWu, L0_ffn_gbu, L0_ffn_gWd, L0_ffn_gbd, L0_ffn_sWg, L0_ffn_sbg, L0_ffn_sWu, L0_ffn_sbu, L0_ffn_sWd, L0_ffn_sbd)[0]
    return x

_drawn_inputs = setup_inputs


def setup_inputs(seed=0):
    import zlib

    import numpy as np

    out = dict(_drawn_inputs(seed))
    spreads = {'L0_gnn_norm_g': (1.0, 0.588),
     'L0_gnn_norm_b': (0.0, 0.1),
     'L0_gnn_b1': (0.0, 0.1),
     'L0_gnn_b2': (0.0, 0.1),
     'L0_gnn_bu': (0.0, 0.1),
     'L0_ffn_router_b': (0.0, 0.1),
     'L0_ffn_corr_bias': (0.0, 0.1),
     'L0_ffn_gbg': (0.0, 0.1),
     'L0_ffn_gbu': (0.0, 0.1),
     'L0_ffn_gbd': (0.0, 0.1),
     'L0_ffn_sbg': (0.0, 0.1),
     'L0_ffn_sbu': (0.0, 0.1),
     'L0_ffn_sbd': (0.0, 0.1)}
    factors = {'L0_gnn_a_dst1': 5.185, 'L0_gnn_a_src2': 8.0, 'L0_gnn_a_dst2': 8.0}
    for name, (base, spread) in spreads.items():
        noise = np.random.default_rng([zlib.crc32(name.encode()), seed]).standard_normal(out[name].shape)
        drawn = base * np.exp(spread * noise) if base else spread * noise
        out[name] = jnp.asarray(drawn.astype(out[name].dtype))
    for name, factor in factors.items():
        out[name] = (out[name] * factor).astype(out[name].dtype)
    return out
```

```python
from contextlib import ExitStack, contextmanager

import concourse.bass as bass
from concourse import mybir

ALU = mybir.AluOpType
ACT = mybir.ActivationFunctionType
AX_X = mybir.AxisListType.X
F32 = mybir.dt.float32
BF16 = mybir.dt.bfloat16
F16 = mybir.dt.float16
I32 = mybir.dt.int32
U16 = mybir.dt.uint16

P = 128
NODES = 1250
EDGES = 40000
D = 768
T = -(-NODES // P)
NP = T * P
KD = D // P
HALF = D // 2
EPS = 1e-5
SLOPE = 0.2

CHUNK = 4
GROUPS = 80
LISTED = GROUPS + 1
WIN = 64
PAD_SRC = 4095
NEG = -3.0e38

H1, C1 = 4, 192
H2, C2 = 2, 96

EXPERTS = 16
CHOSEN = 4
IN_GROUP = 4
SCALE = 2.5
I = 384
KI = I // P
SHARED = 2
ALL = SHARED + EXPERTS
SHARED_TILES = SHARED * T
ROUTED_TILES = (NODES * CHOSEN + EXPERTS * (P - 1)) // P
TILES = SHARED_TILES + ROUTED_TILES

AHEAD = 1

ds = bass.ds


class Count:

    def __init__(self):
        self.fixed = 0
        self.loops = []

    def up(self, by=1):
        self.fixed += by
        return self.now()

    def now(self):
        value = self.fixed
        for turn, per in self.loops:
            value = turn * per + value
        return value

    @contextmanager
    def turns(self, turn, per, count):
        start = self.fixed
        self.loops.append((turn, per))
        yield
        self.loops.pop()
        assert self.fixed - start == per, (self.fixed - start, per)
        self.fixed = start + per * count


def edges_and_projection(nc, a, keep):
    ctx = ExitStack()
    with ctx:
        def sb(name, shape, dt=F32):
            return ctx.enter_context(nc.sbuf_tensor(name, shape, dt))

        def sem(name):
            return ctx.enter_context(nc.semaphore(name))

        counts, acc, h1, s_src, s_dst = keep["counts"], keep["acc"], keep["h1"], keep["s_src1"], keep["s_dst1"]
        ident, ones, eps = keep["ident"], keep["ones"], keep["eps"]

        src_i = sb("src_i", [P, LISTED * CHUNK], I32)
        dst_i = sb("dst_i", [P, LISTED * CHUNK], I32)
        src_f = sb("src_f", [P, LISTED * CHUNK])
        dst_f = sb("dst_f", [P, LISTED * CHUNK])
        dst_w = sb("dst_w", [P, LISTED * CHUNK])
        node_ids = sb("node_ids", [P, NP], F16)
        group_lo = sb("group_lo", [P, LISTED])
        group_hi = sb("group_hi", [P, LISTED])
        lo = sb("lo", [LISTED, 1])
        hi = sb("hi", [LISTED, 1])
        bases = sb("bases", [LISTED, LISTED + 1])
        base_i = sb("base_i", [1, LISTED + 1], I32)
        hot_src = [sb(f"hot_src{b}", [P, CHUNK, NP], BF16) for b in range(2)]
        hot_dst = [sb(f"hot_dst{b}", [P, CHUNK, WIN], BF16) for b in range(2)]
        w1 = sb("w1", [P, KD, D])
        wu = sb("wu", [P, KD, D])
        g_row = sb("g_row", [P, D])
        b_row = sb("b_row", [P, D])
        bu_row = sb("bu_row", [P, D])
        a_src = sb("a_src", [P, D])
        a_dst = sb("a_dst", [P, D])
        x_in = [sb(f"x_in{b}", [P, D]) for b in range(2)]
        x0 = [sb(f"x0_{b}", [P, D]) for b in range(2)]
        xn = [sb(f"xn_{b}", [P, D]) for b in range(2)]
        x0_t = [sb(f"x0_t{b}", [P, KD, P]) for b in range(2)]
        xn_t = [sb(f"xn_t{b}", [P, KD, P]) for b in range(2)]
        stats = sb("stats", [P, 2, 6])
        mean_var = sb("mean_var", [P, 2])
        std = sb("std", [P, 1])
        rstd = sb("rstd", [P, 1])
        dot = sb("dot", [P, 2 * H1, C1])

        ps_t = ctx.enter_context(nc.psum_tensor("ps_t", [P, 2, 512], F32))
        ps_h = ctx.enter_context(nc.psum_tensor("ps_h", [P, 2, 512], F32))
        ps_u = ctx.enter_context(nc.psum_tensor("ps_u", [P, 2, 512], F32))
        ps_c = ctx.enter_context(nc.psum_tensor("ps_c", [P, 2, 512], F32))

        edges_in = sem("edges_in")
        weights_in = sem("weights_in")
        rows_in = sem("rows_in")
        x_loaded = [sem(f"x_loaded{b}") for b in range(2)]
        consts_made = sem("consts_made")
        range_found = sem("range_found")
        range_turned = sem("range_turned")
        base_found = sem("base_found")
        base_spread = sem("base_spread")
        base_ready = sem("base_ready")
        counts_clear = sem("counts_clear")
        hot_ready = sem("hot_ready")
        pairs_ready = sem("pairs_ready")
        pairs_added = sem("pairs_added")
        var_ready = sem("var_ready")
        std_ready = sem("std_ready")
        x0_ready = sem("x0_ready")
        xhat_ready = sem("xhat_ready")
        xn_ready = sem("xn_ready")
        acc_seeded = sem("acc_seeded")
        turned = sem("turned")
        turned_out = sem("turned_out")
        h_ready = sem("h_ready")
        u_ready = sem("u_ready")
        h_out = sem("h_out")
        u_out = sem("u_out")
        dots_done = sem("dots_done")
        dve_step = sem("dve_step")
        pool_step = sem("pool_step")
        gen_hot = sem("gen_hot")
        gen_pairs = sem("gen_pairs")
        gen_added = sem("gen_added")

        PAIRS = T // 2
        PER_TILE = GROUPS // T

        with nc.Block() as block:

            @block.sync
            def _(sp):
                sp.dma_start(dst_i[:, :], a["dst"]).then_inc(edges_in, 16)
                sp.dma_start(x_in[0][:, :], a["x"][0:P, :]).then_inc(x_loaded[0], 16)
                sp.dma_start(src_i[:, :], a["src"]).then_inc(edges_in, 16)
                for row, source in ((g_row, "norm_g"), (b_row, "norm_b"), (bu_row, "bu"),
                                    (a_src, "a_src1"), (a_dst, "a_dst1")):
                    sp.dma_start(row[:, :], a[source].partition_broadcast(P)).then_inc(rows_in, 16)
                with sp.Fori(0, PAIRS) as i:
                    for b in range(2):
                        t = 2 * i + b
                        sp.wait_ge(x0_ready, AHEAD + t)
                        sp.wait_ge(acc_seeded, AHEAD + t)
                        sp.dma_start(x_in[1 - b][:, :], a["x"][ds((t + 1) * P, P), :]).then_inc(x_loaded[1 - b], 16)

            @block.gpsimd
            def _(pool):
                pool.nop().then_inc(acc_seeded, AHEAD)
                pool.nop().then_inc(xn_ready, AHEAD)
                nc.gpsimd.memset(ident[:, :], 0.0).then_inc(pool_step, 1)
                nc.gpsimd.memset(ones[:, :], 1.0).then_inc(consts_made, 1)
                nc.gpsimd.memset(eps[:, :], EPS).then_inc(consts_made, 1)
                pool.wait_ge(pool_step, 1)
                nc.gpsimd.affine_select(out=ident[:, :], in_=ident[:, :], compare_op=ALU.not_equal, fill=1.0,
                                        base=0, pattern=[[-1, P]], channel_multiplier=1).then_inc(consts_made, 1)
                nc.gpsimd.iota(node_ids[:, :], pattern=[[1, NP]], base=0, channel_multiplier=0,
                               allow_small_or_imprecise_dtypes=True).then_inc(consts_made, 1)
                nc.gpsimd.memset(counts[:, :, :], 0).then_inc(counts_clear, 1)
                nc.gpsimd.memset(h1[:, :, :], 1.0).then_inc(counts_clear, 1)
                step = Count()
                step.up()
                pool.wait_ge(rows_in, 16 * 5)

                def seed_and_scale(t, b, loaded):
                    pool.wait_ge(x_loaded[b], loaded)
                    nc.gpsimd.tensor_tensor(acc[:, t, :], x_in[b][:, :], bu_row[:, :], ALU.add).then_inc(acc_seeded, 1)
                    pool.wait_ge(xhat_ready, AHEAD + t + 1)
                    nc.gpsimd.tensor_tensor(xn[b][:, :], xn[b][:, :], g_row[:, :], ALU.mult).then_inc(pool_step, 1)
                    pool.wait_ge(pool_step, step.up())
                    nc.gpsimd.tensor_tensor(xn[b][:, :], xn[b][:, :], b_row[:, :], ALU.add).then_inc(xn_ready, 1)

                with pool.Fori(0, PAIRS) as i, step.turns(i, 2, PAIRS):
                    for b in range(2):
                        seed_and_scale(2 * i + b, b, (i + 1) * 16)

            @block.scalar
            def _(act):
                act.nop().then_inc(turned_out, AHEAD)
                act.nop().then_inc(h_out, AHEAD)
                act.dma_start(wu[:, :, :], a["Wu"][0:D, :].rearrange("(k p) n -> p k n", p=P)).then_inc(weights_in, 16)
                act.dma_start(w1[:, :, :], a["W1"].rearrange("(k p) n -> p k n", p=P)).then_inc(weights_in, 16)
                act.wait_ge(consts_made, 2)
                act.wait_ge(counts_clear, 2)

                def root(count):
                    act.wait_ge(var_ready, count)
                    nc.scalar.activation(std[:, :], mean_var[:, 1:2], ACT.Sqrt, bias=eps[:, 0:1],
                                         scale=1.0).then_inc(std_ready, 1)

                def take_turned(out, count):
                    act.wait_ge(turned, AHEAD + count)
                    nc.scalar.copy(out[:, 0:4, :], ps_t[:, 0, 0:512])
                    nc.scalar.copy(out[:, 4:KD, :], ps_t[:, 1, 0:256]).then_inc(turned_out, 1)

                root(1)
                root(2)
                with act.Fori(0, PAIRS) as i:
                    for b in range(2):
                        t = 2 * i + b
                        take_turned(x0_t[b], 2 * t + 1)
                        root(2 * t + 3)
                        take_turned(xn_t[b], 2 * t + 2)
                        root(2 * t + 4)
                        act.wait_ge(h_ready, t + 1)
                        for n in range(2):
                            last = nc.scalar.copy(h1[:, t, 2 * n * (C1 + 2):2 * (n + 1) * (C1 + 2)]
                                                  .rearrange("p (h c) -> p h c", h=2)[:, :, 0:C1],
                                                  ps_h[:, n, 0:HALF].rearrange("p (h c) -> p h c", h=2))
                        last.then_inc(h_out, 1)

            @block.tensor
            def _(pe):
                pe.nop().then_inc(turned, AHEAD)
                pe.wait_ge(consts_made, 4)
                pe.wait_ge(range_found, 1)
                nc.tensor.transpose(ps_c[0:LISTED, 0, 0:P], group_lo[:, :], ident[:, :])
                nc.tensor.transpose(ps_c[0:LISTED, 0, P:2 * P], group_hi[:, :], ident[:, :]).then_inc(range_turned, 1)
                pe.wait_ge(base_found, 2)
                nc.tensor.matmul(ps_c[:, 1, 0:LISTED + 1], ones[0:LISTED, :], bases[:, :], start=True,
                                 stop=True).then_inc(base_spread, 1)
                pe.wait_ge(base_ready, 1)
                pe.wait_ge(weights_in, 32)

                def pair_products(hot_s, hot_d):
                    for c in range(CHUNK):
                        for j in range(T):
                            col = (j % 5) * WIN
                            last = nc.tensor.matmul(ps_c[:, j // 5, col:col + WIN], hot_s[:, c, j * P:(j + 1) * P],
                                                    hot_d[:, c, :], start=(c == 0 and j % 5 == 0),
                                                    stop=(c == CHUNK - 1), skip_group_check=True)
                    return last

                def turn(rows, ready, t, count):
                    pe.wait_ge(ready, AHEAD + t + 1)
                    pe.wait_ge(turned_out, AHEAD + count)
                    for k in range(KD):
                        last = nc.tensor.transpose(ps_t[:, k // 4, (k % 4) * P:(k % 4 + 1) * P],
                                                   rows[:, k * P:(k + 1) * P], ident[:, :])
                    last.then_inc(turned, 1)

                def project(out, lhs, w, ks):
                    for k in ks:
                        for n in range(2):
                            last = nc.tensor.matmul(out[:, n, 0:HALF], lhs[:, k, :], w[:, k, n * HALF:(n + 1) * HALF],
                                                    start=(k == 0), stop=(k == KD - 1))
                    return last

                with pe.Fori(0, PAIRS) as i:
                    for b in range(2):
                        t = 2 * i + b
                        for slot in range(PER_TILE):
                            g = t * PER_TILE + slot
                            pe.wait_ge(hot_ready, g + 1)
                            pe.wait_ge(pairs_added, AHEAD + g)
                            pair_products(hot_src[slot % 2], hot_dst[slot % 2]).then_inc(pairs_ready, 1)
                            if slot == 0:
                                turn(x0[b], x0_ready, t, 2 * t)
                            if slot == 1:
                                turn(xn[b], xn_ready, t, 2 * t + 1)
                                pe.wait_ge(u_out, AHEAD + t)
                            if slot == 4:
                                pe.wait_ge(turned_out, AHEAD + 2 * t + 2)
                                pe.wait_ge(h_out, AHEAD + t)
                            if 1 <= slot <= 3:
                                last = project(ps_u, x0_t[b], wu, range(2 * slot - 2, 2 * slot))
                                if slot == 3:
                                    last.then_inc(u_ready, 1)
                            if 4 <= slot <= 6:
                                last = project(ps_h, xn_t[b], w1, range(2 * slot - 8, 2 * slot - 6))
                                if slot == 6:
                                    last.then_inc(h_ready, 1)

                wide = pe.value_load(base_i[0:1, LISTED:LISTED + 1], min_val=0, max_val=LISTED)
                with pe.If(wide > 0):
                    with pe.Fori(0, NP // WIN) as w:
                        with pe.Fori(0, GROUPS) as g:
                            pe.wait_ge(gen_hot, w * GROUPS + g + 1)
                            pair_products(hot_src[0], hot_dst[0]).then_inc(gen_pairs, 1)

            @block.vector
            def _(dve):
                dve.nop().then_inc(x0_ready, AHEAD)
                dve.nop().then_inc(xhat_ready, AHEAD)
                dve.nop().then_inc(pairs_added, AHEAD)
                dve.nop().then_inc(u_out, AHEAD)
                step = Count()
                dve.wait_ge(edges_in, 32)
                nc.vector.tensor_copy(dst_f[:, :], dst_i[:, :]).then_inc(dve_step, 1)
                nc.vector.tensor_copy(src_f[:, :], src_i[:, :]).then_inc(dve_step, 1)
                dve.wait_ge(dve_step, step.up(2))
                grouped = dst_f[:, :].rearrange("p (g c) -> p g c", c=CHUNK)
                nc.vector.tensor_reduce(group_lo[:, :], grouped, AX_X, ALU.min)
                nc.vector.tensor_reduce(group_hi[:, :], grouped, AX_X, ALU.max).then_inc(range_found, 1)
                dve.wait_ge(range_turned, 1)
                nc.vector.tensor_reduce(lo[:, :], ps_c[0:LISTED, 0, 0:P], AX_X, ALU.min).then_inc(dve_step, 1)
                nc.vector.tensor_reduce(hi[:, :], ps_c[0:LISTED, 0, P:2 * P], AX_X, ALU.max).then_inc(dve_step, 1)
                dve.wait_ge(dve_step, step.up(2))
                nc.vector.tensor_scalar(lo[:, :], lo[:, :], float(NP - WIN), None, ALU.min).then_inc(dve_step, 1)
                dve.wait_ge(dve_step, step.up())
                nc.vector.tensor_tensor(hi[:, :], hi[:, :], lo[:, :], ALU.subtract).then_inc(dve_step, 1)
                nc.vector.tensor_scalar(bases[:, 0:LISTED], ident[0:LISTED, 0:LISTED], lo[:, 0:1], None,
                                        ALU.mult).then_inc(base_found, 1)
                dve.wait_ge(dve_step, step.up())
                nc.vector.tensor_scalar(bases[:, LISTED:LISTED + 1], hi[:, :], float(WIN), None,
                                        ALU.is_ge).then_inc(base_found, 1)
                dve.wait_ge(base_spread, 1)
                nc.vector.tensor_copy(base_i[:, :], ps_c[0:1, 1, 0:LISTED + 1]).then_inc(dve_step, 1)
                for c in range(CHUNK):
                    nc.vector.tensor_tensor(dst_w[:, :].rearrange("p (g c) -> p g c", c=CHUNK)[:, :, c],
                                            dst_f[:, :].rearrange("p (g c) -> p g c", c=CHUNK)[:, :, c],
                                            ps_c[:, 1, 0:LISTED], ALU.subtract).then_inc(dve_step, 1)

                def self_loops():
                    for j in range(T):
                        last = nc.vector.tensor_copy(counts[:, j, j * P:(j + 1) * P], ident[:, :])
                    return last

                dve.wait_ge(consts_made, 4)
                dve.wait_ge(counts_clear, 2)
                self_loops().then_inc(base_ready, 1)
                dve.wait_ge(dve_step, step.up(1 + CHUNK))
                dve.wait_ge(base_ready, 1)

                def one_hots(hot_s, hot_d, g, dsts, base):
                    for c in range(CHUNK):
                        nc.vector.tensor_scalar(hot_s[:, c, :], node_ids[:, :], src_f[:, ds(g * CHUNK + c, 1)],
                                                None, ALU.is_equal)
                        last = nc.vector.tensor_scalar(hot_d[:, c, :], node_ids[:, ds(base, WIN)],
                                                       dsts[:, ds(g * CHUNK + c, 1)], None, ALU.is_equal)
                    return last

                def add_pairs(base):
                    window = counts[:, :, ds(base, WIN)]
                    for n in range(2):
                        last = nc.vector.tensor_tensor(window[:, 5 * n:5 * n + 5, :],
                                                       ps_c[:, n, 0:5 * WIN].rearrange("p (j w) -> p j w", w=WIN),
                                                       window[:, 5 * n:5 * n + 5, :], ALU.add)
                    return last

                def halves(x):
                    for n in range(2):
                        last = nc.vector.bn_stats(stats[:, n, :], x[:, n * HALF:(n + 1) * HALF])
                    return last.then_inc(dve_step, 1)

                def aggregate():
                    return nc.vector.bn_aggr(mean_var[:, :], stats[:, :, :]).then_inc(var_ready, 1)

                def invert(count):
                    dve.wait_ge(std_ready, count)
                    return nc.vector.reciprocal(rstd[:, :], std[:, :]).then_inc(dve_step, 1)

                def normalise(x, out):
                    return nc.vector.tensor_scalar(out[:, :], x[:, :], mean_var[:, 0:1], rstd[:, 0:1],
                                                   ALU.subtract, ALU.mult)

                dve.wait_ge(x_loaded[0], 16)
                for x, out, count, ready in ((x_in[0], x0[0], 1, x0_ready), (x0[0], xn[0], 2, xhat_ready)):
                    halves(x)
                    dve.wait_ge(dve_step, step.up())
                    aggregate()
                    invert(count)
                    dve.wait_ge(dve_step, step.up())
                    normalise(x, out).then_inc(ready, 1)
                    dve.wait_ge(ready, AHEAD + 1)
                one_hots(hot_src[0], hot_dst[0], 0, dst_w, 0).then_inc(hot_ready, 1)

                with dve.Fori(0, PAIRS) as i, step.turns(i, 2 * 4, PAIRS):
                    for b in range(2):
                        t = 2 * i + b
                        other = 1 - b
                        for slot in range(PER_TILE):
                            g = t * PER_TILE + slot
                            if slot == 0:
                                dve.wait_ge(x_loaded[other], (i + 1 + b) * 16)
                                dve.wait_ge(turned, AHEAD + 2 * t)
                                halves(x_in[other])
                            if slot == 2:
                                dve.wait_ge(x0_ready, AHEAD + t + 2)
                                halves(x0[other])
                            if slot in (0, 2):
                                dve.wait_ge(dve_step, step.up())
                            one_hots(hot_src[(slot + 1) % 2], hot_dst[(slot + 1) % 2], g + 1, dst_w, 0)\
                                .then_inc(hot_ready, 1)
                            if slot in (0, 2):
                                aggregate()
                            if slot in (1, 3):
                                invert(2 * t + 2 + (slot + 1) // 2)
                            base = dve.value_load(base_i[0:1, ds(g, 1)], min_val=0, max_val=NP - WIN)
                            dve.wait_ge(pairs_ready, g + 1)
                            dve.wait_ge(pairs_added, AHEAD + g)
                            add_pairs(base).then_inc(pairs_added, 1)
                            if slot == 1:
                                dve.wait_ge(dve_step, step.up())
                                normalise(x_in[other], x0[other]).then_inc(x0_ready, 1)
                            if slot == 3:
                                dve.wait_ge(dve_step, step.up())
                                normalise(x0[other], xn[other]).then_inc(xhat_ready, 1)
                            if slot == 4:
                                dve.wait_ge(u_ready, t + 1)
                                dve.wait_ge(acc_seeded, AHEAD + t + 1)
                                nc.vector.tensor_tensor(acc[:, t, :].rearrange("p (n c) -> p n c", n=2),
                                                        ps_u[:, :, 0:HALF],
                                                        acc[:, t, :].rearrange("p (n c) -> p n c", n=2),
                                                        ALU.add).then_inc(u_out, 1)
                            if slot == 7:
                                dve.wait_ge(h_out, AHEAD + t + 1)
                                for h in range(H1):
                                    for which, weights, scores in ((0, a_src, s_src), (1, a_dst, s_dst)):
                                        last = nc.vector.scalar_tensor_tensor(
                                            out=dot[:, 2 * h + which, :],
                                            in0=h1[:, t, h * (C1 + 2):h * (C1 + 2) + C1], scalar=1.0,
                                            in1=weights[:, h * C1:(h + 1) * C1], op0=ALU.mult, op1=ALU.mult,
                                            accum_out=scores[:, ds(t + h * T, 1)])
                                last.then_inc(dots_done, 1)
                                dve.wait_ge(dots_done, t + 1)

                dve.wait_ge(pairs_added, AHEAD + GROUPS)
                wide = dve.value_load(base_i[0:1, LISTED:LISTED + 1], min_val=0, max_val=LISTED)
                with dve.If(wide > 0):
                    nc.vector.memset(counts[:, :, :], 0).then_inc(gen_added, 1)
                    dve.wait_ge(gen_added, 1)
                    self_loops().then_inc(gen_added, 1)
                    dve.wait_ge(gen_added, 2)
                    with dve.Fori(0, NP // WIN) as w:
                        with dve.Fori(0, GROUPS) as g:
                            one_hots(hot_src[0], hot_dst[0], g, dst_f, w * WIN).then_inc(gen_hot, 1)
                            dve.wait_ge(gen_pairs, w * GROUPS + g + 1)
                            add_pairs(w * WIN).then_inc(gen_added, 1)
                            dve.wait_ge(gen_added, w * GROUPS + g + 3)


def attention(nc, a, keep, layer, heads, width):
    ctx = ExitStack()
    with ctx:
        def sb(name, shape, dt=F32):
            return ctx.enter_context(nc.sbuf_tensor(f"{name}_{layer}", shape, dt))

        def sem(name):
            return ctx.enter_context(nc.semaphore(f"{name}_{layer}"))

        counts, no_edge, ident = keep["counts"], keep["no_edge"], keep["ident"]
        h_rows, s_src, s_dst = keep[f"h{layer}"], keep[f"s_src{layer}"], keep[f"s_dst{layer}"]
        W = width + 2
        PER_BANK = 512 // W if 512 // W < T // 2 else T // 2
        BANKS = T // PER_BANK
        HT = heads * T
        RING = 5

        best = [sb(f"best{b}", [P, NP]) for b in range(2)]
        top = sb("top", [P, HT])
        peak = sb("peak", [P, HT])
        src_low = sb("src_low", [P, HT])
        shifts = sb("shifts", [P, heads, 2, T])
        shifts_t = sb("shifts_t", [2 * HT, P])
        shift_rows = [sb(f"shift_rows{b}", [P, 2, NP]) for b in range(2)]
        weights = [sb(f"weights{b}", [P, NP]) for b in range(RING)]
        rden = sb("rden", [P, T])
        bias_row = sb("bias_row", [P, heads * width])
        shift_dram = nc.dram_tensor(f"shift_dram_{layer}", (2 * HT, P), F32).ap()

        ps_o = ctx.enter_context(nc.psum_tensor(f"ps_o_{layer}", [P, 5, 512], F32))
        ps_m = ctx.enter_context(nc.psum_tensor(f"ps_m_{layer}", [P, 3, 512], F32))

        bias_in = sem("bias_in")
        masked = sem("masked")
        best_step = sem("best_step")
        best_ready = sem("best_ready")
        best_turned = sem("best_turned")
        top_ready = sem("top_ready")
        small_step = sem("small_step")
        shifts_ready = sem("shifts_ready")
        shifts_turned = sem("shifts_turned")
        shifts_out = sem("shifts_out")
        shifts_stored = sem("shifts_stored")
        rows_in = [sem(f"shift_rows_in{b}") for b in range(2)]
        low_ready = sem("low_ready")
        bound_ready = sem("bound_ready")
        exp_ready = sem("exp_ready")
        weights_ready = sem("weights_ready")
        weights_used = sem("weights_used")
        inverse_ready = sem("inverse_ready")
        head_out = sem("head_out")

        with nc.Block() as block:

            @block.sync
            def _(sp):
                sp.dma_start(bias_row[:, :], a[f"b{layer}"].partition_broadcast(P)).then_inc(bias_in, 16)
                sp.wait_ge(shifts_out, 1)
                sp.dma_start(shift_dram, shifts_t[:, :]).then_inc(shifts_stored, 16)
                sp.wait_ge(shifts_stored, 16)
                by_head = shift_dram.rearrange("(h r) p -> h (r p)", h=heads)
                for h in range(heads):
                    if h >= 2:
                        sp.wait_ge(bound_ready, (h - 1) * T)
                    sp.dma_start(shift_rows[h % 2][:, :, :].rearrange("p s n -> p (s n)"),
                                 by_head[h:h + 1, :].broadcast_to([P, 2 * NP])).then_inc(rows_in[h % 2], 16)

            @block.scalar
            def _(act):
                act.wait_ge(shifts_ready, 1)
                act.wait_ge(shifts_turned, 1)
                nc.scalar.copy(shifts_t[:, :], ps_m[0:2 * HT, 0, 0:P]).then_inc(shifts_out, 1)

                def low_part(b, h, s):
                    nc.scalar.activation(weights[s % RING][:, :], shift_rows[b][:, 1, :], ACT.Identity,
                                         bias=src_low[:, ds(h * T + s, 1)], scale=1.0).then_inc(low_ready, 1)

                with act.Fori(0, heads // 2) as i:
                    for b in range(2):
                        h = 2 * i + b
                        act.wait_ge(rows_in[b], (i + 1) * 16)
                        for s in range(T + 2):
                            if s < T:
                                if s >= RING:
                                    act.wait_ge(weights_used, AHEAD + h * T + s - RING + 1)
                                elif s == 0:
                                    act.wait_ge(weights_used, AHEAD + h * T)
                                low_part(b, h, s)
                            if s >= 2:
                                act.wait_ge(bound_ready, h * T + s - 1)
                                w = weights[(s - 2) % RING]
                                nc.scalar.activation(w[:, :], w[:, :], ACT.Exp).then_inc(exp_ready, 1)

            @block.tensor
            def _(pe):
                pe.nop().then_inc(weights_used, AHEAD)
                pe.nop().then_inc(best_turned, AHEAD)
                with pe.Fori(0, heads // 2) as i:
                    for b in range(2):
                        h = 2 * i + b
                        pe.wait_ge(best_ready, h + 1)
                        pe.wait_ge(top_ready, AHEAD + h)
                        for j in range(T):
                            last = nc.tensor.transpose(ps_m[:, j // 4, (j % 4) * P:(j % 4 + 1) * P],
                                                       best[b][:, j * P:(j + 1) * P], ident[:, :])
                        last.then_inc(best_turned, 1)
                pe.wait_ge(shifts_ready, 1)
                nc.tensor.transpose(ps_m[0:2 * HT, 0, 0:P], shifts[:, :, :, :].rearrange("p h s t -> p (h s t)"),
                                    ident[:, :]).then_inc(shifts_turned, 1)
                with pe.Fori(0, heads) as h:
                    pe.wait_ge(head_out, AHEAD + h)
                    for s in range(T):
                        pe.wait_ge(weights_ready, h * T + s + 1)
                        for j in range(T):
                            col = (j % PER_BANK) * W
                            last = nc.tensor.matmul(ps_o[:, j // PER_BANK, col:col + W],
                                                    weights[s % RING][:, j * P:(j + 1) * P],
                                                    h_rows[:, s, ds(h * W, W)],
                                                    start=(s == 0 and j % PER_BANK == 0), stop=(s == T - 1),
                                                    skip_group_check=True)
                        last.then_inc(weights_used, 1)

            @block.vector
            def _(dve):
                dve.nop().then_inc(top_ready, AHEAD)
                dve.nop().then_inc(head_out, AHEAD)
                if layer == 1:
                    nc.vector.tensor_scalar(no_edge[:, :, :], counts[:, :, :], 0.0, NEG, ALU.is_equal,
                                            ALU.mult).then_inc(masked, 1)
                    dve.wait_ge(masked, 1)
                chain = Count()
                with dve.Fori(0, heads // 2) as i, chain.turns(i, 2 * (T - 1), heads // 2):
                    for b in range(2):
                        h = 2 * i + b
                        dve.wait_ge(best_turned, AHEAD + 2 * i)
                        nc.vector.tensor_scalar(best[b][:, :], no_edge[:, 0, :], s_src[:, ds(h * T, 1)], None,
                                                ALU.add).then_inc(best_step, 1)
                        for s in range(1, T):
                            dve.wait_ge(best_step, chain.up())
                            last = nc.vector.scalar_tensor_tensor(
                                out=best[b][:, :], in0=no_edge[:, s, :], scalar=s_src[:, ds(h * T + s, 1)],
                                in1=best[b][:, :], op0=ALU.add, op1=ALU.max)
                            last.then_inc(best_step if s < T - 1 else best_ready, 1)
                        dve.wait_ge(best_turned, AHEAD + h + 1)
                        nc.vector.tensor_reduce(top[:, ds(h * T, 8)], ps_m[:, 0:2, :].rearrange(
                            "p b (j n) -> p (b j) n", n=P), AX_X, ALU.max)
                        nc.vector.tensor_reduce(top[:, ds(h * T + 8, T - 8)], ps_m[:, 2, 0:(T - 8) * P].rearrange(
                            "p (j n) -> p j n", n=P), AX_X, ALU.max).then_inc(top_ready, 1)
                dve.wait_ge(top_ready, AHEAD + heads)
                small = Count()
                nc.vector.tensor_scalar(src_low[:, :], s_src[:, :], SLOPE, None, ALU.mult)
                nc.vector.tensor_tensor(top[:, :], top[:, :], s_dst[:, :], ALU.add).then_inc(small_step, 1)
                dve.wait_ge(small_step, small.up())
                nc.vector.scalar_tensor_tensor(out=peak[:, :], in0=top[:, :], scalar=SLOPE, in1=top[:, :],
                                               op0=ALU.mult, op1=ALU.max).then_inc(small_step, 1)
                dve.wait_ge(small_step, small.up())
                by_head = [x.rearrange("p (h t) -> p h t", t=T) for x in (s_dst[:, :], peak[:, :])]
                nc.vector.tensor_tensor(shifts[:, :, 0, :], by_head[0], by_head[1], ALU.subtract)\
                    .then_inc(small_step, 1)
                nc.vector.scalar_tensor_tensor(out=shifts[:, :, 1, :], in0=by_head[0], scalar=SLOPE, in1=by_head[1],
                                               op0=ALU.mult, op1=ALU.subtract).then_inc(shifts_ready, 1)
                dve.wait_ge(small_step, small.up())
                dve.wait_ge(bias_in, 16)

                def upper(b, h, s):
                    dve.wait_ge(low_ready, h * T + s + 1)
                    w = weights[s % RING]
                    return nc.vector.scalar_tensor_tensor(out=w[:, :], in0=shift_rows[b][:, 0, :],
                                                          scalar=s_src[:, ds(h * T + s, 1)], in1=w[:, :],
                                                          op0=ALU.add, op1=ALU.max)

                with dve.Fori(0, heads // 2) as i:
                    for b in range(2):
                        h = 2 * i + b
                        dve.wait_ge(rows_in[b], (i + 1) * 16)
                        for s in range(T + 2):
                            if s < T:
                                upper(b, h, s).then_inc(bound_ready, 1)
                                if s == T - 1:
                                    dve.wait_ge(bound_ready, h * T + T)
                            if s >= 2:
                                dve.wait_ge(exp_ready, h * T + s - 1)
                                w = weights[(s - 2) % RING]
                                last = nc.vector.scalar_tensor_tensor(
                                    out=w[:, :], in0=w[:, :], scalar=1.0, in1=counts[:, s - 2, :],
                                    op0=ALU.min, op1=ALU.mult).then_inc(weights_ready, 1)
                        dve.wait_ge(weights_used, AHEAD + h * T + T)
                        sums = ps_o[:, 0:BANKS, 0:PER_BANK * W].rearrange("p b (j w) -> p b j w", w=W)
                        nc.vector.reciprocal(rden[:, :].rearrange("p (b j) -> p b j", b=BANKS),
                                             sums[:, :, :, width]).then_inc(inverse_ready, 1)
                        dve.wait_ge(inverse_ready, h + 1)
                        for j in range(T):
                            last = nc.vector.scalar_tensor_tensor(
                                out=h_rows[:, j, ds(h * width, width)],
                                in0=ps_o[:, j // PER_BANK, (j % PER_BANK) * W:(j % PER_BANK) * W + width],
                                scalar=rden[:, j:j + 1], in1=bias_row[:, ds(h * width, width)],
                                op0=ALU.mult, op1=ALU.add)
                        last.then_inc(head_out, 1)

            @block.gpsimd
            def _(pool):
                if layer == 1:
                    nc.gpsimd.memset(keep["h2"][:, :, :], 1.0)


def second_projection(nc, a, keep):
    ctx = ExitStack()
    with ctx:
        def sb(name, shape, dt=F32):
            return ctx.enter_context(nc.sbuf_tensor(name, shape, dt))

        def sem(name):
            return ctx.enter_context(nc.semaphore(name))

        h1, h2, s_src, s_dst, ident = keep["h1"], keep["h2"], keep["s_src2"], keep["s_dst2"], keep["ident"]
        W, N2 = C2 + 2, H2 * C2
        w2 = sb("w2", [P, KD, N2])
        a_src = sb("a_src_b", [P, N2])
        a_dst = sb("a_dst_b", [P, N2])
        out1_t = [sb(f"out1_t{b}", [P, KD, P]) for b in range(2)]
        dot = sb("dot_b", [P, 2 * H2, C2])
        ps_t = [ctx.enter_context(nc.psum_tensor(f"ps_r{b}", [P, 2, 512], F32)) for b in range(2)]
        ps_p = [ctx.enter_context(nc.psum_tensor(f"ps_p{b}", [P, 512], F32)) for b in range(2)]
        loaded = sem("loaded")
        turned = sem("turned_b")
        turned_out = sem("turned_out_b")
        ready = sem("ready_b")
        copied = sem("copied_b")
        dots_done = sem("dots_done_b")

        with nc.Block() as block:

            @block.sync
            def _(sp):
                sp.dma_start(w2[:, :, :], a["W2"].rearrange("(k p) n -> p k n", p=P)).then_inc(loaded, 16)
                sp.dma_start(a_src[:, :], a["a_src2"].partition_broadcast(P)).then_inc(loaded, 16)
                sp.dma_start(a_dst[:, :], a["a_dst2"].partition_broadcast(P)).then_inc(loaded, 16)

            @block.tensor
            def _(pe):
                pe.nop().then_inc(ready, AHEAD)
                pe.wait_ge(loaded, 48)

                def turn(t):
                    for k in range(KD):
                        last = nc.tensor.transpose(ps_t[t % 2][:, k // 4, (k % 4) * P:(k % 4 + 1) * P],
                                                   h1[:, t, k * P:(k + 1) * P], ident[:, :])
                    last.then_inc(turned, 1)

                for t in range(T + 1):
                    if t < T:
                        if t >= 2:
                            pe.wait_ge(turned_out, t - 1)
                        turn(t)
                    if t >= 1:
                        pe.wait_ge(turned_out, t)
                        if t >= 3:
                            pe.wait_ge(copied, t - 2)
                        for k in range(KD):
                            last = nc.tensor.matmul(ps_p[(t - 1) % 2][:, 0:N2], out1_t[(t - 1) % 2][:, k, :],
                                                    w2[:, k, :], start=(k == 0), stop=(k == KD - 1))
                        last.then_inc(ready, 1)

            @block.scalar
            def _(act):
                with act.Fori(0, T // 2) as i:
                    for b in range(2):
                        t = 2 * i + b
                        act.wait_ge(turned, t + 1)
                        act.wait_ge(ready, AHEAD + 2 * i)
                        nc.scalar.copy(out1_t[b][:, 0:4, :], ps_t[b][:, 0, 0:512])
                        nc.scalar.copy(out1_t[b][:, 4:KD, :], ps_t[b][:, 1, 0:256]).then_inc(turned_out, 1)

            @block.vector
            def _(dve):
                dve.wait_ge(loaded, 48)
                with dve.Fori(0, T // 2) as i:
                    for b in range(2):
                        t = 2 * i + b
                        dve.wait_ge(ready, AHEAD + t + 1)
                        nc.vector.tensor_copy(h2[:, t, :].rearrange("p (h c) -> p h c", h=H2)[:, :, 0:C2],
                                              ps_p[b][:, 0:N2].rearrange("p (h c) -> p h c", h=H2))\
                            .then_inc(copied, 1)
                        dve.wait_ge(copied, t + 1)
                        for h in range(H2):
                            for which, weights, scores in ((0, a_src, s_src), (1, a_dst, s_dst)):
                                last = nc.vector.scalar_tensor_tensor(
                                    out=dot[:, 2 * h + which, :], in0=h2[:, t, h * W:h * W + C2], scalar=1.0,
                                    in1=weights[:, h * C2:(h + 1) * C2], op0=ALU.mult, op1=ALU.mult,
                                    accum_out=scores[:, ds(t + h * T, 1)])
                        last.then_inc(dots_done, 1)
                        dve.wait_ge(dots_done, t + 1)


def update_and_route(nc, a, keep):
    ctx = ExitStack()
    with ctx:
        def sb(name, shape, dt=F32):
            return ctx.enter_context(nc.sbuf_tensor(name, shape, dt))

        def sem(name):
            return ctx.enter_context(nc.semaphore(name))

        acc, h2, ident, ones, eps = keep["acc"], keep["h2"], keep["ident"], keep["ones"], keep["eps"]
        token_of, place_i, mix, tile_expert, ends_i = (keep[n] for n in (
            "token_of", "place_i", "mix", "tile_expert", "ends_i"))
        xh_dram, list_dram = keep["xh_dram"], keep["list_dram"]
        N2 = H2 * C2
        REST = N2 - P
        TE = T * EXPERTS

        wu_a = sb("wu_a", [P, D])
        wu_b = sb("wu_b", [REST, D])
        router = sb("router", [P, KD, EXPERTS])
        rb_row = sb("rb_row", [P, EXPERTS])
        cb_row = sb("cb_row", [P, EXPERTS])
        out2_t = [sb(f"out2_t{b}", [P, 2, P]) for b in range(2)]
        xh = [sb(f"xh{b}", [P, D]) for b in range(2)]
        xh_t = [sb(f"xh_t{b}", [P, KD, P]) for b in range(2)]
        stats = sb("stats_c", [P, 2, 6])
        mean_var = sb("mean_var_c", [P, 2])
        std = sb("std_c", [P, 1])
        rstd = sb("rstd_c", [P, 1])
        logits = sb("logits", [P, T, EXPERTS])
        scores = sb("scores", [P, T, EXPERTS])
        biased = sb("biased", [P, T, EXPERTS])
        pair_hi = sb("pair_hi", [P, T, 4, 2])
        pair_lo = sb("pair_lo", [P, T, 4, 2])
        group_score = sb("group_score", [P, T, 4])
        group_next = sb("group_next", [P, T, 4])
        group_kept = sb("group_kept", [P, T, 4])
        ahead = sb("ahead", [P, T, EXPERTS, EXPERTS])
        tied = sb("tied", [P, T, EXPERTS, EXPERTS])
        before = sb("before", [P, EXPERTS, EXPERTS])
        before4 = sb("before4", [P, 4, 4])
        rank = sb("rank", [P, T, EXPERTS])
        chosen = sb("chosen", [P, T, EXPERTS])
        real = sb("real", [P, T, EXPERTS])
        nth = sb("nth", [P, T, EXPERTS])
        mask = sb("mask", [P, T, EXPERTS])
        picked = sb("picked", [P, T, EXPERTS])
        place = sb("place", [P, T, EXPERTS])
        total = sb("total", [P, T])
        earlier = sb("earlier", [P, T + 1, EXPERTS])
        in_tile = sb("in_tile", [P, T, EXPERTS])
        thresholds = sb("thresholds", [P, T])
        filled = sb("filled", [P, EXPERTS, T])
        n_tiles = sb("n_tiles", [P, EXPERTS])
        starts = sb("starts", [P, EXPERTS])
        ends = sb("ends", [P, ALL])
        tile_ids = sb("tile_ids", [P, TILES])
        passed = sb("passed", [P, TILES, ALL])
        tile_f = sb("tile_f", [P, TILES])
        earlier_rows = sb("earlier_rows", [P, P])
        token_ids = sb("token_ids", [P, T], I32)
        place_k = sb("place_k", [P, CHOSEN, T])
        list_k = sb("list_k", [P, CHOSEN, T])
        list_i = sb("list_i", [P, CHOSEN, T], I32)
        dump = sb("dump", [P, CHOSEN, T])
        zeros_i = sb("zeros_i", [ROUTED_TILES, P], I32)
        listed_i = sb("listed_i", [ROUTED_TILES, P], I32)
        listed = sb("listed", [ROUTED_TILES, P])

        ps_a = [ctx.enter_context(nc.psum_tensor(f"ps_a{b}", [P, 512], F32)) for b in range(2)]
        ps_x = ctx.enter_context(nc.psum_tensor("ps_x", [P, 2, 512], F32))
        ps_b = ctx.enter_context(nc.psum_tensor("ps_b", [P, 2, 512], F32))
        ps_l = ctx.enter_context(nc.psum_tensor("ps_l", [P, 512], F32))
        ps_n = ctx.enter_context(nc.psum_tensor("ps_n", [P, 512], F32))

        loaded = sem("loaded_c")
        masks_made = sem("masks_made")
        pool_step = sem("pool_step_c")
        turned = sem("turned_c")
        turned_out = sem("turned_out_c")
        lower_ready = sem("lower_ready")
        x1_ready = sem("x1_ready")
        dve_step = sem("dve_step_c")
        var_ready = sem("var_ready_c")
        std_ready = sem("std_ready_c")
        xh_ready = sem("xh_ready")
        xh_stored = [sem(f"xh_stored{b}") for b in range(2)]
        xh_turned = sem("xh_turned")
        xh_t_out = sem("xh_t_out")
        logits_ready = sem("logits_ready")
        logits_out = sem("logits_out")
        exp_ready = sem("exp_ready_c")
        chosen_ready = sem("chosen_ready")
        counted = sem("counted")
        list_cleared = sem("list_cleared")
        list_ready = sem("list_ready")
        listed_done = sem("listed_done")
        list_loaded = sem("list_loaded")
        list_float = sem("list_float")
        list_turned = sem("list_turned")
        plan_done = sem("plan_done")

        with nc.Block() as block:

            @block.sync
            def _(sp):
                sp.dma_start(wu_a[:, :], a["Wu"][D:D + P, :]).then_inc(loaded, 16)
                sp.dma_start(wu_b[:, :], a["Wu"][D + P:D + N2, :]).then_inc(loaded, 16)
                sp.dma_start(router[:, :, :], a["router_w"].rearrange("(k p) e -> p k e", p=P)).then_inc(loaded, 16)
                sp.dma_start(rb_row[:, :], a["router_b"].partition_broadcast(P)).then_inc(loaded, 16)
                sp.dma_start(cb_row[:, :], a["corr_bias"].partition_broadcast(P)).then_inc(loaded, 16)
                with sp.Fori(0, T // 2) as i:
                    for b in range(2):
                        t = 2 * i + b
                        sp.wait_ge(xh_ready, t + 1)
                        sp.dma_start(xh_dram[ds(t * P, P), :], xh[b][:, :]).then_inc(xh_stored[b], 16)
                for b in range(2):
                    sp.wait_ge(xh_stored[b], 16 * (T // 2))
                sp.wait_ge(listed_done, 16 * CHOSEN * T)
                sp.dma_start(listed_i[:, :], list_dram[0:ROUTED_TILES * P, :].rearrange("(j p) o -> j (p o)", p=P))\
                    .then_inc(list_loaded, 16)

            @block.gpsimd
            def _(pool):
                nc.gpsimd.memset(zeros_i[:, :], 0).then_inc(pool_step, 1)
                nc.gpsimd.memset(before[:, :, :], 1.0).then_inc(pool_step, 1)
                nc.gpsimd.memset(before4[:, :, :], 1.0).then_inc(pool_step, 1)
                nc.gpsimd.memset(real[:, :, :], 1.0).then_inc(pool_step, 1)
                nc.gpsimd.memset(earlier_rows[:, :], 1.0).then_inc(pool_step, 1)
                nc.gpsimd.iota(thresholds[:, :], pattern=[[P, T]], base=0, channel_multiplier=0,
                               allow_small_or_imprecise_dtypes=True).then_inc(masks_made, 1)
                nc.gpsimd.iota(tile_ids[:, :], pattern=[[1, TILES]], base=0, channel_multiplier=0,
                               allow_small_or_imprecise_dtypes=True).then_inc(masks_made, 1)
                nc.gpsimd.iota(dump[:, :, :], pattern=[[P, CHOSEN], [0, T]], base=ROUTED_TILES * P, channel_multiplier=1,
                               allow_small_or_imprecise_dtypes=True).then_inc(masks_made, 1)
                nc.gpsimd.iota(token_ids[:, :], pattern=[[P, T]], base=0, channel_multiplier=1).then_inc(masks_made, 1)
                pool.wait_ge(pool_step, 5)
                for tile, n in ((before, EXPERTS), (before4, 4)):
                    nc.gpsimd.affine_select(out=tile[:, :, :], in_=tile[:, :, :], compare_op=ALU.is_gt, fill=0.0,
                                            base=0, pattern=[[1, n], [-1, n]], channel_multiplier=0)\
                        .then_inc(masks_made, 1)
                nc.gpsimd.affine_select(out=real[:, :, :], in_=real[:, :, :], compare_op=ALU.is_ge, fill=0.0,
                                        base=NODES - 1, pattern=[[-P, T], [0, EXPERTS]], channel_multiplier=-1)\
                    .then_inc(masks_made, 1)
                nc.gpsimd.affine_select(out=earlier_rows[:, :], in_=earlier_rows[:, :], compare_op=ALU.is_gt,
                                        fill=0.0, base=0, pattern=[[1, P]], channel_multiplier=-1)\
                    .then_inc(masks_made, 1)
                pool.dma_start(list_dram[0:ROUTED_TILES * P, :].rearrange("(j p) o -> j (p o)", p=P), zeros_i[:, :])\
                    .then_inc(list_cleared, 16)
                pool.wait_ge(masks_made, 8)
                nc.gpsimd.memset(token_of[:, TILES:TILES + 1], 0)
                for n in range(SHARED):
                    nc.gpsimd.tensor_copy(token_of[:, n * T:(n + 1) * T], token_ids[:, :])
                pool.wait_ge(list_cleared, 16)
                pool.wait_ge(list_ready, 1)
                for t in range(T):
                    for k in range(CHOSEN):
                        pool.indirect_dma_start(out=list_dram, out_offset=bass.IndirectOffsetOnAxis(
                            ap=list_i[:, k, t:t + 1], axis=0), in_=token_ids[:, t:t + 1], in_offset=None)\
                            .then_inc(listed_done, 16)

            @block.tensor
            def _(pe):
                pe.wait_ge(loaded, 80)

                def turn_out2(t):
                    if t >= 2:
                        pe.wait_ge(turned_out, t - 1)
                    nc.tensor.transpose(ps_a[t % 2][:, 0:P], h2[:, t, 0:P], ident[:, :])
                    nc.tensor.transpose(ps_a[t % 2][0:REST, P:2 * P], h2[:, t, P:N2], ident[:, :])\
                        .then_inc(turned, 1)

                def lower(t):
                    pe.wait_ge(turned_out, t + 1)
                    if t >= 1:
                        pe.wait_ge(x1_ready, t)
                    for k, w, m in ((0, wu_a, P), (1, wu_b, REST)):
                        for n in range(2):
                            last = nc.tensor.matmul(ps_x[:, n, 0:HALF], out2_t[t % 2][0:m, k, :],
                                                    w[:, n * HALF:(n + 1) * HALF], start=(k == 0), stop=(k == 1))
                    last.then_inc(lower_ready, 1)

                def turn_xh(t):
                    pe.wait_ge(xh_ready, t + 1)
                    if t >= 1:
                        pe.wait_ge(xh_t_out, t)
                    for k in range(KD):
                        last = nc.tensor.transpose(ps_b[:, k // 4, (k % 4) * P:(k % 4 + 1) * P],
                                                   xh[t % 2][:, k * P:(k + 1) * P], ident[:, :])
                    last.then_inc(xh_turned, 1)

                def route(t):
                    pe.wait_ge(xh_t_out, t + 1)
                    if t >= 1:
                        pe.wait_ge(logits_out, t)
                    for k in range(KD):
                        last = nc.tensor.matmul(ps_l[:, 0:EXPERTS], xh_t[t % 2][:, k, :], router[:, k, :],
                                                start=(k == 0), stop=(k == KD - 1))
                    last.then_inc(logits_ready, 1)

                turn_out2(0)
                for t in range(T + 2):
                    if t + 1 < T:
                        turn_out2(t + 1)
                    if t < T:
                        lower(t)
                    if 1 <= t <= T:
                        turn_xh(t - 1)
                    if t >= 2:
                        route(t - 2)
                pe.wait_ge(masks_made, 8)
                pe.wait_ge(chosen_ready, 1)
                flat = chosen[:, :, :].rearrange("p t e -> p (t e)")
                nc.tensor.matmul(ps_n[:, 0:TE], earlier_rows[:, :], flat, start=True, stop=True)
                nc.tensor.matmul(ps_n[:, 256:256 + TE], ones[:, :], flat, start=True, stop=True,
                                 skip_group_check=True).then_inc(counted, 1)
                pe.wait_ge(list_float, 1)
                nc.tensor.transpose(ps_l[:, 0:ROUTED_TILES], listed[:, :], ident[0:ROUTED_TILES, 0:ROUTED_TILES])\
                    .then_inc(list_turned, 1)

            @block.scalar
            def _(act):
                for t in range(T + 2):
                    b = t % 2
                    if t < T:
                        act.wait_ge(turned, t + 1)
                        if t >= 2:
                            act.wait_ge(lower_ready, t - 1)
                        nc.scalar.copy(out2_t[b][:, 0, :], ps_a[b][:, 0:P])
                        nc.scalar.copy(out2_t[b][0:REST, 1, :], ps_a[b][0:REST, P:2 * P]).then_inc(turned_out, 1)
                    if 1 <= t <= T:
                        act.wait_ge(var_ready, t)
                        nc.scalar.activation(std[:, :], mean_var[:, 1:2], ACT.Sqrt, bias=eps[:, 0:1],
                                             scale=1.0).then_inc(std_ready, 1)
                    if t >= 2:
                        act.wait_ge(xh_turned, t - 1)
                        if t >= 4:
                            act.wait_ge(logits_ready, t - 3)
                        nc.scalar.copy(xh_t[b][:, 0:4, :], ps_b[:, 0, 0:512])
                        nc.scalar.copy(xh_t[b][:, 4:KD, :], ps_b[:, 1, 0:256]).then_inc(xh_t_out, 1)
                act.wait_ge(logits_out, T)
                nc.scalar.activation(scores[:, :, :], logits[:, :, :], ACT.Exp, scale=-1.0).then_inc(exp_ready, 1)

            @block.vector
            def _(dve):
                step = Count()

                def norm(t):
                    x = acc[:, t, :]
                    for n in range(2):
                        last = nc.vector.bn_stats(stats[:, n, :], x[:, n * HALF:(n + 1) * HALF])
                    last.then_inc(dve_step, 1)
                    dve.wait_ge(dve_step, step.up())
                    nc.vector.bn_aggr(mean_var[:, :], stats[:, :, :]).then_inc(var_ready, 1)
                    dve.wait_ge(std_ready, t + 1)
                    nc.vector.reciprocal(rstd[:, :], std[:, :]).then_inc(dve_step, 1)
                    dve.wait_ge(dve_step, step.up())
                    if t >= 2:
                        dve.wait_ge(xh_stored[t % 2], 16 * (t // 2))
                        dve.wait_ge(xh_turned, t - 1)
                    nc.vector.tensor_scalar(xh[t % 2][:, :], x, mean_var[:, 0:1], rstd[:, 0:1], ALU.subtract,
                                            ALU.mult).then_inc(xh_ready, 1)

                for t in range(T + 2):
                    if t < T:
                        dve.wait_ge(lower_ready, t + 1)
                        x = acc[:, t, :].rearrange("p (n c) -> p n c", n=2)
                        nc.vector.tensor_tensor(x, ps_x[:, :, 0:HALF], x, ALU.add).then_inc(x1_ready, 1)
                        dve.wait_ge(x1_ready, t + 1)
                        norm(t)
                    if t >= 2:
                        if t == 2:
                            dve.wait_ge(loaded, 80)
                        dve.wait_ge(logits_ready, t - 1)
                        nc.vector.tensor_tensor(logits[:, t - 2, :], ps_l[:, 0:EXPERTS], rb_row[:, :],
                                                ALU.add).then_inc(logits_out, 1)

                def over_tiles(row):
                    return row.unsqueeze(1).to_broadcast([P, T, EXPERTS])

                def done(ins, by=1):
                    ins.then_inc(dve_step, 1)
                    dve.wait_ge(dve_step, step.up())

                V = nc.vector
                dve.wait_ge(masks_made, 8)
                dve.wait_ge(exp_ready, 1)
                done(V.tensor_scalar(scores[:, :, :], scores[:, :, :], 1.0, None, ALU.add))
                done(V.reciprocal(scores[:, :, :], scores[:, :, :]))
                done(V.tensor_tensor(biased[:, :, :], scores[:, :, :], over_tiles(cb_row[:, :]), ALU.add))
                by_pair = biased[:, :, :].rearrange("p t (g q r) -> p (t g q) r", g=4, q=2)
                hi, lo = (x[:, :, :, :].rearrange("p t g q -> p (t g q)") for x in (pair_hi, pair_lo))
                V.tensor_tensor(hi, by_pair[:, :, 0], by_pair[:, :, 1], ALU.max)
                done(V.tensor_tensor(lo, by_pair[:, :, 0], by_pair[:, :, 1], ALU.min))
                V.tensor_tensor(group_score[:, :, :], pair_hi[:, :, :, 0], pair_hi[:, :, :, 1], ALU.max)
                V.tensor_tensor(group_next[:, :, :], pair_hi[:, :, :, 0], pair_hi[:, :, :, 1], ALU.min)
                done(V.tensor_tensor(group_kept[:, :, :], pair_lo[:, :, :, 0], pair_lo[:, :, :, 1], ALU.max))
                done(V.tensor_tensor(group_next[:, :, :], group_next[:, :, :], group_kept[:, :, :], ALU.max))
                done(V.tensor_tensor(group_score[:, :, :], group_score[:, :, :], group_next[:, :, :], ALU.add))

                def ranks(values, n, first, out):
                    gt, eq = (x[:, :, :, :].rearrange("p t i j -> p t (i j)")[:, :, 0:n * n]
                              .rearrange("p t (i j) -> p t i j", i=n) for x in (ahead, tied))
                    mine = values.unsqueeze(3).to_broadcast([P, T, n, n])
                    other = values.unsqueeze(2).to_broadcast([P, T, n, n])
                    V.tensor_tensor(gt, other, mine, ALU.is_gt)
                    done(V.tensor_tensor(eq, other, mine, ALU.is_equal))
                    done(V.tensor_tensor(eq, eq, first.unsqueeze(1).to_broadcast([P, T, n, n]), ALU.mult))
                    done(V.tensor_tensor(gt, gt, eq, ALU.add))
                    done(V.tensor_reduce(out, gt, AX_X, ALU.add))

                ranks(group_score[:, :, :], 4, before4[:, :, :], group_next[:, :, :])
                done(V.tensor_scalar(group_kept[:, :, :], group_next[:, :, :], 2.0, None, ALU.is_lt))
                done(V.tensor_tensor(biased[:, :, :].rearrange("p t (g r) -> p t g r", g=4),
                                     biased[:, :, :].rearrange("p t (g r) -> p t g r", g=4),
                                     group_kept[:, :, :].unsqueeze(3).to_broadcast([P, T, 4, 4]), ALU.mult))
                ranks(biased[:, :, :], EXPERTS, before[:, :, :], rank[:, :, :])
                V.scalar_tensor_tensor(out=chosen[:, :, :], in0=rank[:, :, :], scalar=float(CHOSEN), in1=real[:, :, :],
                                       op0=ALU.is_lt, op1=ALU.mult).then_inc(chosen_ready, 1)
                dve.wait_ge(chosen_ready, 1)
                done(V.tensor_tensor(scores[:, :, :], scores[:, :, :], chosen[:, :, :], ALU.mult))
                done(V.tensor_reduce(total[:, :], scores[:, :, :], AX_X, ALU.add))
                done(V.tensor_scalar(total[:, :], total[:, :], 1e-20, None, ALU.add))
                done(V.reciprocal(total[:, :], total[:, :]))
                done(V.scalar_tensor_tensor(out=scores[:, :, :], in0=scores[:, :, :], scalar=SCALE,
                                            in1=total[:, :].unsqueeze(2).to_broadcast([P, T, EXPERTS]),
                                            op0=ALU.mult, op1=ALU.mult))
                prior = tied[:, :, :, :]
                done(V.tensor_tensor(prior, chosen[:, :, :].unsqueeze(2).to_broadcast([P, T, EXPERTS, EXPERTS]),
                                     before[:, :, :].unsqueeze(1).to_broadcast([P, T, EXPERTS, EXPERTS]), ALU.mult))
                done(V.tensor_reduce(nth[:, :, :], prior, AX_X, ALU.add))
                dve.wait_ge(counted, 1)
                in_tiles = ps_n[:, 256:256 + TE].rearrange("p (t e) -> p t e", e=EXPERTS)
                done(V.memset(earlier[:, 0, :], 0.0))
                for t in range(T):
                    done(V.tensor_tensor(earlier[:, t + 1, :], in_tiles[:, t, :], earlier[:, t, :], ALU.add))
                done(V.tensor_tensor(filled[:, :, :], earlier[:, T, :].unsqueeze(2).to_broadcast([P, EXPERTS, T]),
                                     thresholds[:, :].unsqueeze(1).to_broadcast([P, EXPERTS, T]), ALU.is_gt))
                done(V.tensor_reduce(n_tiles[:, :], filled[:, :, :], AX_X, ALU.add))
                done(V.tensor_tensor(ahead[:, 0, :, :], n_tiles[:, :].unsqueeze(1).to_broadcast([P, EXPERTS, EXPERTS]),
                                     before[:, :, :], ALU.mult))
                done(V.tensor_reduce(starts[:, :], ahead[:, 0, :, :], AX_X, ALU.add))
                for n in range(SHARED):
                    V.memset(ends[:, n:n + 1], float((n + 1) * T))
                done(V.scalar_tensor_tensor(out=ends[:, SHARED:ALL], in0=starts[:, :], scalar=float(SHARED_TILES),
                                            in1=n_tiles[:, :], op0=ALU.add, op1=ALU.add))
                V.tensor_copy(ends_i[:, :], ends[0:1, :])
                done(V.tensor_tensor(passed[:, :, :], tile_ids[:, :].unsqueeze(2).to_broadcast([P, TILES, ALL]),
                                     ends[:, :].unsqueeze(1).to_broadcast([P, TILES, ALL]), ALU.is_ge))
                done(V.tensor_reduce(tile_f[:, :], passed[:, :, :], AX_X, ALU.add))
                done(V.tensor_scalar(tile_f[:, :], tile_f[:, :], float(ALL - 1), None, ALU.min))
                V.tensor_copy(tile_expert[:, :], tile_f[0:1, :])
                done(V.tensor_tensor(place[:, :, :], ps_n[:, 0:TE].rearrange("p (t e) -> p t e", e=EXPERTS),
                                     earlier[:, 0:T, :], ALU.add))
                done(V.scalar_tensor_tensor(out=place[:, :, :], in0=over_tiles(starts[:, :]), scalar=float(P),
                                            in1=place[:, :, :], op0=ALU.mult, op1=ALU.add))
                for k in range(CHOSEN):
                    done(V.scalar_tensor_tensor(out=mask[:, :, :], in0=nth[:, :, :], scalar=float(k),
                                                in1=chosen[:, :, :], op0=ALU.is_equal, op1=ALU.mult))
                    done(V.tensor_tensor(picked[:, :, :], mask[:, :, :], scores[:, :, :], ALU.mult))
                    done(V.tensor_reduce(mix[:, k, :], picked[:, :, :], AX_X, ALU.add))
                    done(V.tensor_tensor(picked[:, :, :], mask[:, :, :], place[:, :, :], ALU.mult))
                    done(V.tensor_reduce(place_k[:, k, :], picked[:, :, :], AX_X, ALU.add))
                wide_dump = dump[:, :, :]
                wide_real = real[:, :, 0].unsqueeze(1).to_broadcast([P, CHOSEN, T])
                done(V.tensor_tensor(list_k[:, :, :], place_k[:, :, :], wide_dump, ALU.subtract))
                done(V.tensor_tensor(list_k[:, :, :], list_k[:, :, :], wide_real, ALU.mult))
                done(V.tensor_tensor(list_k[:, :, :], list_k[:, :, :], wide_dump, ALU.add))
                V.tensor_copy(list_i[:, :, :], list_k[:, :, :]).then_inc(list_ready, 1)
                V.tensor_scalar(place_i[:, :, :], place_k[:, :, :], float(SHARED_TILES * P), None, ALU.add)\
                    .then_inc(plan_done, 1)
                dve.wait_ge(list_loaded, 16)
                V.tensor_copy(listed[:, :], listed_i[:, :]).then_inc(list_float, 1)
                dve.wait_ge(list_turned, 1)
                V.tensor_copy(token_of[:, SHARED_TILES:TILES], ps_l[:, 0:ROUTED_TILES]).then_inc(plan_done, 1)


def experts(nc, a, keep):
    ctx = ExitStack()
    with ctx:
        def sb(name, shape, dt=F32):
            return ctx.enter_context(nc.sbuf_tensor(name, shape, dt))

        def sem(name):
            return ctx.enter_context(nc.semaphore(name))

        ident, token_of, tile_expert, ends_i = keep["ident"], keep["token_of"], keep["tile_expert"], keep["ends_i"]
        xh_dram, y_dram = keep["xh_dram"], keep["y_dram"]
        wg = sb("wg", [P, 2, KD * I])
        wu = sb("wu_e", [P, 2, KD * I])
        wd = sb("wd", [P, 2, KI * D])
        bg = sb("bg", [P, 2 * I])
        bu = sb("bu", [P, 2 * I])
        bd = sb("bd", [P, 2 * D])
        x = [sb(f"x_e{b}", [P, D]) for b in range(2)]
        x_t = [sb(f"x_t{b}", [P, KD, P]) for b in range(2)]
        at = [sb(f"at{b}", [P, 1], I32) for b in range(2)]
        gate = sb("gate", [P, I])
        up = sb("up", [P, I])
        inner = [sb(f"inner{b}", [P, I]) for b in range(2)]
        inner_t = sb("inner_t", [P, KI, P])
        y = [sb(f"y{b}", [P, D]) for b in range(2)]

        ps_x = ctx.enter_context(nc.psum_tensor("ps_xe", [P, 512], F32))
        ps_i = ctx.enter_context(nc.psum_tensor("ps_ie", [P, 512], F32))
        ps_g = [ctx.enter_context(nc.psum_tensor(f"ps_ge{b}", [P, 512], F32)) for b in range(2)]
        ps_u = [ctx.enter_context(nc.psum_tensor(f"ps_ue{b}", [P, 512], F32)) for b in range(2)]
        ps_y = ctx.enter_context(nc.psum_tensor("ps_ye", [P, 2, 512], F32))

        arrived = [sem(f"arrived{b}") for b in range(2)]
        expert_ready = sem("expert_ready")
        no_bias = sem("no_bias")
        at_ready = sem("at_ready")
        gathered = [sem(f"gathered{b}") for b in range(2)]
        turned = sem("turned_e")
        turned_out = sem("turned_out_e")
        gate_ready = sem("gate_ready")
        up_ready = sem("up_ready")
        gate_biased = sem("gate_biased")
        up_biased = sem("up_biased")
        silu_ready = sem("silu_ready")
        inner_ready = sem("inner_ready")
        inner_turned = sem("inner_turned")
        inner_out = sem("inner_out")
        down_ready = sem("down_ready")
        y_ready = sem("y_ready")
        y_stored = [sem(f"y_stored{b}") for b in range(2)]

        STEPS = TILES // 2
        LOADS = 6

        with nc.Block() as block:

            @block.sync
            def _(sp):
                def load(b, gate_w, up_w, down_w, gate_b, up_b, down_b):
                    for dst, src in ((wg, gate_w), (wu, up_w)):
                        sp.dma_start(dst[:, b, :].rearrange("p (k n) -> p k n", k=KD),
                                     src.rearrange("(k p) n -> p k n", p=P)).then_inc(arrived[b], 16)
                    sp.dma_start(wd[:, b, :].rearrange("p (k n) -> p k n", k=KI),
                                 down_w.rearrange("(k p) n -> p k n", p=P)).then_inc(arrived[b], 16)
                    for dst, src, n in ((bg, gate_b, I), (bu, up_b, I), (bd, down_b, D)):
                        if src is not None:
                            sp.dma_start(dst[:, b * n:(b + 1) * n], src.partition_broadcast(P))\
                                .then_inc(arrived[b], 16)

                for b in range(SHARED):
                    cols = slice(b * I, (b + 1) * I)
                    load(b, a["sWg"][:, cols], a["sWu"][:, cols], a["sWd"][cols, :], a["sbg"][cols], a["sbu"][cols],
                         a["sbd"] if b == 0 else None)
                sp.wait_ge(arrived[0], 16 * LOADS)
                sp.nop().then_inc(expert_ready, 1)
                with sp.Fori(0, EXPERTS // 2) as i:
                    for b in range(2):
                        other = 1 - b
                        sp.wait_ge(arrived[other], (i + 1) * (16 * LOADS) - (16 if other == 1 else 0)
                                   + (16 * LOADS if b == 1 else 0))
                        sp.nop().then_inc(expert_ready, 1)
                        end = sp.value_load(ends_i[0:1, ds(2 * i + b, 1)], min_val=0, max_val=TILES)
                        sp.wait_ge(y_ready, AHEAD + end)
                        e = 2 * i + b
                        load(b, *(a[n][ds(e, 1)].rearrange("o k n -> (o k) n") for n in ("gWg", "gWu", "gWd")),
                             *(a[n][ds(e, 1)].rearrange("o n -> (o n)") for n in ("gbg", "gbu", "gbd")))
                sp.wait_ge(arrived[1], 16 * LOADS * (1 + EXPERTS // 2) - 16)
                sp.nop().then_inc(expert_ready, 1)

            @block.gpsimd
            def _(pool):
                nc.gpsimd.memset(bd[:, D:2 * D], 0.0).then_inc(no_bias, 1)
                pool.wait_ge(no_bias, 1)
                nc.gpsimd.tensor_copy(at[0][:, :], token_of[:, 0:1]).then_inc(at_ready, 1)
                with pool.Fori(0, STEPS) as i:
                    for b in range(2):
                        j = 2 * i + b
                        other = 1 - b
                        pool.wait_ge(turned, AHEAD + 2 * j)
                        pool.wait_ge(at_ready, j + 1)
                        nc.gpsimd.tensor_copy(at[other][:, :], token_of[:, ds(j + 1, 1)]).then_inc(at_ready, 1)
                        pool.indirect_dma_start(out=x[b][:, :], out_offset=None, in_=xh_dram,
                                                in_offset=bass.IndirectOffsetOnAxis(ap=at[b][:, :], axis=0))\
                            .then_inc(gathered[b], 16)

            @block.tensor
            def _(pe):
                pe.nop().then_inc(turned, AHEAD)
                pe.nop().then_inc(down_ready, AHEAD)
                def turn(j, b, part):
                    if part == 0:
                        pe.wait_ge(gathered[b], (j // 2 + 1) * 16 if isinstance(j, int) else j * 8 + 16 - 8 * b)
                    if not isinstance(j, int) or j + part > 0:
                        pe.wait_ge(turned_out, j * 2 + part)
                    for k in range(3):
                        c = 3 * part + k
                        last = nc.tensor.transpose(ps_x[:, k * P:(k + 1) * P], x[b][:, c * P:(c + 1) * P], ident[:, :])
                    last.then_inc(turned, 1)

                def widen(b, w, buffer, ps, ready):
                    for k in range(KD):
                        last = nc.tensor.matmul(ps[b][:, 0:I], x_t[b][:, k, :],
                                                w[:, ds(buffer, 1), k * I:(k + 1) * I].rearrange("p o n -> p (o n)"),
                                                start=(k == 0), stop=(k == KD - 1))
                    last.then_inc(ready, 1)

                def expert_of(j):
                    return pe.value_load(tile_expert[0:1, ds(j, 1)], min_val=0, max_val=ALL - 1)

                def step(j, b, turning, widening):
                    other = 1 - b
                    e = expert_of(j)
                    if turning:
                        turn(j + 2, b, 0)
                    if widening:
                        e_next = expert_of(j + 1)
                        pe.wait_ge(expert_ready, e_next + 1)
                        pe.wait_ge(turned_out, 2 * j + 4)
                        pe.wait_ge(inner_ready, AHEAD + j)
                        widen(other, wg, e_next % 2, ps_g, gate_ready)
                    if turning:
                        turn(j + 2, b, 1)
                    pe.wait_ge(inner_ready, AHEAD + j + 1)
                    pe.wait_ge(inner_out, AHEAD + j)
                    for k in range(KI):
                        last = nc.tensor.transpose(ps_i[:, k * P:(k + 1) * P], inner[b][:, k * P:(k + 1) * P],
                                                   ident[:, :])
                    last.then_inc(inner_turned, 1)
                    if widening:
                        widen(other, wu, e_next % 2, ps_u, up_ready)
                    pe.wait_ge(inner_out, AHEAD + j + 1)
                    pe.wait_ge(y_ready, AHEAD + j)
                    buffer = e % 2
                    for k in range(KI):
                        for n in range(2):
                            col = k * D + n * HALF
                            last = nc.tensor.matmul(ps_y[:, n, 0:HALF], inner_t[:, k, :],
                                                    wd[:, ds(buffer, 1), col:col + HALF].rearrange("p o n -> p (o n)"),
                                                    start=(k == 0), stop=(k == KI - 1))
                    last.then_inc(down_ready, 1)

                for j in range(2):
                    turn(j, j, 0)
                    turn(j, j, 1)
                pe.wait_ge(expert_ready, 1)
                pe.wait_ge(turned_out, 2)
                widen(0, wg, 0, ps_g, gate_ready)
                widen(0, wu, 0, ps_u, up_ready)
                with pe.Fori(0, STEPS - 1) as i:
                    for b in range(2):
                        step(2 * i + b, b, True, True)
                step(TILES - 2, 0, False, True)
                step(TILES - 1, 1, False, False)

            @block.scalar
            def _(act):
                for b in range(2):
                    act.nop().then_inc(y_stored[b], 16 * AHEAD)
                act.nop().then_inc(inner_out, AHEAD)
                def take_turned(j, b, part):
                    act.wait_ge(turned, AHEAD + 2 * j + part + 1)
                    nc.scalar.copy(x_t[b][:, 3 * part:3 * part + 3, :], ps_x[:, 0:I]).then_inc(turned_out, 1)

                def silu(j):
                    act.wait_ge(gate_biased, j + 1)
                    nc.scalar.activation(gate[:, :], gate[:, :], ACT.Silu).then_inc(silu_ready, 1)

                def step(j, b, turning, widening):
                    if turning:
                        act.wait_ge(up_ready, j + 1)
                        take_turned(j + 2, b, 0)
                        take_turned(j + 2, b, 1)
                    act.wait_ge(inner_turned, j + 1)
                    act.wait_ge(down_ready, AHEAD + j)
                    nc.scalar.copy(inner_t[:, :, :], ps_i[:, 0:I]).then_inc(inner_out, 1)
                    if widening:
                        silu(j + 1)
                    act.wait_ge(y_ready, AHEAD + j + 1)
                    act.dma_start(y_dram[ds(j * P, P), :], y[b][:, :]).then_inc(y_stored[b], 16)

                for j in range(2):
                    take_turned(j, j, 0)
                    take_turned(j, j, 1)
                silu(0)
                with act.Fori(0, STEPS - 1) as i:
                    for b in range(2):
                        step(2 * i + b, b, True, True)
                step(TILES - 2, 0, False, True)
                step(TILES - 1, 1, False, False)
                for b in range(2):
                    act.wait_ge(y_stored[b], 16 * (STEPS + AHEAD))

            @block.vector
            def _(dve):
                dve.nop().then_inc(inner_ready, AHEAD)
                dve.nop().then_inc(y_ready, AHEAD)
                def row(rows, buffer, n):
                    return rows[:, ds(buffer * n, n)]

                def expert_of(j):
                    return dve.value_load(tile_expert[0:1, ds(j, 1)], min_val=0, max_val=ALL - 1) % 2

                def inside(j, b, buffer):
                    dve.wait_ge(gate_ready, j + 1)
                    nc.vector.tensor_tensor(gate[:, :], ps_g[b][:, 0:I], row(bg, buffer, I), ALU.add)\
                        .then_inc(gate_biased, 1)
                    dve.wait_ge(up_ready, j + 1)
                    nc.vector.tensor_tensor(up[:, :], ps_u[b][:, 0:I], row(bu, buffer, I), ALU.add)\
                        .then_inc(up_biased, 1)
                    dve.wait_ge(silu_ready, j + 1)
                    dve.wait_ge(up_biased, j + 1)
                    nc.vector.tensor_tensor(inner[b][:, :], gate[:, :], up[:, :], ALU.mult).then_inc(inner_ready, 1)
                    dve.wait_ge(inner_ready, AHEAD + j + 1)

                def step(j, b, widening, stored):
                    buffer = expert_of(j)
                    if widening:
                        inside(j + 1, 1 - b, expert_of(j + 1))
                    dve.wait_ge(down_ready, AHEAD + j + 1)
                    dve.wait_ge(y_stored[b], stored)
                    nc.vector.tensor_tensor(y[b][:, :].rearrange("p (n c) -> p n c", n=2), ps_y[:, :, 0:HALF],
                                            row(bd, buffer, D).rearrange("p (n c) -> p n c", n=2),
                                            ALU.add).then_inc(y_ready, 1)

                dve.wait_ge(no_bias, 1)
                dve.wait_ge(expert_ready, 1)
                inside(0, 0, 0)
                with dve.Fori(0, STEPS - 1) as i:
                    for b in range(2):
                        step(2 * i + b, b, True, 16 * (i + AHEAD))
                step(TILES - 2, 0, True, 16 * (STEPS - 1 + AHEAD))
                step(TILES - 1, 1, False, 16 * (STEPS - 1 + AHEAD))


def combine(nc, a, keep, out):
    ctx = ExitStack()
    with ctx:
        def sb(name, shape, dt=F32):
            return ctx.enter_context(nc.sbuf_tensor(name, shape, dt))

        def sem(name):
            return ctx.enter_context(nc.semaphore(name))

        acc, place_i, mix, y_dram = keep["acc"], keep["place_i"], keep["mix"], keep["y_dram"]
        both = [sb(f"both{b}", [P, SHARED, D]) for b in range(2)]
        routed = [[sb(f"routed{b}{k}", [P, D]) for k in range(CHOSEN)] for b in range(2)]
        shared_in = [sem(f"shared_in{b}") for b in range(2)]
        routed_in = [[sem(f"routed_in{b}{k}") for k in range(CHOSEN)] for b in range(2)]
        summed = sem("summed")
        added = sem("added")
        stored = sem("stored")

        with nc.Block() as block:

            @block.sync
            def _(sp):
                for t in range(T):
                    b = t % 2
                    if t >= 2:
                        sp.wait_ge(summed, t - 1)
                    sp.dma_start(both[b][:, :, :], y_dram[0:SHARED_TILES * P, :].rearrange(
                        "(s t p) n -> t p s n", s=SHARED, t=T)[t]).then_inc(shared_in[b], 16)

            @block.gpsimd
            def _(pool):
                for t in range(T):
                    b = t % 2
                    if t >= 2:
                        pool.wait_ge(summed, t - 1)
                    for k in range(CHOSEN):
                        pool.indirect_dma_start(out=routed[b][k][:, :], out_offset=None, in_=y_dram,
                                                in_offset=bass.IndirectOffsetOnAxis(ap=place_i[:, k, t:t + 1], axis=0))\
                            .then_inc(routed_in[b][k], 16)

            @block.vector
            def _(dve):
                step = Count()
                for t in range(T):
                    b = t % 2
                    row = acc[:, t, :]
                    dve.wait_ge(shared_in[b], 16 * (t // 2 + 1))
                    for n in range(SHARED):
                        nc.vector.tensor_tensor(row, both[b][:, n, :], row, ALU.add).then_inc(added, 1)
                        dve.wait_ge(added, step.up())
                    for k in range(CHOSEN):
                        dve.wait_ge(routed_in[b][k], 16 * (t // 2 + 1))
                        last = nc.vector.scalar_tensor_tensor(out=row, in0=routed[b][k][:, :],
                                                              scalar=mix[:, k, t:t + 1], in1=row,
                                                              op0=ALU.mult, op1=ALU.add)
                        if k < CHOSEN - 1:
                            last.then_inc(added, 1)
                            dve.wait_ge(added, step.up())
                    last.then_inc(summed, 1)

            @block.scalar
            def _(act):
                for t in range(T):
                    act.wait_ge(summed, t + 1)
                    act.dma_start(out[t * P:(t + 1) * P, :], acc[:, t, :]).then_inc(stored, 16)
                act.wait_ge(stored, 16 * T)


def program(nc, a, out):
    ctx = ExitStack()
    with ctx:
        keep = {}

        def sb(name, shape, dt=F32):
            keep[name] = ctx.enter_context(nc.sbuf_tensor(name, shape, dt))
        sb("ident", [P, P])
        sb("ones", [P, P])
        sb("eps", [P, 1])
        sb("acc", [P, T, D])
        sb("token_of", [P, TILES + 1], I32)
        sb("place_i", [P, CHOSEN, T], I32)
        sb("mix", [P, CHOSEN, T])
        sb("tile_expert", [1, TILES], I32)
        sb("ends_i", [1, ALL], I32)
        keep["xh_dram"] = nc.dram_tensor("xh_dram", (NP, D), F32).ap()
        keep["list_dram"] = nc.dram_tensor("list_dram", ((ROUTED_TILES + CHOSEN) * P, 1), I32).ap()
        keep["y_dram"] = nc.dram_tensor("y_dram", (TILES * P, D), F32).ap()
        with ExitStack() as graph:
            def gb(name, shape, dt=F32):
                keep[name] = graph.enter_context(nc.sbuf_tensor(name, shape, dt))
            gb("h1", [P, T, H1 * (C1 + 2)])
            gb("counts", [P, T, NP], U16)
            for name, heads in (("s_src1", H1), ("s_dst1", H1), ("s_src2", H2), ("s_dst2", H2)):
                gb(name, [P, heads * T])
            edges_and_projection(nc, a, keep)
            gb("h2", [P, T, H2 * (C2 + 2)])
            gb("no_edge", [P, T, NP], BF16)
            attention(nc, a, keep, 1, H1, C1)
            second_projection(nc, a, keep)
            attention(nc, a, keep, 2, H2, C2)
            update_and_route(nc, a, keep)
        experts(nc, a, keep)
        combine(nc, a, keep, out)


def kernel(**inputs):
    import numpy as _np
    import concourse.bacc as _bacc
    from concourse import mybir as _mybir
    from concourse.bass_utils import run_bass_kernel_spmd as _run

    given = {name.replace("L0_gnn_", "").replace("L0_ffn_", ""): _np.asarray(v) for name, v in inputs.items()}
    spare = LISTED * CHUNK * P - EDGES

    def grouped(edges, filler):
        padded = _np.concatenate([edges, _np.full(spare, filler, edges.dtype)])
        return padded.reshape(LISTED, P, CHUNK).transpose(1, 0, 2).reshape(P, LISTED * CHUNK)

    given["src"] = grouped(given["src"], PAD_SRC)
    given["dst"] = grouped(given["dst"], NODES - 1)
    given["x"] = _np.concatenate([given["x"], _np.zeros((NP + P - NODES, D), given["x"].dtype)])
    given["router_w"] = given["router_w"].T
    for name in ("a_src1", "a_dst1", "a_src2", "a_dst2"):
        given[name] = given[name].reshape(-1)

    nc = _bacc.Bacc("TRN2", target_bir_lowering=False, num_devices=1)
    arrays, a = {}, {}
    for name, value in given.items():
        value = _np.ascontiguousarray(value)
        arrays[f"in_{name}"] = value
        a[name] = nc.dram_tensor(f"in_{name}", value.shape, _mybir.dt.from_np(value.dtype), kind="ExternalInput").ap()
    out = nc.dram_tensor("out", (NP, D), F32, kind="ExternalOutput").ap()
    program(nc, a, out)
    r = _run(nc, [arrays], core_ids=[0])
    return r.results[0]["out"][:NODES]
```

```python
from contextlib import ExitStack, contextmanager

import concourse.bass as bass
from concourse import mybir

ALU = mybir.AluOpType
ACT = mybir.ActivationFunctionType
AX_X = mybir.AxisListType.X
F32 = mybir.dt.float32
BF16 = mybir.dt.bfloat16
F16 = mybir.dt.float16
F32R = mybir.dt.float32r
I32 = mybir.dt.int32
U16 = mybir.dt.uint16

P = 128
NODES = 1250
EDGES = 40000
D = 768
T = -(-NODES // P)
NP = T * P
KD = D // P
HALF = D // 2
EPS = 1e-5
SLOPE = 0.2

CHUNK = 4
GROUPS = 80
LISTED = GROUPS + 1
WIN = 64
PAD_SRC = 4095
NEG = -3.0e38

H1, C1 = 4, 192
H2, C2 = 2, 96

EXPERTS = 16
CHOSEN = 4
IN_GROUP = 4
SCALE = 2.5
I = 384
KI = I // P
SHARED = 2
PAIRS = -(-((NODES * CHOSEN + EXPERTS * P) // P) // 2)
TILES = 2 * PAIRS
SURE = NODES * CHOSEN // P // 2 * 2
PIECES = KD + KI
RAWS = 3
COUNT_AT = 4
MASKS = 7

AHEAD = 1

ds = bass.ds


class Count:

    def __init__(self):
        self.fixed = 0
        self.loops = []

    def up(self, by=1):
        self.fixed += by
        return self.now()

    def now(self):
        value = self.fixed
        for turn, per in self.loops:
            value = turn * per + value
        return value

    @contextmanager
    def turns(self, turn, per, count):
        start = self.fixed
        self.loops.append((turn, per))
        yield
        self.loops.pop()
        assert self.fixed - start == per, (self.fixed - start, per)
        self.fixed = start + per * count


def edges_and_projection(nc, a, keep):
    ctx = ExitStack()
    with ctx:
        def sb(name, shape, dt=F32):
            return ctx.enter_context(nc.sbuf_tensor(name, shape, dt))

        semaphores = []

        def sem(name):
            semaphores.append(nc.alloc_semaphore(name))
            return semaphores[-1]

        counts, acc, h1, s_src, s_dst = keep["counts"], keep["acc"], keep["h1"], keep["s_src1"], keep["s_dst1"]
        ident, ones, eps = keep["ident"], keep["ones"], keep["eps"]

        src_f = sb("src_f", [P, LISTED * CHUNK])
        dst_f = sb("dst_f", [P, LISTED * CHUNK])
        dst_w = sb("dst_w", [P, LISTED * CHUNK])
        node_ids = sb("node_ids", [P, NP], F16)
        group_hi = sb("group_hi", [P, LISTED])
        lo = sb("lo", [LISTED, 1])
        hi = sb("hi", [LISTED, 1])
        bases = sb("bases", [LISTED, LISTED + 1])
        base_i = sb("base_i", [1, LISTED + 1], I32)
        hot_src = [sb(f"hot_src{b}", [P, CHUNK, NP], BF16) for b in range(2)]
        hot_dst = [sb(f"hot_dst{b}", [P, CHUNK, WIN], BF16) for b in range(2)]
        w1 = sb("w1", [P, KD, D])
        wu = sb("wu", [P, KD, D])
        g_row = sb("g_row", [P, D])
        b_row = sb("b_row", [P, D])
        bu_row = sb("bu_row", [P, D])
        a_src = sb("a_src", [P, D])
        a_dst = sb("a_dst", [P, D])
        x_in = [sb(f"x_in{b}", [P, D]) for b in range(2)]
        x0 = [sb(f"x0_{b}", [P, D]) for b in range(2)]
        xn = [sb(f"xn_{b}", [P, D]) for b in range(2)]
        x0_t = [sb(f"x0_t{b}", [P, KD, P]) for b in range(2)]
        xn_t = [sb(f"xn_t{b}", [P, KD, P]) for b in range(2)]
        stats = sb("stats", [P, 2, 6])
        mean_var = sb("mean_var", [P, 2])
        std = sb("std", [P, 1])
        rstd = sb("rstd", [P, 1])
        dot = sb("dot", [P, H1, C1])
        LIST = LISTED * CHUNK
        flat = dot[:, :, :].rearrange("p k c -> p (k c)")
        src_i, dst_i = flat[:, 0:LIST].bitcast(I32), flat[:, LIST:2 * LIST].bitcast(I32)
        group_lo = flat[:, 2 * LIST:2 * LIST + LISTED]
        zeros = keep["h2"][:, :, :].rearrange("p t c -> p (t c)")[:, 0:D]

        ps_t = ctx.enter_context(nc.psum_tensor("ps_t", [P, 2, 512], F32))
        ps_h = ctx.enter_context(nc.psum_tensor("ps_h", [P, 2, 512], F32))
        ps_u = ctx.enter_context(nc.psum_tensor("ps_u", [P, 2, 512], F32))
        ps_c = ctx.enter_context(nc.psum_tensor("ps_c", [P, 2, 512], F32))

        edges_in = sem("edges_in")
        weights_in = sem("weights_in")
        rows_in = sem("rows_in")
        x_loaded = [sem(f"x_loaded{b}") for b in range(2)]
        consts_made = sem("consts_made")
        range_found = sem("range_found")
        range_turned = sem("range_turned")
        base_found = sem("base_found")
        base_spread = sem("base_spread")
        base_ready = sem("base_ready")
        counts_clear = sem("counts_clear")
        zeros_made = sem("zeros_made")
        lists_clear = sem("lists_clear")
        hot_ready = sem("hot_ready")
        pairs_ready = sem("pairs_ready")
        pairs_added = sem("pairs_added")
        var_ready = sem("var_ready")
        std_ready = sem("std_ready")
        x0_ready = sem("x0_ready")
        xhat_ready = sem("xhat_ready")
        xn_ready = sem("xn_ready")
        acc_seeded = sem("acc_seeded")
        turned = sem("turned")
        turned_out = sem("turned_out")
        h_ready = sem("h_ready")
        u_ready = sem("u_ready")
        h_out = sem("h_out")
        u_out = sem("u_out")
        dots_done = sem("dots_done")
        dve_step = sem("dve_step")
        pool_step = sem("pool_step")
        gen_hot = sem("gen_hot")
        gen_pairs = sem("gen_pairs")
        gen_added = sem("gen_added")

        PAIRS = T // 2
        PER_TILE = GROUPS // T
        LIST_CLEAR = (TILES + CHOSEN) // PAIRS
        Y_CLEAR = -(-(TILES - SURE) // PAIRS)
        assert LIST_CLEAR * PAIRS == TILES + CHOSEN

        with nc.Block() as block:

            @block.sync
            def _(sp):
                sp.dma_start(dst_i, a["dst"]).then_inc(edges_in, 16)
                sp.dma_start(x_in[0][:, :], a["x"][0:P, :]).then_inc(x_loaded[0], 16)
                sp.dma_start(src_i, a["src"]).then_inc(edges_in, 16)
                for row, source in ((g_row, "norm_g"), (b_row, "norm_b"), (bu_row, "bu"),
                                    (a_src, "a_src1"), (a_dst, "a_dst1")):
                    sp.dma_start(row[:, :], a[source].partition_broadcast(P)).then_inc(rows_in, 16)
                with sp.Fori(0, PAIRS) as i:
                    for b in range(2):
                        t = 2 * i + b
                        sp.wait_ge(x0_ready, AHEAD + t)
                        sp.wait_ge(acc_seeded, AHEAD + t)
                        sp.dma_start(x_in[1 - b][:, :], a["x"][ds((t + 1) * P, P), :]).then_inc(x_loaded[1 - b], 16)

            @block.gpsimd
            def _(pool):
                pool.nop().then_inc(acc_seeded, AHEAD)
                pool.nop().then_inc(xn_ready, AHEAD)
                nc.gpsimd.memset(ident[:, :], 0.0).then_inc(pool_step, 1)
                nc.gpsimd.memset(ones[:, :], 1.0).then_inc(consts_made, 1)
                nc.gpsimd.memset(eps[:, :], EPS).then_inc(consts_made, 1)
                pool.wait_ge(pool_step, 1)
                nc.gpsimd.affine_select(out=ident[:, :], in_=ident[:, :], compare_op=ALU.not_equal, fill=1.0,
                                        base=0, pattern=[[-1, P]], channel_multiplier=1).then_inc(consts_made, 1)
                nc.gpsimd.iota(node_ids[:, :], pattern=[[1, NP]], base=0, channel_multiplier=0,
                               allow_small_or_imprecise_dtypes=True).then_inc(consts_made, 1)
                nc.gpsimd.memset(counts[:, :, :], 0).then_inc(counts_clear, 1)
                nc.gpsimd.memset(h1[:, :, :], 1.0).then_inc(counts_clear, 1)
                nc.gpsimd.memset(zeros, 0.0).then_inc(zeros_made, 1)
                step = Count()
                step.up()
                pool.wait_ge(rows_in, 16 * 5)

                def seed_and_scale(t, b, loaded):
                    pool.wait_ge(x_loaded[b], loaded)
                    nc.gpsimd.tensor_tensor(acc[:, t, :], x_in[b][:, :], bu_row[:, :], ALU.add).then_inc(acc_seeded, 1)
                    pool.wait_ge(xhat_ready, AHEAD + t + 1)
                    nc.gpsimd.tensor_tensor(xn[b][:, :], xn[b][:, :], g_row[:, :], ALU.mult).then_inc(pool_step, 1)
                    pool.wait_ge(pool_step, step.up())
                    nc.gpsimd.tensor_tensor(xn[b][:, :], xn[b][:, :], b_row[:, :], ALU.add).then_inc(xn_ready, 1)

                with pool.Fori(0, PAIRS) as i, step.turns(i, 2, PAIRS):
                    for b in range(2):
                        seed_and_scale(2 * i + b, b, (i + 1) * 16)

            @block.scalar
            def _(act):
                act.nop().then_inc(turned_out, AHEAD)
                act.nop().then_inc(h_out, AHEAD)
                act.dma_start(wu[:, :, :], a["Wu"][0:D, :].rearrange("(k p) n -> p k n", p=P)).then_inc(weights_in, 16)
                act.dma_start(w1[:, :, :], a["W1"].rearrange("(k p) n -> p k n", p=P)).then_inc(weights_in, 16)
                act.wait_ge(consts_made, 2)
                act.wait_ge(counts_clear, 2)
                act.wait_ge(zeros_made, 1)

                def clear(name, first, tiles):
                    act.dma_start(keep[name][ds(first * P, tiles * P), :].rearrange("(t p) d -> p t d", p=P),
                                  zeros.unsqueeze(1).to_broadcast([P, tiles, D])).then_inc(lists_clear, 16)

                def root(count):
                    act.wait_ge(var_ready, count)
                    nc.scalar.activation(std[:, :], mean_var[:, 1:2], ACT.Sqrt, bias=eps[:, 0:1],
                                         scale=1.0).then_inc(std_ready, 1)

                def take_turned(out, count):
                    act.wait_ge(turned, AHEAD + count)
                    nc.scalar.copy(out[:, 0:4, :], ps_t[:, 0, 0:512])
                    nc.scalar.copy(out[:, 4:KD, :], ps_t[:, 1, 0:256]).then_inc(turned_out, 1)

                root(1)
                root(2)
                with act.Fori(0, PAIRS) as i:
                    clear("list_dram", i * LIST_CLEAR, LIST_CLEAR)
                    clear("y_dram", i * Y_CLEAR + (TILES - PAIRS * Y_CLEAR), Y_CLEAR)
                    for b in range(2):
                        t = 2 * i + b
                        take_turned(x0_t[b], 2 * t + 1)
                        root(2 * t + 3)
                        take_turned(xn_t[b], 2 * t + 2)
                        root(2 * t + 4)
                        act.wait_ge(h_ready, t + 1)
                        for n in range(2):
                            last = nc.scalar.copy(h1[:, t, 2 * n * (C1 + 2):2 * (n + 1) * (C1 + 2)]
                                                  .rearrange("p (h c) -> p h c", h=2)[:, :, 0:C1],
                                                  ps_h[:, n, 0:HALF].rearrange("p (h c) -> p h c", h=2))
                        last.then_inc(h_out, 1)
                act.wait_ge(lists_clear, 32 * PAIRS)

            @block.tensor
            def _(pe):
                pe.nop().then_inc(turned, AHEAD)
                pe.wait_ge(consts_made, 4)
                pe.wait_ge(range_found, 1)
                nc.tensor.transpose(ps_c[0:LISTED, 0, 0:P], group_lo, ident[:, :])
                nc.tensor.transpose(ps_c[0:LISTED, 0, P:2 * P], group_hi[:, :], ident[:, :]).then_inc(range_turned, 1)
                pe.wait_ge(base_found, 2)
                nc.tensor.matmul(ps_c[:, 1, 0:LISTED + 1], ones[0:LISTED, :], bases[:, :], start=True,
                                 stop=True).then_inc(base_spread, 1)
                pe.wait_ge(base_ready, 1)
                pe.wait_ge(weights_in, 32)

                def pair_products(hot_s, hot_d):
                    for c in range(CHUNK):
                        for j in range(T):
                            col = (j % 5) * WIN
                            last = nc.tensor.matmul(ps_c[:, j // 5, col:col + WIN], hot_s[:, c, j * P:(j + 1) * P],
                                                    hot_d[:, c, :], start=(c == 0 and j % 5 == 0),
                                                    stop=(c == CHUNK - 1), skip_group_check=True)
                    return last

                def turn(rows, ready, t, count):
                    pe.wait_ge(ready, AHEAD + t + 1)
                    pe.wait_ge(turned_out, AHEAD + count)
                    for k in range(KD):
                        last = nc.tensor.transpose(ps_t[:, k // 4, (k % 4) * P:(k % 4 + 1) * P],
                                                   rows[:, k * P:(k + 1) * P], ident[:, :])
                    last.then_inc(turned, 1)

                def project(out, lhs, w, ks):
                    for k in ks:
                        for n in range(2):
                            last = nc.tensor.matmul(out[:, n, 0:HALF], lhs[:, k, :], w[:, k, n * HALF:(n + 1) * HALF],
                                                    start=(k == 0), stop=(k == KD - 1))
                    return last

                with pe.Fori(0, PAIRS) as i:
                    for b in range(2):
                        t = 2 * i + b
                        for slot in range(PER_TILE):
                            g = t * PER_TILE + slot
                            pe.wait_ge(hot_ready, g + 1)
                            pe.wait_ge(pairs_added, AHEAD + g)
                            pair_products(hot_src[slot % 2], hot_dst[slot % 2]).then_inc(pairs_ready, 1)
                            if slot == 0:
                                turn(x0[b], x0_ready, t, 2 * t)
                            if slot == 1:
                                turn(xn[b], xn_ready, t, 2 * t + 1)
                                pe.wait_ge(u_out, AHEAD + t)
                            if slot == 4:
                                pe.wait_ge(turned_out, AHEAD + 2 * t + 2)
                                pe.wait_ge(h_out, AHEAD + t)
                            if 1 <= slot <= 3:
                                last = project(ps_u, x0_t[b], wu, range(2 * slot - 2, 2 * slot))
                                if slot == 3:
                                    last.then_inc(u_ready, 1)
                            if 4 <= slot <= 6:
                                last = project(ps_h, xn_t[b], w1, range(2 * slot - 8, 2 * slot - 6))
                                if slot == 6:
                                    last.then_inc(h_ready, 1)

                wide = pe.value_load(base_i[0:1, LISTED:LISTED + 1], min_val=0, max_val=LISTED)
                with pe.If(wide > 0):
                    with pe.Fori(0, NP // WIN) as w:
                        with pe.Fori(0, GROUPS) as g:
                            pe.wait_ge(gen_hot, w * GROUPS + g + 1)
                            pair_products(hot_src[0], hot_dst[0]).then_inc(gen_pairs, 1)

            @block.vector
            def _(dve):
                dve.nop().then_inc(x0_ready, AHEAD)
                dve.nop().then_inc(xhat_ready, AHEAD)
                dve.nop().then_inc(pairs_added, AHEAD)
                dve.nop().then_inc(u_out, AHEAD)
                step = Count()
                dve.wait_ge(edges_in, 32)
                nc.vector.tensor_copy(dst_f[:, :], dst_i).then_inc(dve_step, 1)
                nc.vector.tensor_copy(src_f[:, :], src_i).then_inc(dve_step, 1)
                dve.wait_ge(dve_step, step.up(2))
                grouped = dst_f[:, :].rearrange("p (g c) -> p g c", c=CHUNK)
                nc.vector.tensor_reduce(group_lo, grouped, AX_X, ALU.min)
                nc.vector.tensor_reduce(group_hi[:, :], grouped, AX_X, ALU.max).then_inc(range_found, 1)
                dve.wait_ge(range_turned, 1)
                nc.vector.tensor_reduce(lo[:, :], ps_c[0:LISTED, 0, 0:P], AX_X, ALU.min).then_inc(dve_step, 1)
                nc.vector.tensor_reduce(hi[:, :], ps_c[0:LISTED, 0, P:2 * P], AX_X, ALU.max).then_inc(dve_step, 1)
                dve.wait_ge(dve_step, step.up(2))
                nc.vector.tensor_scalar(lo[:, :], lo[:, :], float(NP - WIN), None, ALU.min).then_inc(dve_step, 1)
                dve.wait_ge(dve_step, step.up())
                nc.vector.tensor_tensor(hi[:, :], hi[:, :], lo[:, :], ALU.subtract).then_inc(dve_step, 1)
                nc.vector.tensor_scalar(bases[:, 0:LISTED], ident[0:LISTED, 0:LISTED], lo[:, 0:1], None,
                                        ALU.mult).then_inc(base_found, 1)
                dve.wait_ge(dve_step, step.up())
                nc.vector.tensor_scalar(bases[:, LISTED:LISTED + 1], hi[:, :], float(WIN), None,
                                        ALU.is_ge).then_inc(base_found, 1)
                dve.wait_ge(base_spread, 1)
                nc.vector.tensor_copy(base_i[:, :], ps_c[0:1, 1, 0:LISTED + 1]).then_inc(dve_step, 1)
                for c in range(CHUNK):
                    nc.vector.tensor_tensor(dst_w[:, :].rearrange("p (g c) -> p g c", c=CHUNK)[:, :, c],
                                            dst_f[:, :].rearrange("p (g c) -> p g c", c=CHUNK)[:, :, c],
                                            ps_c[:, 1, 0:LISTED], ALU.subtract).then_inc(dve_step, 1)

                def self_loops():
                    for j in range(T):
                        last = nc.vector.tensor_copy(counts[:, j, j * P:(j + 1) * P], ident[:, :])
                    return last

                dve.wait_ge(consts_made, 4)
                dve.wait_ge(counts_clear, 2)
                self_loops().then_inc(base_ready, 1)
                dve.wait_ge(dve_step, step.up(1 + CHUNK))
                dve.wait_ge(base_ready, 1)

                def one_hots(hot_s, hot_d, g, dsts, base):
                    for c in range(CHUNK):
                        nc.vector.tensor_scalar(hot_s[:, c, :], node_ids[:, :], src_f[:, ds(g * CHUNK + c, 1)],
                                                None, ALU.is_equal)
                        last = nc.vector.tensor_scalar(hot_d[:, c, :], node_ids[:, ds(base, WIN)],
                                                       dsts[:, ds(g * CHUNK + c, 1)], None, ALU.is_equal)
                    return last

                def add_pairs(base):
                    window = counts[:, :, ds(base, WIN)]
                    for n in range(2):
                        last = nc.vector.tensor_tensor(window[:, 5 * n:5 * n + 5, :],
                                                       ps_c[:, n, 0:5 * WIN].rearrange("p (j w) -> p j w", w=WIN),
                                                       window[:, 5 * n:5 * n + 5, :], ALU.add)
                    return last

                def halves(x):
                    for n in range(2):
                        last = nc.vector.bn_stats(stats[:, n, :], x[:, n * HALF:(n + 1) * HALF])
                    return last.then_inc(dve_step, 1)

                def aggregate():
                    return nc.vector.bn_aggr(mean_var[:, :], stats[:, :, :]).then_inc(var_ready, 1)

                def invert(count):
                    dve.wait_ge(std_ready, count)
                    return nc.vector.reciprocal(rstd[:, :], std[:, :]).then_inc(dve_step, 1)

                def normalise(x, out):
                    return nc.vector.tensor_scalar(out[:, :], x[:, :], mean_var[:, 0:1], rstd[:, 0:1],
                                                   ALU.subtract, ALU.mult)

                dve.wait_ge(x_loaded[0], 16)
                for x, out, count, ready in ((x_in[0], x0[0], 1, x0_ready), (x0[0], xn[0], 2, xhat_ready)):
                    halves(x)
                    dve.wait_ge(dve_step, step.up())
                    aggregate()
                    invert(count)
                    dve.wait_ge(dve_step, step.up())
                    normalise(x, out).then_inc(ready, 1)
                    dve.wait_ge(ready, AHEAD + 1)
                one_hots(hot_src[0], hot_dst[0], 0, dst_w, 0).then_inc(hot_ready, 1)

                with dve.Fori(0, PAIRS) as i, step.turns(i, 2 * 4, PAIRS):
                    for b in range(2):
                        t = 2 * i + b
                        other = 1 - b
                        for slot in range(PER_TILE):
                            g = t * PER_TILE + slot
                            if slot == 0:
                                dve.wait_ge(x_loaded[other], (i + 1 + b) * 16)
                                dve.wait_ge(turned, AHEAD + 2 * t)
                                halves(x_in[other])
                            if slot == 2:
                                dve.wait_ge(x0_ready, AHEAD + t + 2)
                                halves(x0[other])
                            if slot in (0, 2):
                                dve.wait_ge(dve_step, step.up())
                            one_hots(hot_src[(slot + 1) % 2], hot_dst[(slot + 1) % 2], g + 1, dst_w, 0)\
                                .then_inc(hot_ready, 1)
                            if slot in (0, 2):
                                aggregate()
                            if slot in (1, 3):
                                invert(2 * t + 2 + (slot + 1) // 2)
                            base = dve.value_load(base_i[0:1, ds(g, 1)], min_val=0, max_val=NP - WIN)
                            dve.wait_ge(pairs_ready, g + 1)
                            dve.wait_ge(pairs_added, AHEAD + g)
                            add_pairs(base).then_inc(pairs_added, 1)
                            if slot == 1:
                                dve.wait_ge(dve_step, step.up())
                                normalise(x_in[other], x0[other]).then_inc(x0_ready, 1)
                            if slot == 3:
                                dve.wait_ge(dve_step, step.up())
                                normalise(x0[other], xn[other]).then_inc(xhat_ready, 1)
                            if slot == 4:
                                dve.wait_ge(u_ready, t + 1)
                                dve.wait_ge(acc_seeded, AHEAD + t + 1)
                                nc.vector.tensor_tensor(acc[:, t, :].rearrange("p (n c) -> p n c", n=2),
                                                        ps_u[:, :, 0:HALF],
                                                        acc[:, t, :].rearrange("p (n c) -> p n c", n=2),
                                                        ALU.add).then_inc(u_out, 1)
                            if slot == 7:
                                dve.wait_ge(h_out, AHEAD + t + 1)
                                for h in range(H1):
                                    for which, weights, scores in ((0, a_src, s_src), (1, a_dst, s_dst)):
                                        last = nc.vector.scalar_tensor_tensor(
                                            out=dot[:, 2 * (h % 2) + which, :],
                                            in0=h1[:, t, h * (C1 + 2):h * (C1 + 2) + C1], scalar=1.0,
                                            in1=weights[:, h * C1:(h + 1) * C1], op0=ALU.mult, op1=ALU.mult,
                                            accum_out=scores[:, ds(t + h * T, 1)])
                                    if h % 2 == 1:
                                        last.then_inc(dots_done, 1)
                                        dve.wait_ge(dots_done, 2 * t + h // 2 + 1)

                dve.wait_ge(pairs_added, AHEAD + GROUPS)
                wide = dve.value_load(base_i[0:1, LISTED:LISTED + 1], min_val=0, max_val=LISTED)
                with dve.If(wide > 0):
                    nc.vector.memset(counts[:, :, :], 0).then_inc(gen_added, 1)
                    dve.wait_ge(gen_added, 1)
                    self_loops().then_inc(gen_added, 1)
                    dve.wait_ge(gen_added, 2)
                    with dve.Fori(0, NP // WIN) as w:
                        with dve.Fori(0, GROUPS) as g:
                            one_hots(hot_src[0], hot_dst[0], g, dst_f, w * WIN).then_inc(gen_hot, 1)
                            dve.wait_ge(gen_pairs, w * GROUPS + g + 1)
                            add_pairs(w * WIN).then_inc(gen_added, 1)
                            dve.wait_ge(gen_added, w * GROUPS + g + 3)

        nc.clear_and_free_semaphores(semaphores)
        nc.all_engine_barrier()


def attention(nc, a, keep, layer, heads, width):
    ctx = ExitStack()
    with ctx:
        def sb(name, shape, dt=F32):
            return ctx.enter_context(nc.sbuf_tensor(f"{name}_{layer}", shape, dt))

        def sem(name):
            return ctx.enter_context(nc.semaphore(f"{name}_{layer}"))

        counts, no_edge, ident = keep["counts"], keep["no_edge"], keep["ident"]
        h_rows, s_src, s_dst = keep[f"h{layer}"], keep[f"s_src{layer}"], keep[f"s_dst{layer}"]
        W = width + 2
        PER_BANK = 512 // W if 512 // W < T // 2 else T // 2
        BANKS = T // PER_BANK
        HT = heads * T
        RING = 5

        best = [sb(f"best{b}", [P, NP]) for b in range(2)]
        top = sb("top", [P, HT])
        peak = sb("peak", [P, HT])
        src_low = sb("src_low", [P, HT])
        shifts = sb("shifts", [P, heads, 2, T])
        shifts_t = sb("shifts_t", [2 * HT, P])
        shift_rows = [sb(f"shift_rows{b}", [P, 2, NP]) for b in range(2)]
        weights = [sb(f"weights{b}", [P, NP]) for b in range(RING)]
        rden = sb("rden", [P, T])
        bias_row = sb("bias_row", [P, heads * width])
        shift_dram = nc.dram_tensor(f"shift_dram_{layer}", (2 * HT, P), F32).ap()

        ps_o = ctx.enter_context(nc.psum_tensor(f"ps_o_{layer}", [P, 5, 512], F32))
        ps_m = ctx.enter_context(nc.psum_tensor(f"ps_m_{layer}", [P, 3, 512], F32))

        bias_in = sem("bias_in")
        masked = sem("masked")
        best_step = sem("best_step")
        best_ready = sem("best_ready")
        best_turned = sem("best_turned")
        top_ready = sem("top_ready")
        small_step = sem("small_step")
        shifts_ready = sem("shifts_ready")
        shifts_turned = sem("shifts_turned")
        shifts_out = sem("shifts_out")
        shifts_stored = sem("shifts_stored")
        rows_in = [sem(f"shift_rows_in{b}") for b in range(2)]
        low_ready = sem("low_ready")
        bound_ready = sem("bound_ready")
        exp_ready = sem("exp_ready")
        weights_ready = sem("weights_ready")
        weights_used = sem("weights_used")
        inverse_ready = sem("inverse_ready")
        head_out = sem("head_out")

        with nc.Block() as block:

            @block.sync
            def _(sp):
                sp.dma_start(bias_row[:, :], a[f"b{layer}"].partition_broadcast(P)).then_inc(bias_in, 16)
                sp.wait_ge(shifts_out, 1)
                sp.dma_start(shift_dram, shifts_t[:, :]).then_inc(shifts_stored, 16)
                sp.wait_ge(shifts_stored, 16)
                by_head = shift_dram.rearrange("(h r) p -> h (r p)", h=heads)
                for h in range(heads):
                    if h >= 2:
                        sp.wait_ge(bound_ready, (h - 1) * T)
                    sp.dma_start(shift_rows[h % 2][:, :, :].rearrange("p s n -> p (s n)"),
                                 by_head[h:h + 1, :].broadcast_to([P, 2 * NP])).then_inc(rows_in[h % 2], 16)

            @block.scalar
            def _(act):
                act.wait_ge(shifts_ready, 1)
                act.wait_ge(shifts_turned, 1)
                nc.scalar.copy(shifts_t[:, :], ps_m[0:2 * HT, 0, 0:P]).then_inc(shifts_out, 1)

                def low_part(b, h, s):
                    nc.scalar.activation(weights[s % RING][:, :], shift_rows[b][:, 1, :], ACT.Identity,
                                         bias=src_low[:, ds(h * T + s, 1)], scale=1.0).then_inc(low_ready, 1)

                with act.Fori(0, heads // 2) as i:
                    for b in range(2):
                        h = 2 * i + b
                        act.wait_ge(rows_in[b], (i + 1) * 16)
                        for s in range(T + 2):
                            if s < T:
                                if s >= RING:
                                    act.wait_ge(weights_used, AHEAD + h * T + s - RING + 1)
                                elif s == 0:
                                    act.wait_ge(weights_used, AHEAD + h * T)
                                low_part(b, h, s)
                            if s >= 2:
                                act.wait_ge(bound_ready, h * T + s - 1)
                                w = weights[(s - 2) % RING]
                                nc.scalar.activation(w[:, :], w[:, :], ACT.Exp).then_inc(exp_ready, 1)

            @block.tensor
            def _(pe):
                pe.nop().then_inc(weights_used, AHEAD)
                pe.nop().then_inc(best_turned, AHEAD)
                with pe.Fori(0, heads // 2) as i:
                    for b in range(2):
                        h = 2 * i + b
                        pe.wait_ge(best_ready, h + 1)
                        pe.wait_ge(top_ready, AHEAD + h)
                        for j in range(T):
                            last = nc.tensor.transpose(ps_m[:, j // 4, (j % 4) * P:(j % 4 + 1) * P],
                                                       best[b][:, j * P:(j + 1) * P], ident[:, :])
                        last.then_inc(best_turned, 1)
                pe.wait_ge(shifts_ready, 1)
                nc.tensor.transpose(ps_m[0:2 * HT, 0, 0:P], shifts[:, :, :, :].rearrange("p h s t -> p (h s t)"),
                                    ident[:, :]).then_inc(shifts_turned, 1)
                with pe.Fori(0, heads) as h:
                    pe.wait_ge(head_out, AHEAD + h)
                    for s in range(T):
                        pe.wait_ge(weights_ready, h * T + s + 1)
                        for j in range(T):
                            col = (j % PER_BANK) * W
                            last = nc.tensor.matmul(ps_o[:, j // PER_BANK, col:col + W],
                                                    weights[s % RING][:, j * P:(j + 1) * P],
                                                    h_rows[:, s, ds(h * W, W)],
                                                    start=(s == 0 and j % PER_BANK == 0), stop=(s == T - 1),
                                                    skip_group_check=True)
                        last.then_inc(weights_used, 1)

            @block.vector
            def _(dve):
                dve.nop().then_inc(top_ready, AHEAD)
                dve.nop().then_inc(head_out, AHEAD)
                if layer == 1:
                    nc.vector.tensor_scalar(no_edge[:, :, :], counts[:, :, :], 0.0, NEG, ALU.is_equal,
                                            ALU.mult).then_inc(masked, 1)
                    dve.wait_ge(masked, 1)
                chain = Count()
                with dve.Fori(0, heads // 2) as i, chain.turns(i, 2 * (T - 1), heads // 2):
                    for b in range(2):
                        h = 2 * i + b
                        dve.wait_ge(best_turned, AHEAD + 2 * i)
                        nc.vector.tensor_scalar(best[b][:, :], no_edge[:, 0, :], s_src[:, ds(h * T, 1)], None,
                                                ALU.add).then_inc(best_step, 1)
                        for s in range(1, T):
                            dve.wait_ge(best_step, chain.up())
                            last = nc.vector.scalar_tensor_tensor(
                                out=best[b][:, :], in0=no_edge[:, s, :], scalar=s_src[:, ds(h * T + s, 1)],
                                in1=best[b][:, :], op0=ALU.add, op1=ALU.max)
                            last.then_inc(best_step if s < T - 1 else best_ready, 1)
                        dve.wait_ge(best_turned, AHEAD + h + 1)
                        nc.vector.tensor_reduce(top[:, ds(h * T, 8)], ps_m[:, 0:2, :].rearrange(
                            "p b (j n) -> p (b j) n", n=P), AX_X, ALU.max)
                        nc.vector.tensor_reduce(top[:, ds(h * T + 8, T - 8)], ps_m[:, 2, 0:(T - 8) * P].rearrange(
                            "p (j n) -> p j n", n=P), AX_X, ALU.max).then_inc(top_ready, 1)
                dve.wait_ge(top_ready, AHEAD + heads)
                small = Count()
                nc.vector.tensor_scalar(src_low[:, :], s_src[:, :], SLOPE, None, ALU.mult)
                nc.vector.tensor_tensor(top[:, :], top[:, :], s_dst[:, :], ALU.add).then_inc(small_step, 1)
                dve.wait_ge(small_step, small.up())
                nc.vector.scalar_tensor_tensor(out=peak[:, :], in0=top[:, :], scalar=SLOPE, in1=top[:, :],
                                               op0=ALU.mult, op1=ALU.max).then_inc(small_step, 1)
                dve.wait_ge(small_step, small.up())
                by_head = [x.rearrange("p (h t) -> p h t", t=T) for x in (s_dst[:, :], peak[:, :])]
                nc.vector.tensor_tensor(shifts[:, :, 0, :], by_head[0], by_head[1], ALU.subtract)\
                    .then_inc(small_step, 1)
                nc.vector.scalar_tensor_tensor(out=shifts[:, :, 1, :], in0=by_head[0], scalar=SLOPE, in1=by_head[1],
                                               op0=ALU.mult, op1=ALU.subtract).then_inc(shifts_ready, 1)
                dve.wait_ge(small_step, small.up())
                dve.wait_ge(bias_in, 16)

                def upper(b, h, s):
                    dve.wait_ge(low_ready, h * T + s + 1)
                    w = weights[s % RING]
                    return nc.vector.scalar_tensor_tensor(out=w[:, :], in0=shift_rows[b][:, 0, :],
                                                          scalar=s_src[:, ds(h * T + s, 1)], in1=w[:, :],
                                                          op0=ALU.add, op1=ALU.max)

                with dve.Fori(0, heads // 2) as i:
                    for b in range(2):
                        h = 2 * i + b
                        dve.wait_ge(rows_in[b], (i + 1) * 16)
                        for s in range(T + 2):
                            if s < T:
                                upper(b, h, s).then_inc(bound_ready, 1)
                                if s == T - 1:
                                    dve.wait_ge(bound_ready, h * T + T)
                            if s >= 2:
                                dve.wait_ge(exp_ready, h * T + s - 1)
                                w = weights[(s - 2) % RING]
                                last = nc.vector.scalar_tensor_tensor(
                                    out=w[:, :], in0=w[:, :], scalar=1.0, in1=counts[:, s - 2, :],
                                    op0=ALU.min, op1=ALU.mult).then_inc(weights_ready, 1)
                        dve.wait_ge(weights_used, AHEAD + h * T + T)
                        sums = ps_o[:, 0:BANKS, 0:PER_BANK * W].rearrange("p b (j w) -> p b j w", w=W)
                        nc.vector.reciprocal(rden[:, :].rearrange("p (b j) -> p b j", b=BANKS),
                                             sums[:, :, :, width]).then_inc(inverse_ready, 1)
                        dve.wait_ge(inverse_ready, h + 1)
                        for j in range(T):
                            last = nc.vector.scalar_tensor_tensor(
                                out=h_rows[:, j, ds(h * width, width)],
                                in0=ps_o[:, j // PER_BANK, (j % PER_BANK) * W:(j % PER_BANK) * W + width],
                                scalar=rden[:, j:j + 1], in1=bias_row[:, ds(h * width, width)],
                                op0=ALU.mult, op1=ALU.add)
                        last.then_inc(head_out, 1)

            @block.gpsimd
            def _(pool):
                if layer == 1:
                    nc.gpsimd.memset(keep["h2"][:, :, :], 1.0)


def second_projection(nc, a, keep):
    ctx = ExitStack()
    with ctx:
        def sb(name, shape, dt=F32):
            return ctx.enter_context(nc.sbuf_tensor(name, shape, dt))

        def sem(name):
            return ctx.enter_context(nc.semaphore(name))

        h1, h2, s_src, s_dst, ident = keep["h1"], keep["h2"], keep["s_src2"], keep["s_dst2"], keep["ident"]
        W, N2 = C2 + 2, H2 * C2
        w2 = sb("w2", [P, KD, N2])
        a_src = sb("a_src_b", [P, N2])
        a_dst = sb("a_dst_b", [P, N2])
        out1_t = [sb(f"out1_t{b}", [P, KD, P]) for b in range(2)]
        dot = sb("dot_b", [P, 2 * H2, C2])
        ps_t = [ctx.enter_context(nc.psum_tensor(f"ps_r{b}", [P, 2, 512], F32)) for b in range(2)]
        ps_p = [ctx.enter_context(nc.psum_tensor(f"ps_p{b}", [P, 512], F32)) for b in range(2)]
        loaded = sem("loaded")
        turned = sem("turned_b")
        turned_out = sem("turned_out_b")
        ready = sem("ready_b")
        copied = sem("copied_b")
        dots_done = sem("dots_done_b")

        with nc.Block() as block:

            @block.sync
            def _(sp):
                sp.dma_start(w2[:, :, :], a["W2"].rearrange("(k p) n -> p k n", p=P)).then_inc(loaded, 16)
                sp.dma_start(a_src[:, :], a["a_src2"].partition_broadcast(P)).then_inc(loaded, 16)
                sp.dma_start(a_dst[:, :], a["a_dst2"].partition_broadcast(P)).then_inc(loaded, 16)

            @block.tensor
            def _(pe):
                pe.nop().then_inc(ready, AHEAD)
                pe.wait_ge(loaded, 48)

                def turn(t):
                    for k in range(KD):
                        last = nc.tensor.transpose(ps_t[t % 2][:, k // 4, (k % 4) * P:(k % 4 + 1) * P],
                                                   h1[:, t, k * P:(k + 1) * P], ident[:, :])
                    last.then_inc(turned, 1)

                for t in range(T + 1):
                    if t < T:
                        if t >= 2:
                            pe.wait_ge(turned_out, t - 1)
                        turn(t)
                    if t >= 1:
                        pe.wait_ge(turned_out, t)
                        if t >= 3:
                            pe.wait_ge(copied, t - 2)
                        for k in range(KD):
                            last = nc.tensor.matmul(ps_p[(t - 1) % 2][:, 0:N2], out1_t[(t - 1) % 2][:, k, :],
                                                    w2[:, k, :], start=(k == 0), stop=(k == KD - 1))
                        last.then_inc(ready, 1)

            @block.scalar
            def _(act):
                with act.Fori(0, T // 2) as i:
                    for b in range(2):
                        t = 2 * i + b
                        act.wait_ge(turned, t + 1)
                        act.wait_ge(ready, AHEAD + 2 * i)
                        nc.scalar.copy(out1_t[b][:, 0:4, :], ps_t[b][:, 0, 0:512])
                        nc.scalar.copy(out1_t[b][:, 4:KD, :], ps_t[b][:, 1, 0:256]).then_inc(turned_out, 1)

            @block.vector
            def _(dve):
                dve.wait_ge(loaded, 48)
                with dve.Fori(0, T // 2) as i:
                    for b in range(2):
                        t = 2 * i + b
                        dve.wait_ge(ready, AHEAD + t + 1)
                        nc.vector.tensor_copy(h2[:, t, :].rearrange("p (h c) -> p h c", h=H2)[:, :, 0:C2],
                                              ps_p[b][:, 0:N2].rearrange("p (h c) -> p h c", h=H2))\
                            .then_inc(copied, 1)
                        dve.wait_ge(copied, t + 1)
                        for h in range(H2):
                            for which, weights, scores in ((0, a_src, s_src), (1, a_dst, s_dst)):
                                last = nc.vector.scalar_tensor_tensor(
                                    out=dot[:, 2 * h + which, :], in0=h2[:, t, h * W:h * W + C2], scalar=1.0,
                                    in1=weights[:, h * C2:(h + 1) * C2], op0=ALU.mult, op1=ALU.mult,
                                    accum_out=scores[:, ds(t + h * T, 1)])
                        last.then_inc(dots_done, 1)
                        dve.wait_ge(dots_done, t + 1)


def network(nc, a, keep, out):
    ctx = ExitStack()
    with ctx:
        def sb(name, shape, dt=F32):
            return ctx.enter_context(nc.sbuf_tensor(name, shape, dt))

        def sem(name):
            return ctx.enter_context(nc.semaphore(name))

        acc, h2, ident, ones, eps = keep["acc"], keep["h2"], keep["ident"], keep["ones"], keep["eps"]
        place_i, mix, tile_expert, ends_i = (keep[n] for n in ("place_i", "mix", "tile_expert", "ends_i"))
        xh_dram, x1_dram, base_dram = keep["xh_dram"], keep["x1_dram"], keep["base_dram"]
        list_dram, y_dram = keep["list_dram"], keep["y_dram"]
        N2 = H2 * C2
        REST = N2 - P
        TE = T * EXPERTS

        w_hi = sb("w_hi", [P, 2, PIECES * D], F32R)
        w_lo = sb("w_lo", [P, 2, PIECES * D], F32R)
        raw = [sb(f"raw{q}", [P, D]) for q in range(RAWS)]
        bg = sb("bg", [P, 2 * I])
        bu = sb("bu", [P, 2 * I])
        bd = sb("bd", [P, 2 * D])
        x_row = [sb(f"x_row{b}", [P, D]) for b in range(2)]
        x_hi = [sb(f"x_hi{b}", [P, KD, P], F32R) for b in range(2)]
        x_lo = [sb(f"x_lo{b}", [P, KD, P], F32R) for b in range(2)]
        widened = sb("widened", [P, 2, I])
        gate, up = widened[:, 0, :], widened[:, 1, :]
        inner = [sb(f"inner{b}", [P, I]) for b in range(2)]
        i_hi = sb("i_hi", [P, KI, P], F32R)
        i_lo = sb("i_lo", [P, KI, P], F32R)
        y = [sb(f"y{b}", [P, D]) for b in range(2)]
        wu_a, wu_b = x_row[0][:, :], x_row[1][0:REST, :]
        out2_t = [inner[b][:, 0:2 * P].rearrange("p (k n) -> p k n", k=2) for b in range(2)]
        xh_t = [sb("xh_t", [P, KD, P])[:, :, :],
                widened[:, :, :].rearrange("p w n -> p (w n)").rearrange("p (k n) -> p k n", k=KD)]
        router = sb("router", [P, KD, EXPERTS])
        rb_row = sb("rb_row", [P, EXPERTS])
        cb_row = sb("cb_row", [P, EXPERTS])
        logits = sb("logits", [P, T, EXPERTS])
        before = sb("before", [P, EXPERTS, EXPERTS], BF16)
        before4 = sb("before4", [P, 4, 4], BF16)
        real = sb("real", [P, T, EXPERTS])
        thresholds = sb("thresholds", [P, T])
        tile_ids = sb("tile_ids", [P, TILES + 1])
        earlier_rows = sb("earlier_rows", [P, P])
        dump = sb("dump", [P, CHOSEN, T])

        mean_var = sb("mean_var_c", [P, 2])
        stats = sb("stats_c", [P, 2, 6])
        std_c = sb("std_c", [P, 1])
        rstd = sb("rstd_c", [P, 1])
        acc_flat, taken = acc[:, :, :].rearrange("p t d -> p (t d)"), [0]

        def room(shape, dt=F32):
            size = 1
            for n in shape[1:]:
                size *= n
            words = size // 2 if dt == BF16 else size
            flat = acc_flat[:, taken[0]:taken[0] + words]
            taken[0] += words
            assert taken[0] <= T * D
            dims = dict(zip("abc", shape[1:]))
            return (flat if dt == F32 else flat.bitcast(dt)).rearrange(
                f"p ({' '.join(dims)}) -> p {' '.join(dims)}", **dims)

        scores = room([P, T, EXPERTS])
        biased = room([P, T, EXPERTS])
        pair_hi = room([P, T, 4, 2])
        pair_lo = room([P, T, 4, 2])
        group_score = room([P, T, 4])
        group_next = room([P, T, 4])
        group_kept = room([P, T, 4])
        ahead = room([P, T, EXPERTS, EXPERTS], BF16)
        tied = room([P, T, EXPERTS, EXPERTS], BF16)
        rank = room([P, T, EXPERTS])
        chosen = room([P, T, EXPERTS])
        nth = room([P, T, EXPERTS])
        mask = room([P, T, EXPERTS])
        picked = room([P, T, EXPERTS])
        place = room([P, T, EXPERTS])
        tallies = room([P, 2, T, EXPERTS])
        total = room([P, T])
        earlier = room([P, T + 1, EXPERTS])
        filled = room([P, EXPERTS, T])
        n_tiles = room([P, EXPERTS])
        starts = room([P, EXPERTS])
        ends = room([P, EXPERTS])
        passed = room([P, TILES + 1, EXPERTS], BF16)
        tile_f = room([P, TILES + 1])
        place_k = room([P, CHOSEN, T])
        list_k = room([P, CHOSEN, T])
        list_i = room([P, CHOSEN, T], I32)
        spread = [room([P, D]) for b in range(2)]

        banks = ctx.enter_context(nc.psum_tensor("banks", [P, 8, 512], F32))
        ps_a = [banks[:, b, :] for b in (0, 1)]
        ps_l, ps_b, ps_w = banks[:, 2, :], banks[:, 4:6, :], banks[:, 6:8, :]
        ps_x, ps_i = banks[:, 0, :], banks[:, 1, :]
        ps_g = [banks[:, b, :] for b in (2, 3)]
        ps_u = [banks[:, b, :] for b in (4, 5)]
        ps_y = banks[:, 6:8, :]
        gathered = [raw[q][:, :] for q in range(RAWS)]
        late = gathered + [y[b][:, :] for b in range(2)]
        EARLY = 2

        ps_plan = banks[:, 0, 0:2 * TE]

        loaded = sem("loaded_c")
        masks_made = sem("masks_made")
        pool_step = sem("pool_step_c")
        o_turned = sem("o_turned")
        o_turned_out = sem("o_turned_out")
        lower_ready = sem("lower_ready")
        x1_ready = sem("x1_ready")
        dve_step = sem("dve_step_c")
        var_ready = sem("var_ready_c")
        std_ready = sem("std_ready_c")
        xh_ready = sem("xh_ready")
        xh_stored = [sem(f"xh_stored{b}") for b in range(2)]
        x1_stored = sem("x1_stored")
        xh_turned = sem("xh_turned")
        xh_t_out = sem("xh_t_out")
        logits_ready = sem("logits_ready")
        logits_out = sem("logits_out")
        exp_ready = sem("exp_ready_c")
        chosen_ready = sem("chosen_ready")
        counted = sem("counted")
        counts_taken = sem("counts_taken")
        list_ready = sem("list_ready")
        plan_ready = sem("plan_ready")
        spread_in = [sem(f"spread_in{b}") for b in range(2)]
        spread_done = [sem(f"spread_done{b}") for b in range(2)]
        raw_in = [sem(f"raw_in{q}") for q in range(RAWS)]
        piece_cut = sem("piece_cut")
        hi_cut = sem("hi_cut")
        bias_in = [sem(f"bias_in{b}") for b in range(2)]
        bd_in = [sem(f"bd_in{b}") for b in range(2)]
        x_in = [sem(f"x_in_sem{b}") for b in range(2)]
        base_in = [sem(f"base_in{b}") for b in range(2)]
        turned = sem("turned_e")
        x_hi_ready = sem("x_hi_ready")
        x_lo_ready = sem("x_lo_ready")
        gate_ready = sem("gate_ready")
        up_ready = sem("up_ready")
        gate_biased = sem("gate_biased")
        up_biased = sem("up_biased")
        silu_ready = sem("silu_ready")
        inner_ready = sem("inner_ready")
        inner_turned = sem("inner_turned")
        i_hi_ready = sem("i_hi_ready")
        i_lo_ready = sem("i_lo_ready")
        down_ready = sem("down_ready")
        y_ready = sem("y_ready")
        y_stored = [sem(f"y_stored{b}") for b in range(2)]
        sums_seeded = sem("sums_seeded")
        stage_open = sem("stage_open")
        gathered_in = [sem(f"gathered_in{q}") for q in range(RAWS)]
        late_in = [sem(f"late_in{q}") for q in range(RAWS + 2)]
        weighted = sem("weighted")
        added = sem("added")
        summed = sem("summed")
        out_stored = sem("out_stored")

        R0, V0, N0 = T, SHARED * T, T
        WIDENED, COMPLETE = SHARED * PIECES + KD, (SHARED + 1) * PIECES

        with nc.Block() as block:

            @block.sync
            def _(sp):
                sp.dma_start(wu_a, a["Wu"][D:D + P, :]).then_inc(loaded, 16)
                sp.dma_start(wu_b, a["Wu"][D + P:D + N2, :]).then_inc(loaded, 16)
                sp.dma_start(router[:, :, :], a["router_w"].rearrange("(k p) e -> p k e", p=P))\
                    .then_inc(loaded, 16)
                sp.dma_start(rb_row[:, :], a["router_b"].partition_broadcast(P)).then_inc(loaded, 16)
                sp.dma_start(cb_row[:, :], a["corr_bias"].partition_broadcast(P)).then_inc(loaded, 16)

                def inner_biases(b, gate_b, up_b):
                    for dst, src in ((bg, gate_b), (bu, up_b)):
                        sp.dma_start(dst[:, b * I:(b + 1) * I], src.partition_broadcast(P)).then_inc(bias_in[b], 16)

                def down_bias(b, down_b):
                    sp.dma_start(bd[:, b * D:(b + 1) * D], down_b.partition_broadcast(P)).then_inc(bd_in[b], 16)

                def pieces(which, first, gate_w, up_w, down_w):
                    for q in which:
                        r = raw[q % RAWS]
                        if not isinstance(first, int) or first + q >= RAWS:
                            sp.wait_ge(piece_cut, first + q - RAWS + 1)
                        if q < KD:
                            for n, w in ((0, gate_w), (1, up_w)):
                                sp.dma_start(r[:, n * I:(n + 1) * I], w[q * P:(q + 1) * P, :])\
                                    .then_inc(raw_in[q % RAWS], 16)
                        else:
                            sp.dma_start(r[:, :], down_w[(q - KD) * P:(q - KD + 1) * P, :])\
                                .then_inc(raw_in[q % RAWS], 16)

                for b in range(SHARED):
                    cols = slice(b * I, (b + 1) * I)
                    inner_biases(b, a["sbg"][cols], a["sbu"][cols])
                    down_bias(b, a["sbd"])
                    pieces(range(PIECES), b * PIECES, a["sWg"][:, cols], a["sWu"][:, cols], a["sWd"][cols, :])
                for t in range(T):
                    sp.wait_ge(x1_ready, t + 1)
                    sp.dma_start(x1_dram[t * P:(t + 1) * P, :], acc[:, t, :]).then_inc(x1_stored, 16)
                    sp.wait_ge(xh_ready, t + 1)
                    sp.dma_start(xh_dram[t * P:(t + 1) * P, :], y[t % 2][:, :]).then_inc(xh_stored[t % 2], 16)
                def load_expert(e, b, parts, passes, results):
                    gate_w, up_w, down_w, gate_b, up_b, down_b = parts
                    first = (e + SHARED) * PIECES
                    pieces(range(RAWS), first, gate_w, up_w, down_w)
                    sp.wait_ge(inner_ready, AHEAD + passes)
                    inner_biases(b, gate_b, up_b)
                    pieces(range(RAWS, PIECES), first, gate_w, up_w, down_w)
                    sp.wait_ge(y_ready, AHEAD + results)
                    down_bias(b, down_b)

                names = ("gWg", "gWu", "gWd", "gbg", "gbu", "gbd")
                for b in range(2):
                    load_expert(b, b, [a[n][b] for n in names], V0 - 1 + b, N0)
                sp.wait_ge(list_ready, 1)
                for b in range(2):
                    sp.wait_ge(spread_done[b], 16 * CHOSEN * (T // 2))
                    sp.wait_ge(y_stored[b], 16 * (AHEAD + T // 2))
                sp.dma_start(acc[:, :, :], base_dram.rearrange("(t p) d -> p t d", p=P)).then_inc(sums_seeded, 16)
                with sp.Fori(1, EXPERTS // 2) as i:
                    for b in range(2):
                        e = 2 * i + b
                        end = sp.value_load(ends_i[0:1, ds(e - 2, 1)], min_val=0, max_val=TILES)
                        load_expert(e, b, [a[n][ds(e, 1)].rearrange("o k n -> (o k) n") for n in names[0:3]]
                                    + [a[n][ds(e, 1)].rearrange("o n -> (o n)") for n in names[3:]],
                                    end + V0, end + N0)

                for k in range(EARLY + 1):
                    at = EXPERTS - CHOSEN + k
                    end = sp.value_load(ends_i[0:1, at:at + 1], min_val=0, max_val=TILES)
                    for b in range(2):
                        sp.wait_ge(y_stored[b], (end + end % 2) * 8 + 16 * (AHEAD + T // 2))
                    sp.nop().then_inc(stage_open, 1)
                for t in range(T):
                    sp.wait_ge(summed, (CHOSEN - EARLY - 1) * T + t + 1)
                    sp.dma_start(out[t * P:(t + 1) * P, :], acc[:, t, :]).then_inc(out_stored, 16)
                sp.wait_ge(out_stored, 16 * T)

            @block.gpsimd
            def _(pool):
                nc.gpsimd.memset(before[:, :, :], 1.0).then_inc(pool_step, 1)
                nc.gpsimd.memset(before4[:, :, :], 1.0).then_inc(pool_step, 1)
                nc.gpsimd.memset(real[:, :, :], 1.0).then_inc(pool_step, 1)
                nc.gpsimd.memset(earlier_rows[:, :], 1.0).then_inc(pool_step, 1)
                nc.gpsimd.iota(thresholds[:, :], pattern=[[P, T]], base=0, channel_multiplier=0,
                               allow_small_or_imprecise_dtypes=True).then_inc(masks_made, 1)
                nc.gpsimd.iota(tile_ids[:, :], pattern=[[1, TILES + 1]], base=0, channel_multiplier=0,
                               allow_small_or_imprecise_dtypes=True).then_inc(masks_made, 1)
                nc.gpsimd.iota(dump[:, :, :], pattern=[[P, CHOSEN], [0, T]], base=TILES * P, channel_multiplier=1,
                               allow_small_or_imprecise_dtypes=True).then_inc(masks_made, 1)
                pool.wait_ge(pool_step, 4)
                for tile, n in ((before, EXPERTS), (before4, 4)):
                    nc.gpsimd.affine_select(out=tile[:, :, :], in_=tile[:, :, :], compare_op=ALU.is_gt, fill=0.0,
                                            base=0, pattern=[[1, n], [-1, n]], channel_multiplier=0)\
                        .then_inc(masks_made, 1)
                nc.gpsimd.affine_select(out=real[:, :, :], in_=real[:, :, :], compare_op=ALU.is_ge, fill=0.0,
                                        base=NODES - 1, pattern=[[-P, T], [0, EXPERTS]], channel_multiplier=-1)\
                    .then_inc(masks_made, 1)
                nc.gpsimd.affine_select(out=earlier_rows[:, :], in_=earlier_rows[:, :], compare_op=ALU.is_gt,
                                        fill=0.0, base=0, pattern=[[1, P]], channel_multiplier=-1)\
                    .then_inc(masks_made, 1)

                def scatter(pool, t):
                    pool.wait_ge(spread_in[t % 2], 16 * (t // 2 + 1))
                    for k in range(CHOSEN):
                        pool.indirect_dma_start(out=list_dram, out_offset=bass.IndirectOffsetOnAxis(
                            ap=list_i[:, k, t:t + 1], axis=0), in_=spread[t % 2][:, :], in_offset=None)\
                            .then_inc(spread_done[t % 2], 16)

                def cut_pieces(b, seen, turns, biases, passes=None):
                    pool.wait_ge(raw_in[0], seen[0])
                    for q in range(PIECES):
                        r, hi = raw[q % RAWS][:, :], w_hi[:, b, q * D:(q + 1) * D]
                        if q in (0, KD):
                            if passes is not None:
                                if q == 0:
                                    pool.wait_ge(up_ready, passes)
                                else:
                                    pool.wait_ge(down_ready, AHEAD + passes)
                            nc.gpsimd.tensor_tensor(hi, r, ones[:, 0:1].to_broadcast([P, D]), ALU.mult)\
                                .then_inc(hi_cut, 1)
                        else:
                            nc.gpsimd.tensor_scalar(hi, r, 1.0, 1.0, ALU.mult, ALU.mult).then_inc(hi_cut, 1)
                        pool.wait_ge(hi_cut, turns * PIECES + q + 1)
                        if q == KD - 1:
                            pool.wait_ge(bias_in[b], 32 * biases)
                        if q + 1 < PIECES:
                            pool.wait_ge(raw_in[(q + 1) % RAWS], seen[q + 1])
                        else:
                            pool.wait_ge(bd_in[b], 16 * biases)
                        nc.gpsimd.tensor_tensor(w_lo[:, b, q * D:(q + 1) * D], r, hi.bitcast(F32),
                                                ALU.subtract).then_inc(piece_cut, 1)

                sizes = [2] * KD + [1] * KI
                per_turn = [sum(sizes[q] for q in range(PIECES) if q % RAWS == slot) for slot in range(RAWS)]

                def transfers(turns):
                    return [16 * (turns * per_turn[q % RAWS] + sum(sizes[q % RAWS:q + 1:RAWS])) for q in range(PIECES)]

                for b in range(SHARED):
                    cut_pieces(b, transfers(b), b, 1)
                for t in range(T):
                    b = t % 2
                    if t == 0:
                        for n in range(2):
                            pool.wait_ge(xh_stored[n], 16 * (T // 2))
                        pool.wait_ge(list_ready, 1)
                    if t >= 2:
                        pool.wait_ge(spread_done[b], 16 * CHOSEN * (t // 2))
                    pool.dma_start(spread[b][:, :], xh_dram[t * P:(t + 1) * P, :]).then_inc(spread_in[b], 16)
                    if t >= 1:
                        scatter(pool, t - 1)
                scatter(pool, T - 1)
                for b in range(2):
                    cut_pieces(b, transfers(SHARED + b), SHARED + b, 2, V0 - 1 + b)
                with pool.Fori(1, EXPERTS // 2) as i:
                    for b in range(2):
                        e = 2 * i + b
                        n = e + SHARED
                        end = pool.value_load(ends_i[0:1, ds(e - 2, 1)], min_val=0, max_val=TILES)
                        cut_pieces(b, transfers(n), n, i + 2, end + V0)

                def gather(k, t, into, arrived):
                    pool.indirect_dma_start(out=into, out_offset=None, in_=y_dram,
                                            in_offset=bass.IndirectOffsetOnAxis(ap=place_i[:, k, t:t + 1], axis=0))\
                        .then_inc(arrived, 16)

                pool.wait_ge(sums_seeded, 16)
                pool.wait_ge(piece_cut, (SHARED + EXPERTS) * PIECES)
                for n in range(EARLY * T + RAWS - 1):
                    if n < EARLY * T:
                        if n % T == 0:
                            pool.wait_ge(stage_open, n // T + 1)
                        if n >= RAWS:
                            pool.wait_ge(added, n - RAWS + 1)
                        gather(n // T, n % T, gathered[n % RAWS], gathered_in[n % RAWS])
                    m = n - (RAWS - 1)
                    if m >= 0:
                        k, t, rows = m // T, m % T, gathered[m % RAWS]
                        pool.wait_ge(gathered_in[m % RAWS], 16 * (m // RAWS + 1))
                        nc.gpsimd.tensor_scalar(rows, rows, mix[:, k, t:t + 1], 1.0, ALU.mult, ALU.mult)\
                            .then_inc(weighted, 1)
                        pool.wait_ge(weighted, m + 1)
                        if k > 0:
                            pool.wait_ge(added, m - T + 1)
                        nc.gpsimd.tensor_tensor(acc[:, t, :], rows, acc[:, t, :], ALU.add).then_inc(added, 1)
                pool.wait_ge(added, EARLY * T)
                pool.wait_ge(stage_open, EARLY + 1)
                for n in range((CHOSEN - EARLY) * T):
                    q = n % len(late)
                    if n == RAWS:
                        for b in range(2):
                            pool.wait_ge(y_stored[b], 16 * (AHEAD + T // 2 + PAIRS))
                    if n >= len(late):
                        pool.wait_ge(summed, n - len(late) + 1)
                    gather(EARLY + n // T, n % T, late[q], late_in[q])

            @block.tensor
            def _(pe):
                for s in (turned, down_ready):
                    pe.nop().then_inc(s, AHEAD)
                pe.wait_ge(loaded, 80)

                def turn_out2(t):
                    if t >= 2:
                        pe.wait_ge(o_turned_out, t - 1)
                    nc.tensor.transpose(ps_a[t % 2][:, 0:P], h2[:, t, 0:P], ident[:, :])
                    nc.tensor.transpose(ps_a[t % 2][0:REST, P:2 * P], h2[:, t, P:N2], ident[:, :])\
                        .then_inc(o_turned, 1)

                def lower(t):
                    pe.wait_ge(o_turned_out, t + 1)
                    if t >= 1:
                        pe.wait_ge(x1_ready, t)
                    for k, w, m in ((0, wu_a, P), (1, wu_b, REST)):
                        for n in range(2):
                            last = nc.tensor.matmul(ps_w[:, n, 0:HALF], out2_t[t % 2][0:m, k, :],
                                                    w[:, n * HALF:(n + 1) * HALF], start=(k == 0), stop=(k == 1))
                    last.then_inc(lower_ready, 1)

                def turn_xh(t):
                    pe.wait_ge(xh_ready, t + 1)
                    if t >= 1:
                        pe.wait_ge(xh_t_out, t)
                    for k in range(KD):
                        last = nc.tensor.transpose(ps_b[:, k // 4, (k % 4) * P:(k % 4 + 1) * P],
                                                   y[t % 2][:, k * P:(k + 1) * P], ident[:, :])
                    last.then_inc(xh_turned, 1)

                def route(t):
                    pe.wait_ge(xh_t_out, t + 1)
                    if t >= 1:
                        pe.wait_ge(logits_out, t)
                    for k in range(KD):
                        last = nc.tensor.matmul(ps_l[:, 0:EXPERTS], xh_t[t % 2][:, k, :],
                                                router[:, k, :], start=(k == 0), stop=(k == KD - 1))
                    last.then_inc(logits_ready, 1)

                turn_out2(0)
                for t in range(T + 2):
                    if t + 1 < T:
                        turn_out2(t + 1)
                    if t < T:
                        lower(t)
                    if 1 <= t <= T:
                        turn_xh(t - 1)
                    if t >= 2:
                        route(t - 2)

                def turn(r, b, part, arrived=None):
                    if part == 0:
                        pe.wait_ge(x_in[b], arrived)
                    if isinstance(r, int) and r + part == 0:
                        pe.wait_ge(xh_t_out, T)
                        pe.wait_ge(logits_out, T)
                    else:
                        pe.wait_ge(x_lo_ready, r * 2 + part)
                    for k in range(3):
                        c = 3 * part + k
                        last = nc.tensor.transpose(ps_x[:, k * P:(k + 1) * P], x_row[b][:, c * P:(c + 1) * P],
                                                   ident[:, :])
                    last.then_inc(turned, 1)

                def piece(buffer, w, q, col, n):
                    if isinstance(buffer, int):
                        return w[:, buffer, q * D + col:q * D + col + n]
                    return w[:, ds(buffer, 1), q * D + col:q * D + col + n].rearrange("p o n -> p (o n)")

                def widen(b, buffer, which, ps, ready):
                    for k in range(KD):
                        for m, (rows, w) in enumerate(((x_hi, w_hi), (x_hi, w_lo), (x_lo, w_hi))):
                            last = nc.tensor.matmul(ps[:, 0:I], rows[b][:, k, :], piece(buffer, w, k, which * I, I),
                                                    start=(k == 0 and m == 0), stop=(k == KD - 1 and m == 2))
                    last.then_inc(ready, 1)

                def turn_inner(v, b):
                    pe.wait_ge(inner_ready, AHEAD + v + 1)
                    pe.wait_ge(i_lo_ready, AHEAD + v)
                    for k in range(KI):
                        last = nc.tensor.transpose(ps_i[:, k * P:(k + 1) * P], inner[b][:, k * P:(k + 1) * P],
                                                   ident[:, :])
                    last.then_inc(inner_turned, 1)

                def narrow(v, n, buffer, first=True, final=True):
                    pe.wait_ge(i_lo_ready, AHEAD + v + 1)
                    if first:
                        pe.wait_ge(y_ready, AHEAD + n)
                    for k in range(KI):
                        for m, (rows, w) in enumerate(((i_hi, w_hi), (i_hi, w_lo), (i_lo, w_hi))):
                            for c in range(2):
                                last = nc.tensor.matmul(ps_y[:, c, 0:HALF], rows[:, k, :],
                                                        piece(buffer, w, KD + k, c * HALF, HALF),
                                                        start=(first and k == 0 and m == 0),
                                                        stop=(final and k == KI - 1 and m == 2))
                    last.then_inc(down_ready, 1)

                def shared_steps(t, b, more, arrived):
                    v = 2 * t
                    if more:
                        turn(t + 1, 1 - b, 0, arrived)
                    pe.wait_ge(inner_ready, AHEAD + v)
                    widen(b, 1, 0, ps_g[1], gate_ready)
                    if more:
                        turn(t + 1, 1 - b, 1)
                    turn_inner(v, 0)
                    widen(b, 1, 1, ps_u[1], up_ready)
                    narrow(v, t, 0, True, False)
                    if more:
                        pe.wait_ge(x_lo_ready, t * 2 + 4)
                        widen(1 - b, 0, 0, ps_g[0], gate_ready)
                    turn_inner(v + 1, 1)
                    if more:
                        widen(1 - b, 0, 1, ps_u[0], up_ready)
                    narrow(v + 1, t, 1, False, True)

                turn(0, 0, 0, 16)
                turn(0, 0, 1)
                pe.wait_ge(piece_cut, KD)
                pe.wait_ge(x_lo_ready, 2)
                widen(0, 0, 0, ps_g[0], gate_ready)
                widen(0, 0, 1, ps_u[0], up_ready)
                pe.wait_ge(piece_cut, 2 * PIECES)
                with pe.Fori(0, COUNT_AT // 2) as i:
                    for b in range(2):
                        shared_steps(2 * i + b, b, True, (i + 1 + b) * 16)
                pe.wait_ge(masks_made, MASKS)
                pe.wait_ge(chosen_ready, 1)
                flat = chosen[:, :, :].rearrange("p t e -> p (t e)")
                pe.wait_ge(x_lo_ready, 2 * COUNT_AT + 2)
                nc.tensor.matmul(ps_plan[:, 0:TE], earlier_rows[:, :], flat, start=True, stop=True,
                                 skip_group_check=True)
                nc.tensor.matmul(ps_plan[:, TE:2 * TE], ones[:, :], flat, start=True, stop=True,
                                 skip_group_check=True).then_inc(counted, 1)
                pe.wait_ge(counts_taken, 1)
                with pe.Fori(COUNT_AT // 2, T // 2 - 1) as i:
                    for b in range(2):
                        shared_steps(2 * i + b, b, True, (i + 1 + b) * 16)
                shared_steps(T - 2, 0, True, 16 * (T // 2))
                shared_steps(T - 1, 1, False, None)

                def expert_of(j):
                    return pe.value_load(tile_expert[0:1, ds(j, 1)], min_val=0, max_val=EXPERTS - 1)

                def step(j, b):
                    other = 1 - b
                    v = j + V0
                    e = expert_of(j)
                    turn(j + (2 + R0), b, 0, arrivals(j, b))
                    e_next = expert_of(j + 1)
                    pe.wait_ge(piece_cut, e_next * PIECES + WIDENED)
                    pe.wait_ge(x_lo_ready, 2 * j + (4 + 2 * R0))
                    pe.wait_ge(inner_ready, AHEAD + v)
                    widen(other, e_next % 2, 0, ps_g[other], gate_ready)
                    turn(j + (2 + R0), b, 1)
                    turn_inner(v, b)
                    widen(other, e_next % 2, 1, ps_u[other], up_ready)
                    pe.wait_ge(piece_cut, e * PIECES + COMPLETE)
                    narrow(v, j + N0, e % 2)

                def arrivals(j, b):
                    return 16 * (T // 2 + 2) + (j - b) * 8

                pe.wait_ge(plan_ready, 1)
                for b in range(2):
                    turn(R0 + b, b, 0, 16 * (T // 2 + 1))
                    turn(R0 + b, b, 1)
                e0 = expert_of(0)
                pe.wait_ge(piece_cut, e0 * PIECES + WIDENED)
                pe.wait_ge(x_lo_ready, 2 * R0 + 2)
                widen(0, e0 % 2, 0, ps_g[0], gate_ready)
                widen(0, e0 % 2, 1, ps_u[0], up_ready)
                tiles = pe.value_load(ends_i[0:1, EXPERTS - 1:EXPERTS], min_val=EXPERTS, max_val=TILES)
                with pe.Fori(0, PAIRS) as i:
                    with pe.If(tiles > 2 * i):
                        for b in range(2):
                            step(2 * i + b, b)

            @block.scalar
            def _(act):
                act.nop().then_inc(i_hi_ready, AHEAD)
                for b in range(2):
                    act.nop().then_inc(y_stored[b], 16 * AHEAD)
                for t in range(T + 2):
                    b = t % 2
                    if t < T:
                        act.wait_ge(o_turned, t + 1)
                        if t >= 2:
                            act.wait_ge(lower_ready, t - 1)
                        nc.scalar.copy(out2_t[b][:, 0, :], ps_a[b][:, 0:P])
                        nc.scalar.copy(out2_t[b][0:REST, 1, :], ps_a[b][0:REST, P:2 * P])\
                            .then_inc(o_turned_out, 1)
                    if 1 <= t <= T:
                        act.wait_ge(var_ready, t)
                        nc.scalar.activation(std_c[:, :], mean_var[:, 1:2], ACT.Sqrt, bias=eps[:, 0:1],
                                             scale=1.0).then_inc(std_ready, 1)
                    if t >= 2:
                        act.wait_ge(xh_turned, t - 1)
                        if t >= 4:
                            act.wait_ge(logits_ready, t - 3)
                        nc.scalar.copy(xh_t[b][:, 0:4, :], ps_b[:, 0, 0:512])
                        nc.scalar.copy(xh_t[b][:, 4:KD, :], ps_b[:, 1, 0:256]).then_inc(xh_t_out, 1)
                act.wait_ge(logits_out, T)
                act.wait_ge(x1_stored, 16 * T)
                nc.scalar.activation(scores[:, :, :], logits[:, :, :], ACT.Exp, scale=-1.0).then_inc(exp_ready, 1)
                act.wait_ge(xh_stored[0], 16 * (T // 2))
                act.wait_ge(xh_stored[1], 16 * (T // 2))

                def load_shared(t, b):
                    act.dma_start(x_row[b][:, :], xh_dram[ds(t * P, P), :]).then_inc(x_in[b], 16)

                def round_rows(r, b, part):
                    act.wait_ge(turned, AHEAD + 2 * r + part + 1)
                    nc.scalar.copy(x_hi[b][:, 3 * part:3 * part + 3, :], ps_x[:, 0:I]).then_inc(x_hi_ready, 1)

                def round_inner(v):
                    act.wait_ge(inner_turned, v + 1)
                    act.wait_ge(down_ready, AHEAD + v)
                    nc.scalar.copy(i_hi[:, :, :], ps_i[:, 0:I]).then_inc(i_hi_ready, 1)

                def silu(v):
                    act.wait_ge(gate_biased, v + 1)
                    nc.scalar.activation(gate, gate, ACT.Silu).then_inc(silu_ready, 1)

                def store(n, b, dram, at):
                    act.wait_ge(y_ready, AHEAD + n + 1)
                    act.dma_start(dram[ds(at * P, P), :], y[b][:, :]).then_inc(y_stored[b], 16)

                def load_base(t, b, stored):
                    act.wait_ge(y_stored[b], stored)
                    act.dma_start(y[b][:, :], x1_dram[ds(t * P, P), :]).then_inc(base_in[b], 16)

                def shared_steps(t, b, more, stored):
                    v = 2 * t
                    if more:
                        round_rows(t + 1, 1 - b, 0)
                        round_rows(t + 1, 1 - b, 1)
                    round_inner(v)
                    silu(v + 1)
                    round_inner(v + 1)
                    if more:
                        silu(v + 2)
                        load_base(t + 1, 1 - b, stored)
                    store(t, b, base_dram, t)

                load_shared(0, 0)
                load_shared(1, 1)
                load_base(0, 0, 16 * AHEAD)
                round_rows(0, 0, 0)
                round_rows(0, 0, 1)
                load_shared(2, 0)
                silu(0)
                with act.Fori(0, T // 2 - 2) as i:
                    for b in range(2):
                        t = 2 * i + b
                        shared_steps(t, b, True, 16 * (i + b + AHEAD))
                        load_shared(t + 3, 1 - b)
                shared_steps(T - 4, 0, True, 16 * (T // 2 - 2 + AHEAD))
                load_shared(T - 1, 1)
                shared_steps(T - 3, 1, True, 16 * (T // 2 - 1 + AHEAD))
                shared_steps(T - 2, 0, True, 16 * (T // 2 - 1 + AHEAD))
                shared_steps(T - 1, 1, False, None)

                def load_rows(j, b):
                    act.dma_start(x_row[b][:, :], list_dram[ds(j * P, P), :]).then_inc(x_in[b], 16)

                def step(j, b):
                    v = j + V0
                    act.wait_ge(up_ready, v + 1)
                    round_rows(j + (2 + R0), b, 0)
                    round_rows(j + (2 + R0), b, 1)
                    load_rows(j + 4, b)
                    round_inner(v)
                    silu(v + 1)
                    store(j + N0, b, y_dram, j)

                act.wait_ge(spread_done[0], 16 * CHOSEN * (T // 2))
                act.wait_ge(spread_done[1], 16 * CHOSEN * (T // 2))
                for b in range(2):
                    load_rows(b, b)
                for b in range(2):
                    round_rows(R0 + b, b, 0)
                    round_rows(R0 + b, b, 1)
                    load_rows(2 + b, b)
                silu(V0)
                tiles = act.value_load(ends_i[0:1, EXPERTS - 1:EXPERTS], min_val=EXPERTS, max_val=TILES)
                with act.Fori(0, PAIRS) as i:
                    with act.If(tiles > 2 * i):
                        for b in range(2):
                            step(2 * i + b, b)
                    with act.If(tiles <= 2 * i):
                        for b in range(2):
                            act.nop().then_inc(x_in[b], 16)
                            act.nop().then_inc(y_stored[b], 16)
                for b in range(2):
                    act.wait_ge(y_stored[b], 16 * (AHEAD + T // 2 + PAIRS))
                    act.wait_ge(x_in[b], 16 * (T // 2 + 2 + PAIRS))

            @block.vector
            def _(dve):
                for s in (inner_ready, y_ready, i_lo_ready):
                    dve.nop().then_inc(s, AHEAD)
                step = Count()

                def norm(t):
                    x = acc[:, t, :]
                    for n in range(2):
                        last = nc.vector.bn_stats(stats[:, n, :], x[:, n * HALF:(n + 1) * HALF])
                    last.then_inc(dve_step, 1)
                    dve.wait_ge(dve_step, step.up())
                    nc.vector.bn_aggr(mean_var[:, :], stats[:, :, :]).then_inc(var_ready, 1)
                    dve.wait_ge(std_ready, t + 1)
                    nc.vector.reciprocal(rstd[:, :], std_c[:, :]).then_inc(dve_step, 1)
                    dve.wait_ge(dve_step, step.up())
                    if t >= 2:
                        dve.wait_ge(xh_stored[t % 2], 16 * (t // 2))
                        dve.wait_ge(xh_turned, t - 1)
                    nc.vector.tensor_scalar(y[t % 2][:, :], x, mean_var[:, 0:1], rstd[:, 0:1], ALU.subtract,
                                            ALU.mult).then_inc(xh_ready, 1)

                for t in range(T + 2):
                    if t < T:
                        dve.wait_ge(lower_ready, t + 1)
                        x = acc[:, t, :].rearrange("p (n c) -> p n c", n=2)
                        nc.vector.tensor_tensor(x, ps_w[:, :, 0:HALF], x, ALU.add).then_inc(x1_ready, 1)
                        dve.wait_ge(x1_ready, t + 1)
                        norm(t)
                    if t >= 2:
                        if t == 2:
                            dve.wait_ge(loaded, 80)
                        dve.wait_ge(logits_ready, t - 1)
                        nc.vector.tensor_tensor(logits[:, t - 2, :], ps_l[:, 0:EXPERTS], rb_row[:, :],
                                                ALU.add).then_inc(logits_out, 1)

                def over_tiles(row):
                    return row.unsqueeze(1).to_broadcast([P, T, EXPERTS])

                def done(ins, by=1):
                    ins.then_inc(dve_step, 1)
                    dve.wait_ge(dve_step, step.up())

                V = nc.vector

                def ranks(values, n, first, out):
                    gt, eq = (x[:, :, :, :].rearrange("p t i j -> p t (i j)")[:, :, 0:n * n]
                              .rearrange("p t (i j) -> p t i j", i=n) for x in (ahead, tied))
                    mine = values.unsqueeze(3).to_broadcast([P, T, n, n])
                    other = values.unsqueeze(2).to_broadcast([P, T, n, n])
                    V.tensor_tensor(gt, other, mine, ALU.is_gt)
                    done(V.tensor_tensor(eq, other, mine, ALU.is_equal))
                    done(V.tensor_tensor(eq, eq, first.unsqueeze(1).to_broadcast([P, T, n, n]), ALU.mult))
                    done(V.tensor_tensor(gt, gt, eq, ALU.add))
                    done(V.tensor_reduce(out, gt, AX_X, ALU.add))

                def score_groups():
                    dve.wait_ge(masks_made, MASKS)
                    dve.wait_ge(exp_ready, 1)
                    done(V.tensor_scalar(scores[:, :, :], scores[:, :, :], 1.0, None, ALU.add))
                    done(V.reciprocal(scores[:, :, :], scores[:, :, :]))
                    done(V.tensor_tensor(biased[:, :, :], scores[:, :, :], over_tiles(cb_row[:, :]), ALU.add))
                    by_pair = biased[:, :, :].rearrange("p t (g q r) -> p (t g q) r", g=4, q=2)
                    hi, lo = (x[:, :, :, :].rearrange("p t g q -> p (t g q)") for x in (pair_hi, pair_lo))
                    V.tensor_tensor(hi, by_pair[:, :, 0], by_pair[:, :, 1], ALU.max)
                    done(V.tensor_tensor(lo, by_pair[:, :, 0], by_pair[:, :, 1], ALU.min))
                    V.tensor_tensor(group_score[:, :, :], pair_hi[:, :, :, 0], pair_hi[:, :, :, 1], ALU.max)
                    V.tensor_tensor(group_next[:, :, :], pair_hi[:, :, :, 0], pair_hi[:, :, :, 1], ALU.min)
                    done(V.tensor_tensor(group_kept[:, :, :], pair_lo[:, :, :, 0], pair_lo[:, :, :, 1], ALU.max))
                    done(V.tensor_tensor(group_next[:, :, :], group_next[:, :, :], group_kept[:, :, :], ALU.max))
                    done(V.tensor_tensor(group_score[:, :, :], group_score[:, :, :], group_next[:, :, :], ALU.add))

                def keep_groups():
                    ranks(group_score[:, :, :], 4, before4[:, :, :], group_next[:, :, :])
                    done(V.tensor_scalar(group_kept[:, :, :], group_next[:, :, :], 2.0, None, ALU.is_lt))
                    done(V.tensor_tensor(biased[:, :, :].rearrange("p t (g r) -> p t g r", g=4),
                                         biased[:, :, :].rearrange("p t (g r) -> p t g r", g=4),
                                         group_kept[:, :, :].unsqueeze(3).to_broadcast([P, T, 4, 4]), ALU.mult))

                def choose():
                    ranks(biased[:, :, :], EXPERTS, before[:, :, :], rank[:, :, :])
                    V.scalar_tensor_tensor(out=chosen[:, :, :], in0=rank[:, :, :], scalar=float(CHOSEN), in1=real[:, :, :],
                                           op0=ALU.is_lt, op1=ALU.mult).then_inc(chosen_ready, 1)
                    dve.wait_ge(chosen_ready, 1)

                def weigh():
                    done(V.tensor_tensor(scores[:, :, :], scores[:, :, :], chosen[:, :, :], ALU.mult))
                    done(V.tensor_reduce(total[:, :], scores[:, :, :], AX_X, ALU.add))
                    done(V.tensor_scalar(total[:, :], total[:, :], 1e-20, None, ALU.add))
                    done(V.reciprocal(total[:, :], total[:, :]))
                    done(V.scalar_tensor_tensor(out=scores[:, :, :], in0=scores[:, :, :], scalar=SCALE,
                                                in1=total[:, :].unsqueeze(2).to_broadcast([P, T, EXPERTS]),
                                                op0=ALU.mult, op1=ALU.mult))
                    prior = tied[:, :, :, :]
                    done(V.tensor_tensor(prior, chosen[:, :, :].unsqueeze(2).to_broadcast([P, T, EXPERTS, EXPERTS]),
                                         before[:, :, :].unsqueeze(1).to_broadcast([P, T, EXPERTS, EXPERTS]), ALU.mult))
                    done(V.tensor_reduce(nth[:, :, :], prior, AX_X, ALU.add))

                def count_tiles():
                    done(V.memset(earlier[:, 0, :], 0.0))
                    for t in range(T):
                        done(V.tensor_tensor(earlier[:, t + 1, :], tallies[:, 1, t, :], earlier[:, t, :], ALU.add))
                    done(V.tensor_tensor(filled[:, :, :], earlier[:, T, :].unsqueeze(2).to_broadcast([P, EXPERTS, T]),
                                         thresholds[:, :].unsqueeze(1).to_broadcast([P, EXPERTS, T]), ALU.is_gt))
                    done(V.tensor_reduce(n_tiles[:, :], filled[:, :, :], AX_X, ALU.add))
                    done(V.tensor_scalar(n_tiles[:, :], n_tiles[:, :], 1.0, None, ALU.max))
                    done(V.tensor_tensor(ahead[:, 0, :, :], n_tiles[:, :].unsqueeze(1).to_broadcast([P, EXPERTS, EXPERTS]),
                                         before[:, :, :], ALU.mult))
                    done(V.tensor_reduce(starts[:, :], ahead[:, 0, :, :], AX_X, ALU.add))

                def lay_out():
                    done(V.tensor_tensor(ends[:, :], starts[:, :], n_tiles[:, :], ALU.add))
                    V.tensor_copy(ends_i[:, :], ends[0:1, :])
                    done(V.tensor_tensor(passed[:, :, :], tile_ids[:, :].unsqueeze(2).to_broadcast([P, TILES + 1, EXPERTS]),
                                         ends[:, :].unsqueeze(1).to_broadcast([P, TILES + 1, EXPERTS]), ALU.is_ge))
                    done(V.tensor_reduce(tile_f[:, :], passed[:, :, :], AX_X, ALU.add))
                    done(V.tensor_scalar(tile_f[:, :], tile_f[:, :], float(EXPERTS - 1), None, ALU.min))
                    V.tensor_copy(tile_expert[:, :], tile_f[0:1, :]).then_inc(plan_ready, 1)
                    done(V.tensor_tensor(place[:, :, :], tallies[:, 0, :, :], earlier[:, 0:T, :], ALU.add))
                    done(V.scalar_tensor_tensor(out=place[:, :, :], in0=over_tiles(starts[:, :]), scalar=float(P),
                                                in1=place[:, :, :], op0=ALU.mult, op1=ALU.add))

                def pick(k):
                    done(V.scalar_tensor_tensor(out=mask[:, :, :], in0=nth[:, :, :], scalar=float(k),
                                                in1=chosen[:, :, :], op0=ALU.is_equal, op1=ALU.mult))
                    done(V.tensor_tensor(picked[:, :, :], mask[:, :, :], scores[:, :, :], ALU.mult))
                    done(V.tensor_reduce(mix[:, k, :], picked[:, :, :], AX_X, ALU.add))
                    done(V.tensor_tensor(picked[:, :, :], mask[:, :, :], place[:, :, :], ALU.mult))
                    done(V.tensor_reduce(place_k[:, k, :], picked[:, :, :], AX_X, ALU.add))

                def list_places():
                    wide_dump = dump[:, :, :]
                    wide_real = real[:, :, 0].unsqueeze(1).to_broadcast([P, CHOSEN, T])
                    done(V.tensor_tensor(list_k[:, :, :], place_k[:, :, :], wide_dump, ALU.subtract))
                    done(V.tensor_tensor(list_k[:, :, :], list_k[:, :, :], wide_real, ALU.mult))
                    done(V.tensor_tensor(list_k[:, :, :], list_k[:, :, :], wide_dump, ALU.add))
                    V.tensor_copy(place_i[:, :, :], place_k[:, :, :])
                    V.tensor_copy(list_i[:, :, :], list_k[:, :, :]).then_inc(list_ready, 1)

                def rest_of_rows(r, b, part):
                    dve.wait_ge(x_hi_ready, 2 * r + part + 1)
                    V.tensor_tensor(x_lo[b][:, 3 * part:3 * part + 3, :], ps_x[:, 0:I].rearrange("p (k n) -> p k n", k=3),
                                    x_hi[b][:, 3 * part:3 * part + 3, :].bitcast(F32), ALU.subtract)\
                        .then_inc(x_lo_ready, 1)

                def rest_of_inner(v):
                    dve.wait_ge(i_hi_ready, AHEAD + v + 1)
                    V.tensor_tensor(i_lo[:, :, :], ps_i[:, 0:I].rearrange("p (k n) -> p k n", k=KI),
                                    i_hi[:, :, :].bitcast(F32), ALU.subtract).then_inc(i_lo_ready, 1)

                def bias_of(rows, buffer, n):
                    return rows[:, ds(buffer * n, n)]

                def bias_gate(v, b, buffer):
                    dve.wait_ge(gate_ready, v + 1)
                    V.tensor_tensor(gate, ps_g[b][:, 0:I], bias_of(bg, buffer, I), ALU.add).then_inc(gate_biased, 1)

                def inside(v, b, buffer):
                    dve.wait_ge(up_ready, v + 1)
                    V.tensor_tensor(up, ps_u[b][:, 0:I], bias_of(bu, buffer, I), ALU.add).then_inc(up_biased, 1)
                    dve.wait_ge(silu_ready, v + 1)
                    dve.wait_ge(up_biased, v + 1)
                    V.tensor_tensor(inner[b][:, :], gate, up, ALU.mult).then_inc(inner_ready, 1)
                    dve.wait_ge(inner_ready, AHEAD + v + 1)

                def add_shared(t, b):
                    rows = y[b][:, :].rearrange("p (n c) -> p n c", n=2)
                    dve.wait_ge(base_in[b], 16 * (t // 2 + 1))
                    done(V.tensor_tensor(rows, bias_of(bd, 0, D).rearrange("p (n c) -> p n c", n=2), rows, ALU.add))
                    dve.wait_ge(down_ready, AHEAD + 2 * t + 2)
                    V.tensor_tensor(rows, ps_y[:, :, 0:HALF], rows, ALU.add).then_inc(y_ready, 1)

                dve.wait_ge(exp_ready, 1)
                rest_of_rows(0, 0, 0)
                rest_of_rows(0, 0, 1)
                dve.wait_ge(piece_cut, KD)
                bias_gate(0, 0, 0)
                inside(0, 0, 0)
                dve.wait_ge(piece_cut, 2 * PIECES)
                for t in range(T):
                    b = t % 2
                    v = 2 * t
                    more = t + 1 < T
                    if t == COUNT_AT:
                        dve.wait_ge(counted, 1)
                        V.tensor_copy(tallies[:, :, :, :].rearrange("p w t e -> p (w t e)"), ps_plan)\
                            .then_inc(counts_taken, 1)
                        dve.wait_ge(counts_taken, 1)
                    if more:
                        rest_of_rows(t + 1, 1 - b, 0)
                    bias_gate(v + 1, 1, 1)
                    if more:
                        rest_of_rows(t + 1, 1 - b, 1)
                    rest_of_inner(v)
                    inside(v + 1, 1, 1)
                    if t == 0:
                        score_groups()
                        keep_groups()
                    if t == 1:
                        choose()
                    if t == 2:
                        weigh()
                    if t == COUNT_AT + 1:
                        pick(0)
                        pick(1)
                    if more:
                        bias_gate(v + 2, 0, 0)
                    rest_of_inner(v + 1)
                    if more:
                        inside(v + 2, 0, 0)
                    add_shared(t, b)
                    if t == COUNT_AT:
                        count_tiles()
                        lay_out()
                    if t == COUNT_AT + 1:
                        pick(2)
                        pick(3)
                        list_places()

                def expert_of(j):
                    return dve.value_load(tile_expert[0:1, ds(j, 1)], min_val=0, max_val=EXPERTS - 1)

                def step(j, b, stored):
                    v = j + V0
                    buffer = expert_of(j) % 2
                    rest_of_rows(j + (2 + R0), b, 0)
                    e_next = expert_of(j + 1)
                    dve.wait_ge(piece_cut, e_next * PIECES + WIDENED)
                    bias_gate(v + 1, 1 - b, e_next % 2)
                    rest_of_rows(j + (2 + R0), b, 1)
                    rest_of_inner(v)
                    inside(v + 1, 1 - b, e_next % 2)
                    dve.wait_ge(down_ready, AHEAD + v + 1)
                    dve.wait_ge(y_stored[b], stored)
                    V.tensor_tensor(y[b][:, :].rearrange("p (n c) -> p n c", n=2), ps_y[:, :, 0:HALF],
                                    bias_of(bd, buffer, D).rearrange("p (n c) -> p n c", n=2), ALU.add)\
                        .then_inc(y_ready, 1)

                dve.wait_ge(plan_ready, 1)
                for b in range(2):
                    rest_of_rows(R0 + b, b, 0)
                    rest_of_rows(R0 + b, b, 1)
                e0 = expert_of(0)
                dve.wait_ge(piece_cut, e0 * PIECES + WIDENED)
                bias_gate(V0, 0, e0 % 2)
                inside(V0, 0, e0 % 2)
                before_tiles = AHEAD + T // 2
                tiles = dve.value_load(ends_i[0:1, EXPERTS - 1:EXPERTS], min_val=EXPERTS, max_val=TILES)
                with dve.Fori(0, PAIRS) as i:
                    with dve.If(tiles > 2 * i):
                        for b in range(2):
                            step(2 * i + b, b, 16 * (i + before_tiles))
                dve.wait_ge(added, EARLY * T)
                for n in range((CHOSEN - EARLY) * T):
                    k, t, q = EARLY + n // T, n % T, n % len(late)
                    dve.wait_ge(late_in[q], 16 * (n // len(late) + 1))
                    if n >= T:
                        dve.wait_ge(summed, n - T + 1)
                    V.scalar_tensor_tensor(out=acc[:, t, :], in0=late[q], scalar=mix[:, k, t:t + 1],
                                           in1=acc[:, t, :], op0=ALU.mult, op1=ALU.add).then_inc(summed, 1)


def program(nc, a, out):
    ctx = ExitStack()
    with ctx:
        keep = {}

        def held(stack, name, shape, dt=F32):
            keep[name] = stack.enter_context(nc.sbuf_tensor(name, shape, dt))

        held(ctx, "ident", [P, P])
        held(ctx, "ones", [P, P])
        held(ctx, "eps", [P, 1])
        held(ctx, "place_i", [P, CHOSEN, T], I32)
        held(ctx, "mix", [P, CHOSEN, T])
        held(ctx, "tile_expert", [1, TILES + 1], I32)
        held(ctx, "ends_i", [1, EXPERTS], I32)
        for name, rows in (("xh_dram", NP), ("x1_dram", NP), ("base_dram", NP), ("y_dram", TILES * P),
                           ("list_dram", (TILES + CHOSEN) * P)):
            keep[name] = nc.dram_tensor(name, (rows, D), F32).ap()
        with ExitStack() as tokens:
            held(tokens, "acc", [P, T, D])
            held(tokens, "h2", [P, T, H2 * (C2 + 2)])
            with ExitStack() as graph:
                held(graph, "h1", [P, T, H1 * (C1 + 2)])
                held(graph, "counts", [P, T, NP], U16)
                for name, heads in (("s_src1", H1), ("s_dst1", H1), ("s_src2", H2), ("s_dst2", H2)):
                    held(graph, name, [P, heads * T])
                edges_and_projection(nc, a, keep)
                held(graph, "no_edge", [P, T, NP], BF16)
                attention(nc, a, keep, 1, H1, C1)
                second_projection(nc, a, keep)
                attention(nc, a, keep, 2, H2, C2)
            network(nc, a, keep, out)


def kernel(**inputs):
    import numpy as _np
    import concourse.bacc as _bacc
    from concourse import mybir as _mybir
    from concourse.bass_utils import run_bass_kernel_spmd as _run

    given = {name.replace("L0_gnn_", "").replace("L0_ffn_", ""): _np.asarray(v) for name, v in inputs.items()}
    spare = LISTED * CHUNK * P - EDGES

    def grouped(edges, filler):
        padded = _np.concatenate([edges, _np.full(spare, filler, edges.dtype)])
        return padded.reshape(LISTED, P, CHUNK).transpose(1, 0, 2).reshape(P, LISTED * CHUNK)

    given["src"] = grouped(given["src"], PAD_SRC)
    given["dst"] = grouped(given["dst"], NODES - 1)
    given["x"] = _np.concatenate([given["x"], _np.zeros((NP + P - NODES, D), given["x"].dtype)])
    given["router_w"] = given["router_w"].T
    for name in ("a_src1", "a_dst1", "a_src2", "a_dst2"):
        given[name] = given[name].reshape(-1)

    nc = _bacc.Bacc("TRN2", target_bir_lowering=False, num_devices=1)
    arrays, a = {}, {}
    for name, value in given.items():
        value = _np.ascontiguousarray(value)
        arrays[f"in_{name}"] = value
        a[name] = nc.dram_tensor(f"in_{name}", value.shape, _mybir.dt.from_np(value.dtype), kind="ExternalInput").ap()
    out = nc.dram_tensor("out", (NP, D), F32, kind="ExternalOutput").ap()
    program(nc, a, out)
    r = _run(nc, [arrays], core_ids=[0])
    return r.results[0]["out"][:NODES]
```

```python
from contextlib import ExitStack, contextmanager

import concourse.bass as bass
from concourse import mybir

ALU = mybir.AluOpType
ACT = mybir.ActivationFunctionType
AX_X = mybir.AxisListType.X
F32 = mybir.dt.float32
BF16 = mybir.dt.bfloat16
F16 = mybir.dt.float16
F32R = mybir.dt.float32r
I32 = mybir.dt.int32
U16 = mybir.dt.uint16

P = 128
NODES = 1250
EDGES = 40000
D = 768
T = -(-NODES // P)
NP = T * P
KD = D // P
HALF = D // 2
EPS = 1e-5
SLOPE = 0.2

CHUNK = 4
GROUPS = 80
LISTED = GROUPS + 1
WIN = 64
PAD_SRC = 4095
NEG = -3.0e38

H1, C1 = 4, 192
H2, C2 = 2, 96

EXPERTS = 16
CHOSEN = 4
IN_GROUP = 4
SCALE = 2.5
I = 384
KI = I // P
SHARED = 2
PAIRS = -(-((NODES * CHOSEN + EXPERTS * P) // P) // 2)
TILES = 2 * PAIRS
SURE = NODES * CHOSEN // P // 2 * 2
PIECES = KD + KI
RAWS = 3
COUNT_AT = 4
MASKS = 7

AHEAD = 1

ds = bass.ds


class Count:

    def __init__(self):
        self.fixed = 0
        self.loops = []

    def up(self, by=1):
        self.fixed += by
        return self.now()

    def now(self):
        value = self.fixed
        for turn, per in self.loops:
            value = turn * per + value
        return value

    @contextmanager
    def turns(self, turn, per, count):
        start = self.fixed
        self.loops.append((turn, per))
        yield
        self.loops.pop()
        assert self.fixed - start == per, (self.fixed - start, per)
        self.fixed = start + per * count


def edges_and_projection(nc, a, keep):
    ctx = ExitStack()
    with ctx:
        def sb(name, shape, dt=F32):
            return ctx.enter_context(nc.sbuf_tensor(name, shape, dt))

        semaphores = []

        def sem(name):
            semaphores.append(nc.alloc_semaphore(name))
            return semaphores[-1]

        counts, acc, h1, s_src, s_dst = keep["counts"], keep["acc"], keep["h1"], keep["s_src1"], keep["s_dst1"]
        ident, ones, eps = keep["ident"], keep["ones"], keep["eps"]

        src_f = sb("src_f", [P, LISTED * CHUNK])
        dst_f = sb("dst_f", [P, LISTED * CHUNK])
        dst_w = sb("dst_w", [P, LISTED * CHUNK])
        node_ids = sb("node_ids", [P, NP], F16)
        group_hi = sb("group_hi", [P, LISTED])
        lo = sb("lo", [LISTED, 1])
        hi = sb("hi", [LISTED, 1])
        bases = sb("bases", [LISTED, LISTED + 1])
        base_i = sb("base_i", [1, LISTED + 1], I32)
        hot_src = [sb(f"hot_src{b}", [P, CHUNK, NP], BF16) for b in range(2)]
        hot_dst = [sb(f"hot_dst{b}", [P, CHUNK, WIN], BF16) for b in range(2)]
        w1 = sb("w1", [P, KD, D])
        wu = sb("wu", [P, KD, D])
        g_row = sb("g_row", [P, D])
        b_row = sb("b_row", [P, D])
        bu_row = sb("bu_row", [P, D])
        a_src = sb("a_src", [P, D])
        a_dst = sb("a_dst", [P, D])
        x_in = [sb(f"x_in{b}", [P, D]) for b in range(2)]
        x0 = [sb(f"x0_{b}", [P, D]) for b in range(2)]
        xn = [sb(f"xn_{b}", [P, D]) for b in range(2)]
        x0_t = [sb(f"x0_t{b}", [P, KD, P]) for b in range(2)]
        xn_t = [sb(f"xn_t{b}", [P, KD, P]) for b in range(2)]
        stats = sb("stats", [P, 2, 6])
        mean_var = sb("mean_var", [P, 2])
        std = sb("std", [P, 1])
        rstd = sb("rstd", [P, 1])
        dot = sb("dot", [P, H1, C1])
        LIST = LISTED * CHUNK
        flat = dot[:, :, :].rearrange("p k c -> p (k c)")
        src_i, dst_i = flat[:, 0:LIST].bitcast(I32), flat[:, LIST:2 * LIST].bitcast(I32)
        group_lo = flat[:, 2 * LIST:2 * LIST + LISTED]
        zeros = keep["h2"][:, :, :].rearrange("p t c -> p (t c)")[:, 0:D]

        ps_t = ctx.enter_context(nc.psum_tensor("ps_t", [P, 2, 512], F32))
        ps_p = ctx.enter_context(nc.psum_tensor("ps_p", [P, 2, 512], F32))
        ps_pairs = [ctx.enter_context(nc.psum_tensor(f"ps_c{b}", [P, 2, 512], F32)) for b in range(2)]
        ps_c = ps_pairs[0]

        edges_in = sem("edges_in")
        weights_in = sem("weights_in")
        rows_in = sem("rows_in")
        x_loaded = [sem(f"x_loaded{b}") for b in range(2)]
        consts_made = sem("consts_made")
        range_found = sem("range_found")
        range_turned = sem("range_turned")
        base_found = sem("base_found")
        base_spread = sem("base_spread")
        base_ready = sem("base_ready")
        counts_clear = sem("counts_clear")
        ones_set = sem("ones_set")
        zeros_made = sem("zeros_made")
        lists_clear = sem("lists_clear")
        hot_ready = sem("hot_ready")
        last_ready = sem("last_ready")
        act_step = sem("act_step")
        pairs_ready = sem("pairs_ready")
        pairs_added = sem("pairs_added")
        var_ready = sem("var_ready")
        std_ready = sem("std_ready")
        x0_ready = sem("x0_ready")
        xhat_ready = sem("xhat_ready")
        xn_ready = sem("xn_ready")
        acc_seeded = sem("acc_seeded")
        turned = sem("turned")
        turned_out = sem("turned_out")
        h_ready = sem("h_ready")
        u_ready = sem("u_ready")
        h_out = sem("h_out")
        u_copied = sem("u_copied")
        u_added = sem("u_added")
        dots_done = sem("dots_done")
        dve_step = sem("dve_step")
        pool_step = sem("pool_step")
        gen_hot = sem("gen_hot")
        gen_pairs = sem("gen_pairs")
        gen_added = sem("gen_added")

        PAIRS = T // 2
        PER_TILE = GROUPS // T
        LIST_CLEAR = (TILES + CHOSEN) // PAIRS
        Y_CLEAR = -(-(TILES - SURE) // PAIRS)
        assert LIST_CLEAR * PAIRS == TILES + CHOSEN

        with nc.Block() as block:

            @block.sync
            def _(sp):
                sp.dma_start(dst_i, a["dst"]).then_inc(edges_in, 16)
                sp.dma_start(x_in[0][:, :], a["x"][0:P, :]).then_inc(x_loaded[0], 16)
                sp.dma_start(src_i, a["src"]).then_inc(edges_in, 16)
                for row, source in ((g_row, "norm_g"), (b_row, "norm_b"), (bu_row, "bu"),
                                    (a_src, "a_src1"), (a_dst, "a_dst1")):
                    sp.dma_start(row[:, :], a[source].partition_broadcast(P)).then_inc(rows_in, 16)
                with sp.Fori(0, PAIRS) as i:
                    for b in range(2):
                        t = 2 * i + b
                        sp.wait_ge(x0_ready, AHEAD + t)
                        sp.wait_ge(acc_seeded, AHEAD + t)
                        sp.dma_start(x_in[1 - b][:, :], a["x"][ds((t + 1) * P, P), :]).then_inc(x_loaded[1 - b], 16)

            @block.gpsimd
            def _(pool):
                pool.nop().then_inc(acc_seeded, AHEAD)
                pool.nop().then_inc(xn_ready, AHEAD)
                pool.nop().then_inc(u_added, AHEAD)
                nc.gpsimd.memset(ident[:, :], 0.0).then_inc(pool_step, 1)
                nc.gpsimd.memset(ones[:, :], 1.0).then_inc(consts_made, 1)
                nc.gpsimd.memset(eps[:, :], EPS).then_inc(consts_made, 1)
                pool.wait_ge(pool_step, 1)
                nc.gpsimd.affine_select(out=ident[:, :], in_=ident[:, :], compare_op=ALU.not_equal, fill=1.0,
                                        base=0, pattern=[[-1, P]], channel_multiplier=1).then_inc(consts_made, 1)
                nc.gpsimd.iota(node_ids[:, :], pattern=[[1, NP]], base=0, channel_multiplier=0,
                               allow_small_or_imprecise_dtypes=True).then_inc(consts_made, 1)
                nc.gpsimd.memset(h1[:, :, :], 1.0).then_inc(ones_set, 1)
                nc.gpsimd.memset(zeros, 0.0).then_inc(zeros_made, 1)
                step = Count()
                step.up()
                pool.wait_ge(rows_in, 16 * 5)

                def seed_and_scale(t, b, loaded):
                    pool.wait_ge(x_loaded[b], loaded)
                    nc.gpsimd.tensor_tensor(acc[:, t, :], x_in[b][:, :], bu_row[:, :], ALU.add).then_inc(acc_seeded, 1)
                    pool.wait_ge(xhat_ready, AHEAD + t + 1)
                    nc.gpsimd.tensor_tensor(xn[b][:, :], xn[b][:, :], g_row[:, :], ALU.mult).then_inc(pool_step, 1)
                    pool.wait_ge(pool_step, step.up())
                    nc.gpsimd.tensor_tensor(xn[b][:, :], xn[b][:, :], b_row[:, :], ALU.add).then_inc(xn_ready, 1)

                def add_u(t, b):
                    pool.wait_ge(u_copied, AHEAD + t + 1)
                    nc.gpsimd.tensor_tensor(acc[:, t, :], x0[b][:, :], acc[:, t, :], ALU.add).then_inc(u_added, 1)

                for t in range(T + 1):
                    if t < T:
                        seed_and_scale(t, t % 2, (t // 2 + 1) * 16)
                    if t >= 1:
                        add_u(t - 1, (t - 1) % 2)

            @block.scalar
            def _(act):
                act.nop().then_inc(turned_out, AHEAD)
                act.nop().then_inc(h_out, AHEAD)
                act.nop().then_inc(u_copied, AHEAD)
                act.wait_ge(edges_in, 32)
                act.dma_start(wu[:, :, :], a["Wu"][0:D, :].rearrange("(k p) n -> p k n", p=P)).then_inc(weights_in, 16)
                act.dma_start(w1[:, :, :], a["W1"].rearrange("(k p) n -> p k n", p=P)).then_inc(weights_in, 16)
                act.wait_ge(consts_made, 2)
                act.wait_ge(ones_set, 1)
                act.wait_ge(zeros_made, 1)

                def clear(name, first, tiles):
                    act.dma_start(keep[name][ds(first * P, tiles * P), :].rearrange("(t p) d -> p t d", p=P),
                                  zeros.unsqueeze(1).to_broadcast([P, tiles, D])).then_inc(lists_clear, 16)

                def root(count):
                    act.wait_ge(var_ready, count)
                    nc.scalar.activation(std[:, :], mean_var[:, 1:2], ACT.Sqrt, bias=eps[:, 0:1],
                                         scale=1.0).then_inc(std_ready, 1)

                def take_turned(out, count):
                    act.wait_ge(turned, AHEAD + count)
                    nc.scalar.copy(out[:, 0:4, :], ps_t[:, 0, 0:512])
                    nc.scalar.copy(out[:, 4:KD, :], ps_t[:, 1, 0:256]).then_inc(turned_out, 1)

                def last_sources(hot_s, g):
                    row = hot_s[:, CHUNK - 1, :]
                    nc.scalar.activation(row, node_ids[:, :], ACT.Abs, bias=src_f[:, ds(g * CHUNK + CHUNK - 1, 1)],
                                         scale=-1.0).then_inc(act_step, 1)
                    act.wait_ge(act_step, g + 1)
                    nc.scalar.activation(row, row, ACT.Relu, bias=ones[:, 0:1], scale=-1.0)\
                        .then_inc(last_ready, 1)

                act.wait_ge(consts_made, 4)
                act.wait_ge(range_found, 1)
                last_sources(hot_src[0], 0)
                root(1)
                root(2)
                with act.Fori(0, PAIRS) as i:
                    clear("list_dram", i * LIST_CLEAR, LIST_CLEAR)
                    clear("y_dram", i * Y_CLEAR + (TILES - PAIRS * Y_CLEAR), Y_CLEAR)
                    for b in range(2):
                        t = 2 * i + b
                        for slot in range(PER_TILE):
                            g = t * PER_TILE + slot
                            if slot == 5:
                                act.wait_ge(h_ready, t + 1)
                                for n in range(2):
                                    last = nc.scalar.copy(h1[:, t, 2 * n * (C1 + 2):2 * (n + 1) * (C1 + 2)]
                                                          .rearrange("p (h c) -> p h c", h=2)[:, :, 0:C1],
                                                          ps_p[:, n, 0:HALF].rearrange("p (h c) -> p h c", h=2))
                                last.then_inc(h_out, 1)
                            act.wait_ge(pairs_ready, AHEAD + g)
                            last_sources(hot_src[(slot + 1) % 2], g + 1)
                            if slot == 0:
                                take_turned(x0_t[b], 2 * t + 1)
                                root(2 * t + 3)
                            if slot == 1:
                                take_turned(xn_t[b], 2 * t + 2)
                            if slot == 2:
                                root(2 * t + 4)
                        act.wait_ge(u_ready, t + 1)
                        nc.scalar.copy(x0[b][:, :].rearrange("p (n c) -> p n c", n=2), ps_p[:, :, 0:HALF])\
                            .then_inc(u_copied, 1)
                act.wait_ge(lists_clear, 32 * PAIRS)

            @block.tensor
            def _(pe):
                pe.nop().then_inc(turned, AHEAD)
                pe.nop().then_inc(pairs_ready, AHEAD)
                pe.wait_ge(consts_made, 4)
                pe.wait_ge(range_found, 1)
                nc.tensor.transpose(ps_c[0:LISTED, 0, 0:P], group_lo, ident[:, :])
                nc.tensor.transpose(ps_c[0:LISTED, 0, P:2 * P], group_hi[:, :], ident[:, :]).then_inc(range_turned, 1)
                pe.wait_ge(base_found, 2)
                nc.tensor.matmul(ps_c[:, 1, 0:LISTED + 1], ones[0:LISTED, :], bases[:, :], start=True,
                                 stop=True).then_inc(base_spread, 1)
                pe.wait_ge(base_ready, 1)

                def pair_products(hot_s, hot_d, out):
                    for c in range(CHUNK):
                        for j in range(T):
                            col = (j % 5) * WIN
                            last = nc.tensor.matmul(out[:, j // 5, col:col + WIN], hot_s[:, c, j * P:(j + 1) * P],
                                                    hot_d[:, c, :], start=(c == 0 and j % 5 == 0),
                                                    stop=(c == CHUNK - 1), skip_group_check=True)
                    return last

                def turn(rows, ready, t, count):
                    pe.wait_ge(ready, AHEAD + t + 1)
                    pe.wait_ge(turned_out, AHEAD + count)
                    for k in range(KD):
                        last = nc.tensor.transpose(ps_t[:, k // 4, (k % 4) * P:(k % 4 + 1) * P],
                                                   rows[:, k * P:(k + 1) * P], ident[:, :])
                    last.then_inc(turned, 1)

                def project(out, lhs, w, ks):
                    for k in ks:
                        for n in range(2):
                            last = nc.tensor.matmul(out[:, n, 0:HALF], lhs[:, k, :], w[:, k, n * HALF:(n + 1) * HALF],
                                                    start=(k == 0), stop=(k == KD - 1))
                    return last

                with pe.Fori(0, PAIRS) as i:
                    for b in range(2):
                        t = 2 * i + b
                        for slot in range(PER_TILE):
                            g = t * PER_TILE + slot
                            if slot == 7:
                                project(ps_p, x0_t[b], wu, range(4, KD)).then_inc(u_ready, 1)
                            pe.wait_ge(hot_ready, g + 1)
                            pe.wait_ge(last_ready, g + 1)
                            pe.wait_ge(pairs_added, g + 1)
                            pair_products(hot_src[slot % 2], hot_dst[slot % 2], ps_pairs[slot % 2])\
                                .then_inc(pairs_ready, 1)
                            if slot == 0:
                                turn(x0[b], x0_ready, t, 2 * t)
                            if slot == 1:
                                turn(xn[b], xn_ready, t, 2 * t + 1)
                            if slot == 2:
                                pe.wait_ge(weights_in, 32)
                                pe.wait_ge(turned_out, AHEAD + 2 * t + 2)
                                pe.wait_ge(u_copied, AHEAD + t)
                            if slot == 5:
                                pe.wait_ge(h_out, AHEAD + t + 1)
                            if 2 <= slot <= 4:
                                last = project(ps_p, xn_t[b], w1, range(2 * slot - 4, 2 * slot - 2))
                                if slot == 4:
                                    last.then_inc(h_ready, 1)
                            if slot == 5:
                                project(ps_p, x0_t[b], wu, range(0, 2))
                            if slot == 6:
                                project(ps_p, x0_t[b], wu, range(2, 4))

                wide = pe.value_load(base_i[0:1, LISTED:LISTED + 1], min_val=0, max_val=LISTED)
                with pe.If(wide > 0):
                    with pe.Fori(0, NP // WIN) as w:
                        with pe.Fori(0, GROUPS) as g:
                            pe.wait_ge(gen_hot, w * GROUPS + g + 1)
                            pair_products(hot_src[0], hot_dst[0], ps_c).then_inc(gen_pairs, 1)

            @block.vector
            def _(dve):
                dve.nop().then_inc(x0_ready, AHEAD)
                dve.nop().then_inc(xhat_ready, AHEAD)
                dve.nop().then_inc(pairs_added, 2)
                step = Count()
                nc.vector.memset(counts[:, :, :].rearrange("p t n -> p (t n)").bitcast(F32), 0.0)\
                    .then_inc(counts_clear, 1)
                dve.wait_ge(edges_in, 32)
                nc.vector.tensor_copy(dst_f[:, :], dst_i).then_inc(dve_step, 1)
                nc.vector.tensor_copy(src_f[:, :], src_i).then_inc(dve_step, 1)
                dve.wait_ge(dve_step, step.up(2))
                grouped = dst_f[:, :].rearrange("p (g c) -> p g c", c=CHUNK)
                nc.vector.tensor_reduce(group_lo, grouped, AX_X, ALU.min)
                nc.vector.tensor_reduce(group_hi[:, :], grouped, AX_X, ALU.max).then_inc(range_found, 1)
                dve.wait_ge(range_turned, 1)
                nc.vector.tensor_reduce(lo[:, :], ps_c[0:LISTED, 0, 0:P], AX_X, ALU.min).then_inc(dve_step, 1)
                nc.vector.tensor_reduce(hi[:, :], ps_c[0:LISTED, 0, P:2 * P], AX_X, ALU.max).then_inc(dve_step, 1)
                dve.wait_ge(dve_step, step.up(2))
                nc.vector.tensor_scalar(lo[:, :], lo[:, :], float(NP - WIN), None, ALU.min).then_inc(dve_step, 1)
                dve.wait_ge(dve_step, step.up())
                nc.vector.tensor_tensor(hi[:, :], hi[:, :], lo[:, :], ALU.subtract).then_inc(dve_step, 1)
                nc.vector.tensor_scalar(bases[:, 0:LISTED], ident[0:LISTED, 0:LISTED], lo[:, 0:1], None,
                                        ALU.mult).then_inc(base_found, 1)
                dve.wait_ge(dve_step, step.up())
                nc.vector.tensor_scalar(bases[:, LISTED:LISTED + 1], hi[:, :], float(WIN), None,
                                        ALU.is_ge).then_inc(base_found, 1)
                dve.wait_ge(base_spread, 1)
                nc.vector.tensor_copy(base_i[:, :], ps_c[0:1, 1, 0:LISTED + 1]).then_inc(dve_step, 1)
                for c in range(CHUNK):
                    nc.vector.tensor_tensor(dst_w[:, :].rearrange("p (g c) -> p g c", c=CHUNK)[:, :, c],
                                            dst_f[:, :].rearrange("p (g c) -> p g c", c=CHUNK)[:, :, c],
                                            ps_c[:, 1, 0:LISTED], ALU.subtract).then_inc(dve_step, 1)

                def self_loops():
                    for j in range(T):
                        last = nc.vector.tensor_copy(counts[:, j, j * P:(j + 1) * P], ident[:, :])
                    return last

                dve.wait_ge(consts_made, 4)
                dve.wait_ge(counts_clear, 1)
                self_loops().then_inc(base_ready, 1)
                dve.wait_ge(dve_step, step.up(1 + CHUNK))
                dve.wait_ge(base_ready, 1)

                def one_hots(hot_s, hot_d, g, dsts, base, chunks):
                    for c in range(chunks):
                        nc.vector.tensor_scalar(hot_s[:, c, :], node_ids[:, :], src_f[:, ds(g * CHUNK + c, 1)],
                                                None, ALU.is_equal)
                    return nc.vector.tensor_tensor(
                        hot_d[:, :, :], node_ids[:, ds(base, WIN)].unsqueeze(1).to_broadcast([P, CHUNK, WIN]),
                        dsts[:, ds(g * CHUNK, CHUNK)].unsqueeze(2).to_broadcast([P, CHUNK, WIN]), ALU.is_equal)

                def add_pairs(base, ps):
                    window = counts[:, :, ds(base, WIN)].rearrange("p (n j) w -> p n j w", n=2)
                    return nc.vector.tensor_tensor(
                        window, ps[:, :, 0:T // 2 * WIN].rearrange("p n (j w) -> p n j w", w=WIN), window, ALU.add)

                def halves(x):
                    for n in range(2):
                        last = nc.vector.bn_stats(stats[:, n, :], x[:, n * HALF:(n + 1) * HALF])
                    return last.then_inc(dve_step, 1)

                def aggregate():
                    return nc.vector.bn_aggr(mean_var[:, :], stats[:, :, :]).then_inc(var_ready, 1)

                def invert(count):
                    dve.wait_ge(std_ready, count)
                    return nc.vector.reciprocal(rstd[:, :], std[:, :]).then_inc(dve_step, 1)

                def normalise(x, out):
                    return nc.vector.tensor_scalar(out[:, :], x[:, :], mean_var[:, 0:1], rstd[:, 0:1],
                                                   ALU.subtract, ALU.mult)

                one_hots(hot_src[0], hot_dst[0], 0, dst_w, 0, CHUNK - 1).then_inc(hot_ready, 1)
                dve.wait_ge(x_loaded[0], 16)
                for x, out, count, ready in ((x_in[0], x0[0], 1, x0_ready), (x0[0], xn[0], 2, xhat_ready)):
                    halves(x)
                    dve.wait_ge(dve_step, step.up())
                    aggregate()
                    invert(count)
                    dve.wait_ge(dve_step, step.up())
                    normalise(x, out).then_inc(ready, 1)
                    dve.wait_ge(ready, AHEAD + 1)
                with dve.Fori(0, PAIRS) as i, step.turns(i, 2 * 4, PAIRS):
                    for b in range(2):
                        t = 2 * i + b
                        other = 1 - b
                        for slot in range(PER_TILE):
                            g = t * PER_TILE + slot
                            if slot == 0:
                                dve.wait_ge(x_loaded[other], (i + 1 + b) * 16)
                                dve.wait_ge(turned, AHEAD + 2 * t)
                                halves(x_in[other])
                            if slot == 2:
                                dve.wait_ge(x0_ready, AHEAD + t + 2)
                                halves(x0[other])
                            if slot in (0, 2):
                                dve.wait_ge(dve_step, step.up())
                            one_hots(hot_src[(slot + 1) % 2], hot_dst[(slot + 1) % 2], g + 1, dst_w, 0, CHUNK - 1)\
                                .then_inc(hot_ready, 1)
                            if slot in (0, 2):
                                aggregate()
                            if slot in (1, 3):
                                invert(2 * t + 2 + (slot + 1) // 2)
                            base = dve.value_load(base_i[0:1, ds(g, 1)], min_val=0, max_val=NP - WIN)
                            dve.wait_ge(pairs_ready, AHEAD + g + 1)
                            dve.wait_ge(pairs_added, g + 2)
                            add_pairs(base, ps_pairs[slot % 2]).then_inc(pairs_added, 1)
                            if slot == 1:
                                dve.wait_ge(dve_step, step.up())
                                dve.wait_ge(u_added, AHEAD + t)
                                normalise(x_in[other], x0[other]).then_inc(x0_ready, 1)
                            if slot == 3:
                                dve.wait_ge(dve_step, step.up())
                                normalise(x0[other], xn[other]).then_inc(xhat_ready, 1)
                            if slot in (5, 6):
                                dve.wait_ge(h_out, AHEAD + t + 1)
                                for h in range(2 * (slot - 5), 2 * (slot - 4)):
                                    for which, weights, scores in ((0, a_src, s_src), (1, a_dst, s_dst)):
                                        last = nc.vector.scalar_tensor_tensor(
                                            out=dot[:, 2 * (h % 2) + which, :],
                                            in0=h1[:, t, h * (C1 + 2):h * (C1 + 2) + C1], scalar=1.0,
                                            in1=weights[:, h * C1:(h + 1) * C1], op0=ALU.mult, op1=ALU.mult,
                                            accum_out=scores[:, ds(t + h * T, 1)])
                                last.then_inc(dots_done, 1)
                                dve.wait_ge(dots_done, 2 * t + slot - 4)

                dve.wait_ge(pairs_added, 2 + GROUPS)
                dve.wait_ge(last_ready, GROUPS + 1)
                wide = dve.value_load(base_i[0:1, LISTED:LISTED + 1], min_val=0, max_val=LISTED)
                with dve.If(wide > 0):
                    nc.vector.memset(counts[:, :, :], 0).then_inc(gen_added, 1)
                    dve.wait_ge(gen_added, 1)
                    self_loops().then_inc(gen_added, 1)
                    dve.wait_ge(gen_added, 2)
                    with dve.Fori(0, NP // WIN) as w:
                        with dve.Fori(0, GROUPS) as g:
                            one_hots(hot_src[0], hot_dst[0], g, dst_f, w * WIN, CHUNK).then_inc(gen_hot, 1)
                            dve.wait_ge(gen_pairs, w * GROUPS + g + 1)
                            add_pairs(w * WIN, ps_c).then_inc(gen_added, 1)
                            dve.wait_ge(gen_added, w * GROUPS + g + 3)

        nc.clear_and_free_semaphores(semaphores)
        nc.all_engine_barrier()


def attention(nc, a, keep, layer, heads, width):
    ctx = ExitStack()
    with ctx:
        def sb(name, shape, dt=F32):
            return ctx.enter_context(nc.sbuf_tensor(f"{name}_{layer}", shape, dt))

        def sem(name):
            return ctx.enter_context(nc.semaphore(f"{name}_{layer}"))

        counts, no_edge, ident = keep["counts"], keep["no_edge"], keep["ident"]
        h_rows, s_src, s_dst = keep[f"h{layer}"], keep[f"s_src{layer}"], keep[f"s_dst{layer}"]
        W = width + 2
        PER_BANK = 512 // W if 512 // W < T // 2 else T // 2
        BANKS = T // PER_BANK
        HT = heads * T
        RING = 5

        top = sb("top", [P, HT])
        peak = sb("peak", [P, HT])
        src_low = sb("src_low", [P, HT])
        shifts = sb("shifts", [P, heads, 2, T])
        shifts_t = sb("shifts_t", [2 * HT, P])
        shift_rows = [sb(f"shift_rows{b}", [P, 2, NP]) for b in range(2)]
        weights = [sb(f"weights{b}", [P, NP]) for b in range(RING)]
        best = weights[0:heads]
        assert heads <= RING and T % RING == 0
        rden = sb("rden", [P, T])
        bias_row = sb("bias_row", [P, heads * width])
        shift_dram = nc.dram_tensor(f"shift_dram_{layer}", (2 * HT, P), F32).ap()

        ps_o = ctx.enter_context(nc.psum_tensor(f"ps_o_{layer}", [P, 5, 512], F32))
        ps_m = ctx.enter_context(nc.psum_tensor(f"ps_m_{layer}", [P, 3, 512], F32))

        bias_in = sem("bias_in")
        masked = sem("masked")
        best_step = sem("best_step")
        best_turned = sem("best_turned")
        top_ready = sem("top_ready")
        small_step = sem("small_step")
        shifts_ready = sem("shifts_ready")
        shifts_turned = sem("shifts_turned")
        shifts_out = sem("shifts_out")
        shifts_stored = sem("shifts_stored")
        rows_in = [sem(f"shift_rows_in{b}") for b in range(2)]
        low_ready = sem("low_ready")
        bound_ready = sem("bound_ready")
        exp_ready = sem("exp_ready")
        weights_ready = sem("weights_ready")
        weights_used = sem("weights_used")
        inverse_ready = sem("inverse_ready")
        head_out = sem("head_out")

        def best_steps(h):
            return (h // 2) * 2 * T + 2 * (T - 1) + h % 2 + 1

        with nc.Block() as block:

            @block.sync
            def _(sp):
                sp.dma_start(bias_row[:, :], a[f"b{layer}"].partition_broadcast(P)).then_inc(bias_in, 16)
                if layer == 1:
                    loaded = keep["w2_loaded"]
                    sp.dma_start(keep["w2"][:, :, :], a["W2"].rearrange("(k p) n -> p k n", p=P)).then_inc(loaded, 16)
                    sp.dma_start(keep["a_src2"][:, :], a["a_src2"].partition_broadcast(P)).then_inc(loaded, 16)
                    sp.dma_start(keep["a_dst2"][:, :], a["a_dst2"].partition_broadcast(P)).then_inc(loaded, 16)
                sp.wait_ge(shifts_out, 1)
                sp.dma_start(shift_dram, shifts_t[:, :]).then_inc(shifts_stored, 16)
                sp.wait_ge(shifts_stored, 16)
                by_head = shift_dram.rearrange("(h r) p -> h (r p)", h=heads)
                for h in range(heads):
                    if h >= 2:
                        sp.wait_ge(bound_ready, (h - 1) * T)
                    sp.dma_start(shift_rows[h % 2][:, :, :].rearrange("p s n -> p (s n)"),
                                 by_head[h:h + 1, :].broadcast_to([P, 2 * NP])).then_inc(rows_in[h % 2], 16)

            @block.scalar
            def _(act):
                act.wait_ge(shifts_ready, 1)
                act.wait_ge(shifts_turned, 1)
                nc.scalar.copy(shifts_t[:, :], ps_m[0:2 * HT, 0, 0:P]).then_inc(shifts_out, 1)

                def low_part(b, h, s):
                    act.wait_ge(weights_used, h * T + s + 1)
                    nc.scalar.activation(weights[s % RING][:, :], shift_rows[b][:, 1, :], ACT.Identity,
                                         bias=src_low[:, ds(h * T + s, 1)], scale=1.0).then_inc(low_ready, 1)

                def exps(i, b, more):
                    h = 2 * i + b
                    for s in range(T):
                        if s + 2 < T:
                            low_part(b, h, s + 2)
                        elif more:
                            if s + 2 == T:
                                act.wait_ge(rows_in[1 - b], (i + 1 + b) * 16)
                            low_part(1 - b, h + 1, s + 2 - T)
                        act.wait_ge(bound_ready, h * T + s + 1)
                        w = weights[s % RING]
                        nc.scalar.activation(w[:, :], w[:, :], ACT.Exp).then_inc(exp_ready, 1)

                act.wait_ge(rows_in[0], 16)
                low_part(0, 0, 0)
                low_part(0, 0, 1)
                if heads > 2:
                    with act.Fori(0, heads // 2 - 1) as i:
                        for b in range(2):
                            exps(i, b, True)
                for b in range(2):
                    exps(heads // 2 - 1, b, b == 0)

            @block.tensor
            def _(pe):
                pe.nop().then_inc(weights_used, RING)
                for h in range(heads):
                    pe.wait_ge(best_step, best_steps(h))
                    if h >= 1:
                        pe.wait_ge(top_ready, h)
                    for j in range(T):
                        last = nc.tensor.transpose(ps_m[:, j // 4, (j % 4) * P:(j % 4 + 1) * P],
                                                   best[h][:, j * P:(j + 1) * P], ident[:, :])
                    last.then_inc(best_turned, 1)
                pe.wait_ge(shifts_ready, 1)
                nc.tensor.transpose(ps_m[0:2 * HT, 0, 0:P], shifts[:, :, :, :].rearrange("p h s t -> p (h s t)"),
                                    ident[:, :]).then_inc(shifts_turned, 1)
                with pe.Fori(0, heads) as h:
                    for s in range(T):
                        pe.wait_ge(weights_ready, h * T + s + 1)
                        for j in range(T):
                            col = (j % PER_BANK) * W
                            if s == 0 and j % PER_BANK == 0:
                                pe.wait_ge(head_out, h * BANKS + j // PER_BANK + 1)
                            last = nc.tensor.matmul(ps_o[:, j // PER_BANK, col:col + W],
                                                    weights[s % RING][:, j * P:(j + 1) * P],
                                                    h_rows[:, s, ds(h * W, W)],
                                                    start=(s == 0 and j % PER_BANK == 0), stop=(s == T - 1),
                                                    skip_group_check=True)
                        last.then_inc(weights_used, 1)

            @block.vector
            def _(dve):
                dve.nop().then_inc(head_out, BANKS)
                if layer == 1:
                    nc.vector.tensor_scalar(no_edge[:, :, :], counts[:, :, :], 0.0, NEG, ALU.is_equal,
                                            ALU.mult).then_inc(masked, 1)
                    dve.wait_ge(masked, 1)
                def reduce_best(h):
                    dve.wait_ge(best_turned, h + 1)
                    nc.vector.tensor_reduce(top[:, h * T:h * T + 8], ps_m[:, 0:2, :].rearrange(
                        "p b (j n) -> p (b j) n", n=P), AX_X, ALU.max)
                    nc.vector.tensor_reduce(top[:, h * T + 8:(h + 1) * T], ps_m[:, 2, 0:(T - 8) * P].rearrange(
                        "p (j n) -> p j n", n=P), AX_X, ALU.max).then_inc(top_ready, 1)

                step = Count()
                for pair in range(heads // 2):
                    for s in range(T):
                        for h in (2 * pair, 2 * pair + 1):
                            scalar = s_src[:, h * T + s:h * T + s + 1]
                            if s == 0:
                                last = nc.vector.tensor_scalar(best[h][:, :], no_edge[:, 0, :], scalar, None, ALU.add)
                            else:
                                dve.wait_ge(best_step, step.now() - 1)
                                last = nc.vector.scalar_tensor_tensor(
                                    out=best[h][:, :], in0=no_edge[:, s, :], scalar=scalar, in1=best[h][:, :],
                                    op0=ALU.add, op1=ALU.max)
                            last.then_inc(best_step, 1)
                            step.up()
                        if pair >= 1 and s in (2, 5):
                            reduce_best(2 * (pair - 1) + s // 5)
                reduce_best(heads - 2)
                reduce_best(heads - 1)
                dve.wait_ge(top_ready, heads)
                small = Count()
                nc.vector.tensor_scalar(src_low[:, :], s_src[:, :], SLOPE, None, ALU.mult)
                nc.vector.tensor_tensor(top[:, :], top[:, :], s_dst[:, :], ALU.add).then_inc(small_step, 1)
                dve.wait_ge(small_step, small.up())
                nc.vector.scalar_tensor_tensor(out=peak[:, :], in0=top[:, :], scalar=SLOPE, in1=top[:, :],
                                               op0=ALU.mult, op1=ALU.max).then_inc(small_step, 1)
                dve.wait_ge(small_step, small.up())
                by_head = [x.rearrange("p (h t) -> p h t", t=T) for x in (s_dst[:, :], peak[:, :])]
                nc.vector.tensor_tensor(shifts[:, :, 0, :], by_head[0], by_head[1], ALU.subtract)\
                    .then_inc(small_step, 1)
                nc.vector.scalar_tensor_tensor(out=shifts[:, :, 1, :], in0=by_head[0], scalar=SLOPE, in1=by_head[1],
                                               op0=ALU.mult, op1=ALU.subtract).then_inc(shifts_ready, 1)
                dve.wait_ge(small_step, small.up())
                dve.wait_ge(bias_in, 16)

                def upper(b, h, s):
                    dve.wait_ge(low_ready, h * T + s + 1)
                    w = weights[s % RING]
                    return nc.vector.scalar_tensor_tensor(out=w[:, :], in0=shift_rows[b][:, 0, :],
                                                          scalar=s_src[:, ds(h * T + s, 1)], in1=w[:, :],
                                                          op0=ALU.add, op1=ALU.max)

                def weigh(h, s):
                    dve.wait_ge(exp_ready, h * T + s + 1)
                    w = weights[s % RING]
                    nc.vector.scalar_tensor_tensor(out=w[:, :], in0=w[:, :], scalar=1.0, in1=counts[:, s, :],
                                                   op0=ALU.min, op1=ALU.mult).then_inc(weights_ready, 1)

                def finish(h):
                    dve.wait_ge(weights_used, (h + 1) * T + RING)
                    sums = ps_o[:, 0:BANKS, 0:PER_BANK * W].rearrange("p b (j w) -> p b j w", w=W)
                    nc.vector.reciprocal(rden[:, :].rearrange("p (b j) -> p b j", b=BANKS),
                                         sums[:, :, :, width]).then_inc(inverse_ready, 1)
                    dve.wait_ge(inverse_ready, h + 1)
                    for j in range(T):
                        last = nc.vector.scalar_tensor_tensor(
                            out=h_rows[:, j, ds(h * width, width)],
                            in0=ps_o[:, j // PER_BANK, (j % PER_BANK) * W:(j % PER_BANK) * W + width],
                            scalar=rden[:, j:j + 1], in1=bias_row[:, ds(h * width, width)],
                            op0=ALU.mult, op1=ALU.add)
                        if j % PER_BANK == PER_BANK - 1:
                            last.then_inc(head_out, 1)

                def head(i, b, more):
                    h = 2 * i + b
                    for s in range(1, T):
                        if s + 2 < T:
                            upper(b, h, s + 2).then_inc(bound_ready, 1)
                        elif more:
                            if s + 2 == T:
                                dve.wait_ge(rows_in[1 - b], (i + 1 + b) * 16)
                            upper(1 - b, h + 1, s + 2 - T).then_inc(bound_ready, 1)
                        weigh(h, s)
                    if more:
                        upper(1 - b, h + 1, 2).then_inc(bound_ready, 1)
                        weigh(h + 1, 0)
                    finish(h)

                dve.wait_ge(rows_in[0], 16)
                for s in range(3):
                    upper(0, 0, s).then_inc(bound_ready, 1)
                weigh(0, 0)
                if heads > 2:
                    with dve.Fori(0, heads // 2 - 1) as i:
                        for b in range(2):
                            head(i, b, True)
                for b in range(2):
                    head(heads // 2 - 1, b, b == 0)

            @block.gpsimd
            def _(pool):
                if layer == 1:
                    nc.gpsimd.memset(keep["h2"][:, :, :], 1.0)


def second_projection(nc, a, keep):
    ctx = ExitStack()
    with ctx:
        def sb(name, shape, dt=F32):
            return ctx.enter_context(nc.sbuf_tensor(name, shape, dt))

        def sem(name):
            return ctx.enter_context(nc.semaphore(name))

        h1, h2, s_src, s_dst, ident = keep["h1"], keep["h2"], keep["s_src2"], keep["s_dst2"], keep["ident"]
        W, N2 = C2 + 2, H2 * C2
        w2, a_src, a_dst, loaded = keep["w2"], keep["a_src2"], keep["a_dst2"], keep["w2_loaded"]
        out1_t = [sb(f"out1_t{b}", [P, KD, P]) for b in range(2)]
        dot = sb("dot_b", [P, 2 * H2, C2])
        ps_t = [ctx.enter_context(nc.psum_tensor(f"ps_r{b}", [P, 2, 512], F32)) for b in range(2)]
        ps_p = [ctx.enter_context(nc.psum_tensor(f"ps_p{b}", [P, 512], F32)) for b in range(2)]
        turned = sem("turned_b")
        turned_out = sem("turned_out_b")
        ready = sem("ready_b")
        copied = sem("copied_b")
        dots_done = sem("dots_done_b")

        with nc.Block() as block:

            @block.tensor
            def _(pe):
                pe.nop().then_inc(ready, AHEAD)
                pe.wait_ge(loaded, 48)

                def turn(t):
                    for k in range(KD):
                        last = nc.tensor.transpose(ps_t[t % 2][:, k // 4, (k % 4) * P:(k % 4 + 1) * P],
                                                   h1[:, t, k * P:(k + 1) * P], ident[:, :])
                    last.then_inc(turned, 1)

                for t in range(T + 1):
                    if t < T:
                        if t >= 2:
                            pe.wait_ge(turned_out, t - 1)
                        turn(t)
                    if t >= 1:
                        pe.wait_ge(turned_out, t)
                        if t >= 3:
                            pe.wait_ge(copied, t - 2)
                        for k in range(KD):
                            last = nc.tensor.matmul(ps_p[(t - 1) % 2][:, 0:N2], out1_t[(t - 1) % 2][:, k, :],
                                                    w2[:, k, :], start=(k == 0), stop=(k == KD - 1))
                        last.then_inc(ready, 1)

            @block.scalar
            def _(act):
                with act.Fori(0, T // 2) as i:
                    for b in range(2):
                        t = 2 * i + b
                        act.wait_ge(turned, t + 1)
                        act.wait_ge(ready, AHEAD + 2 * i)
                        nc.scalar.copy(out1_t[b][:, 0:4, :], ps_t[b][:, 0, 0:512])
                        nc.scalar.copy(out1_t[b][:, 4:KD, :], ps_t[b][:, 1, 0:256]).then_inc(turned_out, 1)

            @block.vector
            def _(dve):
                dve.wait_ge(loaded, 48)
                with dve.Fori(0, T // 2) as i:
                    for b in range(2):
                        t = 2 * i + b
                        dve.wait_ge(ready, AHEAD + t + 1)
                        nc.vector.tensor_copy(h2[:, t, :].rearrange("p (h c) -> p h c", h=H2)[:, :, 0:C2],
                                              ps_p[b][:, 0:N2].rearrange("p (h c) -> p h c", h=H2))\
                            .then_inc(copied, 1)
                        dve.wait_ge(copied, t + 1)
                        for h in range(H2):
                            for which, weights, scores in ((0, a_src, s_src), (1, a_dst, s_dst)):
                                last = nc.vector.scalar_tensor_tensor(
                                    out=dot[:, 2 * h + which, :], in0=h2[:, t, h * W:h * W + C2], scalar=1.0,
                                    in1=weights[:, h * C2:(h + 1) * C2], op0=ALU.mult, op1=ALU.mult,
                                    accum_out=scores[:, ds(t + h * T, 1)])
                        last.then_inc(dots_done, 1)
                        dve.wait_ge(dots_done, t + 1)


def network(nc, a, keep, out):
    ctx = ExitStack()
    with ctx:
        def sb(name, shape, dt=F32):
            return ctx.enter_context(nc.sbuf_tensor(name, shape, dt))

        def sem(name):
            return ctx.enter_context(nc.semaphore(name))

        acc, h2, ident, ones, eps = keep["acc"], keep["h2"], keep["ident"], keep["ones"], keep["eps"]
        place_i, mix, tile_expert, ends_i = (keep[n] for n in ("place_i", "mix", "tile_expert", "ends_i"))
        xh_dram, x1_dram, base_dram = keep["xh_dram"], keep["x1_dram"], keep["base_dram"]
        list_dram, y_dram = keep["list_dram"], keep["y_dram"]
        N2 = H2 * C2
        REST = N2 - P
        TE = T * EXPERTS

        w_hi = sb("w_hi", [P, 2, PIECES * D], F32R)
        w_lo = sb("w_lo", [P, 2, PIECES * D], F32R)
        raw = [sb(f"raw{q}", [P, D]) for q in range(RAWS)]
        bg = sb("bg", [P, 2 * I])
        bu = sb("bu", [P, 2 * I])
        bd = sb("bd", [P, 2 * D])
        x_row = [sb(f"x_row{b}", [P, D]) for b in range(2)]
        x_hi = [sb(f"x_hi{b}", [P, KD, P], F32R) for b in range(2)]
        x_lo = [sb(f"x_lo{b}", [P, KD, P], F32R) for b in range(2)]
        widened = sb("widened", [P, 2, I])
        gate, up = widened[:, 0, :], widened[:, 1, :]
        inner = [sb(f"inner{b}", [P, I]) for b in range(2)]
        i_hi = sb("i_hi", [P, KI, P], F32R)
        i_lo = sb("i_lo", [P, KI, P], F32R)
        y = [sb(f"y{b}", [P, D]) for b in range(2)]
        wu_a, wu_b = x_row[0][:, :], x_row[1][0:REST, :]
        out2_t = [inner[b][:, 0:2 * P].rearrange("p (k n) -> p k n", k=2) for b in range(2)]
        xh_t = [sb("xh_t", [P, KD, P])[:, :, :],
                widened[:, :, :].rearrange("p w n -> p (w n)").rearrange("p (k n) -> p k n", k=KD)]
        router = sb("router", [P, KD, EXPERTS])
        rb_row = sb("rb_row", [P, EXPERTS])
        cb_row = sb("cb_row", [P, EXPERTS])
        logits = sb("logits", [P, T, EXPERTS])
        before = sb("before", [P, EXPERTS, EXPERTS], BF16)
        before4 = sb("before4", [P, 4, 4], BF16)
        real = sb("real", [P, T, EXPERTS])
        thresholds = sb("thresholds", [P, T])
        tile_ids = sb("tile_ids", [P, TILES + 1])
        earlier_rows = sb("earlier_rows", [P, P])
        dump = sb("dump", [P, CHOSEN, T])

        mean_var = sb("mean_var_c", [P, 2])
        stats = sb("stats_c", [P, 2, 6])
        std_c = sb("std_c", [P, 1])
        rstd = sb("rstd_c", [P, 1])
        acc_flat, taken = acc[:, :, :].rearrange("p t d -> p (t d)"), [0]

        def room(shape, dt=F32):
            size = 1
            for n in shape[1:]:
                size *= n
            words = size // 2 if dt == BF16 else size
            flat = acc_flat[:, taken[0]:taken[0] + words]
            taken[0] += words
            assert taken[0] <= T * D
            dims = dict(zip("abc", shape[1:]))
            return (flat if dt == F32 else flat.bitcast(dt)).rearrange(
                f"p ({' '.join(dims)}) -> p {' '.join(dims)}", **dims)

        scores = room([P, T, EXPERTS])
        biased = room([P, T, EXPERTS])
        pair_hi = room([P, T, 4, 2])
        pair_lo = room([P, T, 4, 2])
        group_score = room([P, T, 4])
        group_next = room([P, T, 4])
        group_kept = room([P, T, 4])
        ahead = room([P, T, EXPERTS, EXPERTS], BF16)
        tied = room([P, T, EXPERTS, EXPERTS], BF16)
        rank = room([P, T, EXPERTS])
        chosen = room([P, T, EXPERTS])
        nth = room([P, T, EXPERTS])
        mask = room([P, T, EXPERTS])
        picked = room([P, T, EXPERTS])
        place = room([P, T, EXPERTS])
        tallies = room([P, 2, T, EXPERTS])
        total = room([P, T])
        earlier = room([P, T + 1, EXPERTS])
        filled = room([P, EXPERTS, T])
        n_tiles = room([P, EXPERTS])
        starts = room([P, EXPERTS])
        ends = room([P, EXPERTS])
        passed = room([P, TILES + 1, EXPERTS], BF16)
        tile_f = room([P, TILES + 1])
        place_k = room([P, CHOSEN, T])
        list_k = room([P, CHOSEN, T])
        list_i = room([P, CHOSEN, T], I32)
        spread = [room([P, D]) for b in range(2)]
        h2_flat = h2[:, :, :].rearrange("p t c -> p (t c)")
        spread += [h2_flat[:, 0:D], h2_flat[:, D:2 * D], xh_t[0].rearrange("p k n -> p (k n)")]
        SPREADS = len(spread)
        gathered = [raw[q][:, :] for q in range(RAWS)]
        late = gathered + spread[2:] + [y[b][:, :] for b in range(2)]
        FREE = len(late) - 2
        EARLY = 3 * T // 2


        banks = ctx.enter_context(nc.psum_tensor("banks", [P, 8, 512], F32))
        ps_a = [banks[:, b, :] for b in (0, 1)]
        ps_l, ps_b, ps_w = banks[:, 2, :], banks[:, 4:6, :], banks[:, 6:8, :]
        ps_x, ps_i = banks[:, 0, :], banks[:, 1, :]
        ps_g = [banks[:, b, :] for b in (2, 3)]
        ps_u = [banks[:, b, :] for b in (4, 5)]
        ps_y = banks[:, 6:8, :]
        ps_plan = banks[:, 0, 0:2 * TE]

        loaded = sem("loaded_c")
        masks_made = sem("masks_made")
        pool_step = sem("pool_step_c")
        o_turned = sem("o_turned")
        o_turned_out = sem("o_turned_out")
        lower_ready = sem("lower_ready")
        x1_ready = sem("x1_ready")
        dve_step = sem("dve_step_c")
        var_ready = sem("var_ready_c")
        std_ready = sem("std_ready_c")
        xh_ready = sem("xh_ready")
        xh_stored = [sem(f"xh_stored{b}") for b in range(2)]
        x1_stored = sem("x1_stored")
        xh_turned = sem("xh_turned")
        xh_t_out = sem("xh_t_out")
        logits_ready = sem("logits_ready")
        logits_out = sem("logits_out")
        exp_ready = sem("exp_ready_c")
        chosen_ready = sem("chosen_ready")
        counted = sem("counted")
        counts_taken = sem("counts_taken")
        list_ready = sem("list_ready")
        plan_ready = sem("plan_ready")
        spread_in = [sem(f"spread_in{q}") for q in range(SPREADS)]
        spread_done = [sem(f"spread_done{q}") for q in range(SPREADS)]
        raw_in = [sem(f"raw_in{q}") for q in range(RAWS)]
        piece_cut = sem("piece_cut")
        hi_cut = sem("hi_cut")
        bias_in = [sem(f"bias_in{b}") for b in range(2)]
        bd_in = [sem(f"bd_in{b}") for b in range(2)]
        x_in = [sem(f"x_in_sem{b}") for b in range(2)]
        base_in = [sem(f"base_in{b}") for b in range(2)]
        turned = sem("turned_e")
        x_hi_ready = sem("x_hi_ready")
        x_lo_ready = sem("x_lo_ready")
        gate_ready = sem("gate_ready")
        up_ready = sem("up_ready")
        gate_biased = sem("gate_biased")
        up_biased = sem("up_biased")
        silu_ready = sem("silu_ready")
        inner_ready = sem("inner_ready")
        inner_turned = sem("inner_turned")
        i_hi_ready = sem("i_hi_ready")
        i_lo_ready = sem("i_lo_ready")
        down_ready = sem("down_ready")
        y_ready = sem("y_ready")
        y_stored = [sem(f"y_stored{b}") for b in range(2)]
        sums_seeded = sem("sums_seeded")
        stage_open = sem("stage_open")
        gathered_in = [sem(f"gathered_in{q}") for q in range(RAWS)]
        late_in = [sem(f"late_in{q}") for q in range(len(late))]
        weighted = sem("weighted")
        added = sem("added")
        summed = sem("summed")
        out_stored = sem("out_stored")

        V0 = SHARED * T
        WIDENED, COMPLETE = SHARED * PIECES + KD, (SHARED + 1) * PIECES

        with nc.Block() as block:

            @block.sync
            def _(sp):
                sp.dma_start(wu_a, a["Wu"][D:D + P, :]).then_inc(loaded, 16)
                sp.dma_start(wu_b, a["Wu"][D + P:D + N2, :]).then_inc(loaded, 16)
                sp.dma_start(router[:, :, :], a["router_w"].rearrange("(k p) e -> p k e", p=P))\
                    .then_inc(loaded, 16)
                sp.dma_start(rb_row[:, :], a["router_b"].partition_broadcast(P)).then_inc(loaded, 16)
                sp.dma_start(cb_row[:, :], a["corr_bias"].partition_broadcast(P)).then_inc(loaded, 16)

                def inner_biases(b, gate_b, up_b):
                    for dst, src in ((bg, gate_b), (bu, up_b)):
                        sp.dma_start(dst[:, b * I:(b + 1) * I], src.partition_broadcast(P)).then_inc(bias_in[b], 16)

                def down_bias(b, down_b):
                    sp.dma_start(bd[:, b * D:(b + 1) * D], down_b.partition_broadcast(P)).then_inc(bd_in[b], 16)

                def pieces(which, first, gate_w, up_w, down_w):
                    for q in which:
                        r = raw[q % RAWS]
                        if not isinstance(first, int) or first + q >= RAWS:
                            sp.wait_ge(piece_cut, first + q - RAWS + 1)
                        if q < KD:
                            for n, w in ((0, gate_w), (1, up_w)):
                                sp.dma_start(r[:, n * I:(n + 1) * I], w[q * P:(q + 1) * P, :])\
                                    .then_inc(raw_in[q % RAWS], 16)
                        else:
                            sp.dma_start(r[:, :], down_w[(q - KD) * P:(q - KD + 1) * P, :])\
                                .then_inc(raw_in[q % RAWS], 16)

                for b in range(SHARED):
                    cols = slice(b * I, (b + 1) * I)
                    inner_biases(b, a["sbg"][cols], a["sbu"][cols])
                    if b == 0:
                        down_bias(b, a["sbd"])
                    pieces(range(PIECES), b * PIECES, a["sWg"][:, cols], a["sWu"][:, cols], a["sWd"][cols, :])

                def load_expert(e, b, parts, passes, early=False):
                    gate_w, up_w, down_w, gate_b, up_b, down_b = parts
                    first = (e + SHARED) * PIECES
                    if not early:
                        pieces(range(RAWS), first, gate_w, up_w, down_w)
                    sp.wait_ge(inner_ready, AHEAD + passes)
                    inner_biases(b, gate_b, up_b)
                    pieces(range(RAWS, PIECES), first, gate_w, up_w, down_w)
                    sp.wait_ge(y_ready, AHEAD + passes)
                    down_bias(b, down_b)

                names = ("gWg", "gWu", "gWd", "gbg", "gbu", "gbd")
                pieces(range(RAWS), SHARED * PIECES, a["gWg"][0], a["gWu"][0], a["gWd"][0])
                for t in range(T):
                    q = t % SPREADS
                    if t == 0:
                        for b in range(2):
                            sp.wait_ge(xh_stored[b], 16 * (T // 2))
                        sp.wait_ge(x1_stored, 16 * T)
                        sp.wait_ge(logits_ready, T)
                    if t >= SPREADS:
                        sp.wait_ge(spread_done[q], 16 * CHOSEN * (t // SPREADS))
                    sp.dma_start(spread[q], xh_dram[t * P:(t + 1) * P, :]).then_inc(spread_in[q], 16)
                for b in range(2):
                    load_expert(b, b, [a[n][b] for n in names], (1 + b) * T, b == 0)
                sp.wait_ge(list_ready, 1)
                for q in range(SPREADS):
                    sp.wait_ge(spread_done[q], 16 * CHOSEN * (T // SPREADS))
                for b in range(2):
                    sp.wait_ge(y_stored[b], 16 * (AHEAD + V0 // 2))
                sp.dma_start(acc[:, :, :], base_dram.rearrange("(t p) d -> p t d", p=P)).then_inc(sums_seeded, 16)
                with sp.Fori(1, EXPERTS // 2) as i:
                    for b in range(2):
                        e = 2 * i + b
                        end = sp.value_load(ends_i[0:1, ds(e - 2, 1)], min_val=0, max_val=TILES)
                        load_expert(e, b, [a[n][ds(e, 1)].rearrange("o k n -> (o k) n") for n in names[0:3]]
                                    + [a[n][ds(e, 1)].rearrange("o n -> (o n)") for n in names[3:]],
                                    end + V0)

                for k in range(CHOSEN - 1):
                    at = EXPERTS - CHOSEN + k
                    end = sp.value_load(ends_i[0:1, at:at + 1], min_val=0, max_val=TILES)
                    for b in range(2):
                        sp.wait_ge(y_stored[b], (end + end % 2) * 8 + 16 * (AHEAD + V0 // 2))
                    sp.nop().then_inc(stage_open, 1)
                end = sp.value_load(ends_i[0:1, EXPERTS - 1:EXPERTS], min_val=EXPERTS, max_val=TILES)
                for done, before in ((y_stored, AHEAD + V0 // 2), (x_in, 2 + V0 // 2)):
                    for b in range(2):
                        sp.wait_ge(done[b], (end + end % 2) * 8 + 16 * before)
                    sp.nop().then_inc(stage_open, 1)
                for t in range(T):
                    sp.wait_ge(summed, (CHOSEN - 1) * T - EARLY + t + 1)
                    sp.dma_start(out[t * P:(t + 1) * P, :], acc[:, t, :]).then_inc(out_stored, 16)
                sp.wait_ge(out_stored, 16 * T)

            @block.gpsimd
            def _(pool):
                nc.gpsimd.memset(before[:, :, :], 1.0).then_inc(pool_step, 1)
                nc.gpsimd.memset(before4[:, :, :], 1.0).then_inc(pool_step, 1)
                nc.gpsimd.memset(real[:, :, :], 1.0).then_inc(pool_step, 1)
                nc.gpsimd.memset(earlier_rows[:, :], 1.0).then_inc(pool_step, 1)
                nc.gpsimd.iota(thresholds[:, :], pattern=[[P, T]], base=0, channel_multiplier=0,
                               allow_small_or_imprecise_dtypes=True).then_inc(masks_made, 1)
                nc.gpsimd.iota(tile_ids[:, :], pattern=[[1, TILES + 1]], base=0, channel_multiplier=0,
                               allow_small_or_imprecise_dtypes=True).then_inc(masks_made, 1)
                nc.gpsimd.iota(dump[:, :, :], pattern=[[P, CHOSEN], [0, T]], base=TILES * P, channel_multiplier=1,
                               allow_small_or_imprecise_dtypes=True).then_inc(masks_made, 1)
                pool.wait_ge(pool_step, 4)
                for tile, n in ((before, EXPERTS), (before4, 4)):
                    nc.gpsimd.affine_select(out=tile[:, :, :], in_=tile[:, :, :], compare_op=ALU.is_gt, fill=0.0,
                                            base=0, pattern=[[1, n], [-1, n]], channel_multiplier=0)\
                        .then_inc(masks_made, 1)
                nc.gpsimd.affine_select(out=real[:, :, :], in_=real[:, :, :], compare_op=ALU.is_ge, fill=0.0,
                                        base=NODES - 1, pattern=[[-P, T], [0, EXPERTS]], channel_multiplier=-1)\
                    .then_inc(masks_made, 1)
                nc.gpsimd.affine_select(out=earlier_rows[:, :], in_=earlier_rows[:, :], compare_op=ALU.is_gt,
                                        fill=0.0, base=0, pattern=[[1, P]], channel_multiplier=-1)\
                    .then_inc(masks_made, 1)

                def cut_pieces(b, seen, turns, biases, passes=None, following=None):
                    for q in range(PIECES):
                        r, hi = raw[q % RAWS][:, :], w_hi[:, b, q * D:(q + 1) * D]
                        nc.gpsimd.tensor_scalar(hi, r, 1.0, 1.0, ALU.mult, ALU.mult).then_inc(hi_cut, 1)
                        pool.wait_ge(hi_cut, turns * PIECES + q + 1)
                        if q == KD - 1:
                            pool.wait_ge(bias_in[b], 32 * biases)
                            if passes is not None:
                                pool.wait_ge(down_ready, AHEAD + passes)
                        if q + 1 < PIECES:
                            pool.wait_ge(raw_in[(q + 1) % RAWS], seen[q + 1])
                        else:
                            if not isinstance(turns, int) or turns != 1:
                                pool.wait_ge(bd_in[b], 16 * (biases - b))
                            if following is not None:
                                next_seen, next_passes = following
                                pool.wait_ge(raw_in[0], next_seen)
                                if next_passes is not None:
                                    pool.wait_ge(up_ready, next_passes)
                        nc.gpsimd.tensor_tensor(w_lo[:, b, q * D:(q + 1) * D], r, hi.bitcast(F32),
                                                ALU.subtract).then_inc(piece_cut, 1)

                sizes = [2] * KD + [1] * KI
                per_turn = [sum(sizes[q] for q in range(PIECES) if q % RAWS == slot) for slot in range(RAWS)]

                def transfers(turns):
                    return [16 * (turns * per_turn[q % RAWS] + sum(sizes[q % RAWS:q + 1:RAWS])) for q in range(PIECES)]

                pool.wait_ge(raw_in[0], transfers(0)[0])
                cut_pieces(0, transfers(0), 0, 1, None, (transfers(1)[0], None))
                cut_pieces(1, transfers(1), 1, 1)
                pool.wait_ge(list_ready, 1)
                for t in range(T):
                    q = t % SPREADS
                    pool.wait_ge(spread_in[q], 16 * (t // SPREADS + 1))
                    for k in range(CHOSEN):
                        pool.indirect_dma_start(out=list_dram, out_offset=bass.IndirectOffsetOnAxis(
                            ap=list_i[:, k, t:t + 1], axis=0), in_=spread[q], in_offset=None)\
                            .then_inc(spread_done[q], 16)

                def end_of(e):
                    return pool.value_load(ends_i[0:1, ds(e, 1)], min_val=0, max_val=TILES)

                pool.wait_ge(raw_in[0], transfers(SHARED)[0])
                pool.wait_ge(up_ready, T)
                cut_pieces(0, transfers(SHARED), SHARED, 2, T, (transfers(SHARED + 1)[0], 2 * T))
                cut_pieces(1, transfers(SHARED + 1), SHARED + 1, 2, 2 * T,
                           (transfers(SHARED + 2)[0], end_of(0) + V0))

                def cut_pair(i, final):
                    e = 2 * i
                    n = e + SHARED
                    ends = [end_of(e - 2) + V0, end_of(e - 1) + V0]
                    cut_pieces(0, transfers(n), n, i + 2, ends[0], (transfers(n + 1)[0], ends[1]))
                    cut_pieces(1, transfers(n + 1), n + 1, i + 2, ends[1],
                               None if final else (transfers(n + 2)[0], end_of(e) + V0))

                with pool.Fori(1, EXPERTS // 2 - 1) as i:
                    cut_pair(i, False)
                cut_pair(EXPERTS // 2 - 1, True)

                def gather(k, t, into, arrived):
                    pool.indirect_dma_start(out=into, out_offset=None, in_=y_dram,
                                            in_offset=bass.IndirectOffsetOnAxis(ap=place_i[:, k, t:t + 1], axis=0))\
                        .then_inc(arrived, 16)

                pool.wait_ge(sums_seeded, 16)
                pool.wait_ge(piece_cut, (SHARED + EXPERTS) * PIECES)
                for n in range(EARLY + RAWS - 1):
                    if n < EARLY:
                        if n % T == 0:
                            pool.wait_ge(stage_open, n // T + 1)
                        if n >= RAWS:
                            pool.wait_ge(added, n - RAWS + 1)
                        gather(n // T, n % T, gathered[n % RAWS], gathered_in[n % RAWS])
                    m = n - (RAWS - 1)
                    if m >= 0:
                        k, t, rows = m // T, m % T, gathered[m % RAWS]
                        pool.wait_ge(gathered_in[m % RAWS], 16 * (m // RAWS + 1))
                        nc.gpsimd.tensor_scalar(rows, rows, mix[:, k, t:t + 1], 1.0, ALU.mult, ALU.mult)\
                            .then_inc(weighted, 1)
                        pool.wait_ge(weighted, m + 1)
                        if m >= T:
                            pool.wait_ge(added, m - T + 1)
                        nc.gpsimd.tensor_tensor(acc[:, t, :], rows, acc[:, t, :], ALU.add).then_inc(added, 1)
                pool.wait_ge(added, EARLY)
                for m in range(CHOSEN * T - EARLY):
                    n, q = m + EARLY, m % len(late)
                    if m < FREE:
                        pool.wait_ge(stage_open, n // T + 1)
                    if m == FREE:
                        pool.wait_ge(stage_open, CHOSEN)
                    if m >= len(late):
                        pool.wait_ge(summed, m - len(late) + 1)
                    gather(n // T, n % T, late[q], late_in[q])

            @block.tensor
            def _(pe):
                for s in (turned, down_ready):
                    pe.nop().then_inc(s, AHEAD)
                pe.wait_ge(loaded, 80)

                def turn_out2(t):
                    if t >= 2:
                        pe.wait_ge(o_turned_out, t - 1)
                    nc.tensor.transpose(ps_a[t % 2][:, 0:P], h2[:, t, 0:P], ident[:, :])
                    nc.tensor.transpose(ps_a[t % 2][0:REST, P:2 * P], h2[:, t, P:N2], ident[:, :])\
                        .then_inc(o_turned, 1)

                def lower(t):
                    pe.wait_ge(o_turned_out, t + 1)
                    if t >= 1:
                        pe.wait_ge(x1_ready, t)
                    for k, w, m in ((0, wu_a, P), (1, wu_b, REST)):
                        for n in range(2):
                            last = nc.tensor.matmul(ps_w[:, n, 0:HALF], out2_t[t % 2][0:m, k, :],
                                                    w[:, n * HALF:(n + 1) * HALF], start=(k == 0), stop=(k == 1))
                    last.then_inc(lower_ready, 1)

                def turn_xh(t):
                    pe.wait_ge(xh_ready, t + 1)
                    if t >= 1:
                        pe.wait_ge(xh_t_out, t)
                    for k in range(KD):
                        last = nc.tensor.transpose(ps_b[:, k // 4, (k % 4) * P:(k % 4 + 1) * P],
                                                   y[t % 2][:, k * P:(k + 1) * P], ident[:, :])
                    last.then_inc(xh_turned, 1)

                def route(t):
                    pe.wait_ge(xh_t_out, t + 1)
                    if t >= 1:
                        pe.wait_ge(logits_out, t)
                    for k in range(KD):
                        last = nc.tensor.matmul(ps_l[:, 0:EXPERTS], xh_t[t % 2][:, k, :],
                                                router[:, k, :], start=(k == 0), stop=(k == KD - 1))
                    last.then_inc(logits_ready, 1)

                turn_out2(0)
                for t in range(T + 2):
                    if t + 1 < T:
                        turn_out2(t + 1)
                    if t < T:
                        lower(t)
                    if 1 <= t <= T:
                        turn_xh(t - 1)
                    if t >= 2:
                        route(t - 2)

                def turn(r, b, part, arrived=None):
                    if part == 0:
                        pe.wait_ge(x_in[b], arrived)
                    if isinstance(r, int) and r + part == 0:
                        pe.wait_ge(xh_t_out, T)
                        pe.wait_ge(logits_out, T)
                    else:
                        pe.wait_ge(x_lo_ready, r * 2 + part)
                    for k in range(3):
                        c = 3 * part + k
                        last = nc.tensor.transpose(ps_x[:, k * P:(k + 1) * P], x_row[b][:, c * P:(c + 1) * P],
                                                   ident[:, :])
                    last.then_inc(turned, 1)

                def piece(buffer, w, q, col, n):
                    if isinstance(buffer, int):
                        return w[:, buffer, q * D + col:q * D + col + n]
                    return w[:, ds(buffer, 1), q * D + col:q * D + col + n].rearrange("p o n -> p (o n)")

                def widen(b, buffer, which, ps, ready):
                    for k in range(KD):
                        for m, (rows, w) in enumerate(((x_hi, w_hi), (x_hi, w_lo), (x_lo, w_hi))):
                            last = nc.tensor.matmul(ps[:, 0:I], rows[b][:, k, :], piece(buffer, w, k, which * I, I),
                                                    start=(k == 0 and m == 0), stop=(k == KD - 1 and m == 2))
                    last.then_inc(ready, 1)

                def turn_inner(v, b):
                    pe.wait_ge(inner_ready, AHEAD + v + 1)
                    pe.wait_ge(i_lo_ready, AHEAD + v)
                    for k in range(KI):
                        last = nc.tensor.transpose(ps_i[:, k * P:(k + 1) * P], inner[b][:, k * P:(k + 1) * P],
                                                   ident[:, :])
                    last.then_inc(inner_turned, 1)

                def narrow(v, buffer):
                    pe.wait_ge(i_lo_ready, AHEAD + v + 1)
                    pe.wait_ge(y_ready, AHEAD + v)
                    for k in range(KI):
                        for m, (rows, w) in enumerate(((i_hi, w_hi), (i_hi, w_lo), (i_lo, w_hi))):
                            for c in range(2):
                                last = nc.tensor.matmul(ps_y[:, c, 0:HALF], rows[:, k, :],
                                                        piece(buffer, w, KD + k, c * HALF, HALF),
                                                        start=(k == 0 and m == 0), stop=(k == KI - 1 and m == 2))
                    last.then_inc(down_ready, 1)

                def step(v, b, turns, buffer, following, widened=None, complete=None):
                    other = 1 - b
                    turn(v + 2, b, 0, 16 * turns)
                    if widened is not None:
                        pe.wait_ge(piece_cut, widened)
                    pe.wait_ge(x_lo_ready, 2 * v + 4)
                    pe.wait_ge(inner_ready, AHEAD + v)
                    widen(other, following, 0, ps_g[other], gate_ready)
                    turn(v + 2, b, 1)
                    turn_inner(v, b)
                    widen(other, following, 1, ps_u[other], up_ready)
                    if complete is not None:
                        pe.wait_ge(piece_cut, complete)
                    narrow(v, buffer)

                for r in range(2):
                    turn(r, r, 0, 16)
                    turn(r, r, 1)
                pe.wait_ge(piece_cut, KD)
                pe.wait_ge(x_lo_ready, 2)
                widen(0, 0, 0, ps_g[0], gate_ready)
                widen(0, 0, 1, ps_u[0], up_ready)
                pe.wait_ge(piece_cut, PIECES)
                with pe.Fori(0, COUNT_AT // 2) as i:
                    for b in range(2):
                        step(2 * i + b, b, i + 2, 0, 0)
                pe.wait_ge(masks_made, MASKS)
                pe.wait_ge(chosen_ready, 3)
                flat = chosen[:, :, :].rearrange("p t e -> p (t e)")
                pe.wait_ge(x_lo_ready, 2 * COUNT_AT + 4)
                nc.tensor.matmul(ps_plan[:, 0:TE], earlier_rows[:, :], flat, start=True, stop=True,
                                 skip_group_check=True)
                nc.tensor.matmul(ps_plan[:, TE:2 * TE], ones[:, :], flat, start=True, stop=True,
                                 skip_group_check=True).then_inc(counted, 1)
                pe.wait_ge(counts_taken, 1)
                with pe.Fori(COUNT_AT // 2, T // 2 - 1) as i:
                    for b in range(2):
                        step(2 * i + b, b, i + 2, 0, 0)
                step(T - 2, 0, T // 2 + 1, 0, 0)
                step(T - 1, 1, T // 2 + 1, 0, 1, widened=PIECES + KD)
                pe.wait_ge(piece_cut, 2 * PIECES)
                with pe.Fori(T // 2, T - 1) as i:
                    for b in range(2):
                        step(2 * i + b, b, i + 2, 1, 1)
                step(V0 - 2, 0, T + 1, 1, 1)
                step(V0 - 1, 1, T + 1, 1, 0, widened=WIDENED)

                def expert_of(j):
                    return pe.value_load(tile_expert[0:1, ds(j, 1)], min_val=0, max_val=EXPERTS - 1)

                pe.wait_ge(plan_ready, 1)
                tiles = pe.value_load(ends_i[0:1, EXPERTS - 1:EXPERTS], min_val=EXPERTS, max_val=TILES)
                with pe.Fori(0, PAIRS) as i:
                    with pe.If(tiles > 2 * i):
                        for b in range(2):
                            j = 2 * i + b
                            e, e_next = expert_of(j), expert_of(j + 1)
                            step(j + V0, b, i + (T + 2), e % 2, e_next % 2,
                                 widened=e_next * PIECES + WIDENED, complete=e * PIECES + COMPLETE)

            @block.scalar
            def _(act):
                act.nop().then_inc(i_hi_ready, AHEAD)
                for b in range(2):
                    act.nop().then_inc(y_stored[b], 16 * AHEAD)
                for t in range(T + 2):
                    b = t % 2
                    if t < T:
                        act.wait_ge(o_turned, t + 1)
                        if t >= 2:
                            act.wait_ge(lower_ready, t - 1)
                        nc.scalar.copy(out2_t[b][:, 0, :], ps_a[b][:, 0:P])
                        nc.scalar.copy(out2_t[b][0:REST, 1, :], ps_a[b][0:REST, P:2 * P])\
                            .then_inc(o_turned_out, 1)
                    if t >= 2:
                        act.wait_ge(xh_ready, t - 1)
                        act.dma_start(xh_dram[(t - 2) * P:(t - 1) * P, :], y[b][:, :]).then_inc(xh_stored[b], 16)
                    if 1 <= t <= T:
                        act.wait_ge(var_ready, t)
                        nc.scalar.activation(std_c[:, :], mean_var[:, 1:2], ACT.Sqrt, bias=eps[:, 0:1],
                                             scale=1.0).then_inc(std_ready, 1)
                        act.wait_ge(x1_ready, t)
                        act.dma_start(x1_dram[(t - 1) * P:t * P, :], acc[:, t - 1, :]).then_inc(x1_stored, 16)
                    if t >= 2:
                        act.wait_ge(xh_turned, t - 1)
                        if t >= 4:
                            act.wait_ge(logits_ready, t - 3)
                        nc.scalar.copy(xh_t[b][:, 0:4, :], ps_b[:, 0, 0:512])
                        nc.scalar.copy(xh_t[b][:, 4:KD, :], ps_b[:, 1, 0:256]).then_inc(xh_t_out, 1)
                act.wait_ge(logits_out, T)
                act.wait_ge(x1_stored, 16 * T)
                nc.scalar.activation(scores[:, :, :], logits[:, :, :], ACT.Exp, scale=-1.0).then_inc(exp_ready, 1)
                act.wait_ge(xh_stored[0], 16 * (T // 2))
                act.wait_ge(xh_stored[1], 16 * (T // 2))

                def load_rows(b, dram, at):
                    act.dma_start(x_row[b][:, :], dram[ds(at * P, P), :]).then_inc(x_in[b], 16)

                def round_rows(r, b, part):
                    act.wait_ge(turned, AHEAD + 2 * r + part + 1)
                    nc.scalar.copy(x_hi[b][:, 3 * part:3 * part + 3, :], ps_x[:, 0:I]).then_inc(x_hi_ready, 1)

                def round_inner(v):
                    act.wait_ge(inner_turned, v + 1)
                    act.wait_ge(down_ready, AHEAD + v)
                    nc.scalar.copy(i_hi[:, :, :], ps_i[:, 0:I]).then_inc(i_hi_ready, 1)

                def silu(v):
                    act.wait_ge(gate_biased, v + 1)
                    nc.scalar.activation(gate, gate, ACT.Silu).then_inc(silu_ready, 1)

                def store(v, b, dram, at):
                    act.wait_ge(y_ready, AHEAD + v + 1)
                    act.dma_start(dram[ds(at * P, P), :], y[b][:, :]).then_inc(y_stored[b], 16)

                def load_base(b, dram, at, stores):
                    act.wait_ge(y_stored[b], 16 * (AHEAD + stores))
                    act.dma_start(y[b][:, :], dram[ds(at * P, P), :]).then_inc(base_in[b], 16)

                def step(v, b, rows, result, base=None):
                    act.wait_ge(up_ready, v + 1)
                    round_rows(v + 2, b, 0)
                    round_rows(v + 2, b, 1)
                    load_rows(b, *rows)
                    round_inner(v)
                    silu(v + 1)
                    if base is not None:
                        load_base(1 - b, *base)
                    store(v, b, *result)

                for b in range(2):
                    load_rows(b, xh_dram, b)
                load_base(0, x1_dram, 0, 0)
                for b in range(2):
                    round_rows(b, b, 0)
                    round_rows(b, b, 1)
                    load_rows(b, xh_dram, 2 + b)
                silu(0)
                with act.Fori(0, (T - 4) // 2) as i:
                    for b in range(2):
                        v = 2 * i + b
                        step(v, b, (xh_dram, v + 4), (base_dram, v), (x1_dram, v + 1, i + b))
                for v in range(T - 4, T):
                    base = (x1_dram, v + 1, (v + 1) // 2) if v + 1 < T else (base_dram, 0, T // 2)
                    step(v, v % 2, (xh_dram, v + 4 - T), (base_dram, v), base)
                with act.Fori(0, (T - 4) // 2) as i:
                    for b in range(2):
                        t = 2 * i + b
                        step(t + T, b, (xh_dram, t + 4), (base_dram, t), (base_dram, t + 1, i + (b + T // 2)))
                for q in range(SPREADS):
                    act.wait_ge(spread_done[q], 16 * CHOSEN * (T // SPREADS))
                for t in range(T - 4, T):
                    v = T + t
                    step(v, v % 2, (list_dram, t + 4 - T), (base_dram, t),
                         (base_dram, t + 1, (v + 1) // 2) if t + 1 < T else None)
                tiles = act.value_load(ends_i[0:1, EXPERTS - 1:EXPERTS], min_val=EXPERTS, max_val=TILES)
                with act.Fori(0, PAIRS) as i:
                    with act.If(tiles > 2 * i):
                        for b in range(2):
                            j = 2 * i + b
                            step(j + V0, b, (list_dram, j + 4), (y_dram, j))

            @block.vector
            def _(dve):
                for s in (inner_ready, y_ready, i_lo_ready):
                    dve.nop().then_inc(s, AHEAD)
                chain = Count()

                def norm(t):
                    x = acc[:, t, :]
                    for n in range(2):
                        last = nc.vector.bn_stats(stats[:, n, :], x[:, n * HALF:(n + 1) * HALF])
                    last.then_inc(dve_step, 1)
                    dve.wait_ge(dve_step, chain.up())
                    nc.vector.bn_aggr(mean_var[:, :], stats[:, :, :]).then_inc(var_ready, 1)
                    dve.wait_ge(std_ready, t + 1)
                    nc.vector.reciprocal(rstd[:, :], std_c[:, :]).then_inc(dve_step, 1)
                    dve.wait_ge(dve_step, chain.up())
                    if t >= 2:
                        dve.wait_ge(xh_stored[t % 2], 16 * (t // 2))
                        dve.wait_ge(xh_turned, t - 1)
                    nc.vector.tensor_scalar(y[t % 2][:, :], x, mean_var[:, 0:1], rstd[:, 0:1], ALU.subtract,
                                            ALU.mult).then_inc(xh_ready, 1)

                for t in range(T + 2):
                    if t < T:
                        dve.wait_ge(lower_ready, t + 1)
                        x = acc[:, t, :].rearrange("p (n c) -> p n c", n=2)
                        nc.vector.tensor_tensor(x, ps_w[:, :, 0:HALF], x, ALU.add).then_inc(x1_ready, 1)
                        dve.wait_ge(x1_ready, t + 1)
                        norm(t)
                    if t >= 2:
                        if t == 2:
                            dve.wait_ge(loaded, 80)
                        dve.wait_ge(logits_ready, t - 1)
                        nc.vector.tensor_tensor(logits[:, t - 2, :], ps_l[:, 0:EXPERTS], rb_row[:, :],
                                                ALU.add).then_inc(logits_out, 1)

                def over_tiles(row):
                    return row.unsqueeze(1).to_broadcast([P, T, EXPERTS])

                def done(ins, by=1):
                    ins.then_inc(dve_step, 1)
                    dve.wait_ge(dve_step, chain.up())

                V = nc.vector

                def ranks(values, n, first, out, tiles=T):
                    gt, eq = (x[:, 0:tiles, :, :].rearrange("p t i j -> p t (i j)")[:, :, 0:n * n]
                              .rearrange("p t (i j) -> p t i j", i=n) for x in (ahead, tied))
                    mine = values.unsqueeze(3).to_broadcast([P, tiles, n, n])
                    other = values.unsqueeze(2).to_broadcast([P, tiles, n, n])
                    V.tensor_tensor(gt, other, mine, ALU.is_gt)
                    done(V.tensor_tensor(eq, other, mine, ALU.is_equal))
                    done(V.tensor_tensor(eq, eq, first.unsqueeze(1).to_broadcast([P, tiles, n, n]), ALU.mult))
                    done(V.tensor_tensor(gt, gt, eq, ALU.add))
                    done(V.tensor_reduce(out, gt, AX_X, ALU.add))

                def score_groups():
                    dve.wait_ge(masks_made, MASKS)
                    dve.wait_ge(exp_ready, 1)
                    done(V.tensor_scalar(scores[:, :, :], scores[:, :, :], 1.0, None, ALU.add))
                    done(V.reciprocal(scores[:, :, :], scores[:, :, :]))
                    done(V.tensor_tensor(biased[:, :, :], scores[:, :, :], over_tiles(cb_row[:, :]), ALU.add))
                    by_pair = biased[:, :, :].rearrange("p t (g q r) -> p (t g q) r", g=4, q=2)
                    hi, lo = (x[:, :, :, :].rearrange("p t g q -> p (t g q)") for x in (pair_hi, pair_lo))
                    V.tensor_tensor(hi, by_pair[:, :, 0], by_pair[:, :, 1], ALU.max)
                    done(V.tensor_tensor(lo, by_pair[:, :, 0], by_pair[:, :, 1], ALU.min))
                    V.tensor_tensor(group_score[:, :, :], pair_hi[:, :, :, 0], pair_hi[:, :, :, 1], ALU.max)
                    V.tensor_tensor(group_next[:, :, :], pair_hi[:, :, :, 0], pair_hi[:, :, :, 1], ALU.min)
                    done(V.tensor_tensor(group_kept[:, :, :], pair_lo[:, :, :, 0], pair_lo[:, :, :, 1], ALU.max))
                    done(V.tensor_tensor(group_next[:, :, :], group_next[:, :, :], group_kept[:, :, :], ALU.max))
                    done(V.tensor_tensor(group_score[:, :, :], group_score[:, :, :], group_next[:, :, :], ALU.add))

                def keep_groups():
                    ranks(group_score[:, :, :], 4, before4[:, :, :], group_next[:, :, :])
                    done(V.tensor_scalar(group_kept[:, :, :], group_next[:, :, :], 2.0, None, ALU.is_lt))
                    done(V.tensor_tensor(biased[:, :, :].rearrange("p t (g r) -> p t g r", g=4),
                                         biased[:, :, :].rearrange("p t (g r) -> p t g r", g=4),
                                         group_kept[:, :, :].unsqueeze(3).to_broadcast([P, T, 4, 4]), ALU.mult))

                parts = [slice(0, 4), slice(4, 7), slice(7, T)]

                def choose(n):
                    p = parts[n]
                    ranks(biased[:, p, :], EXPERTS, before[:, :, :], rank[:, p, :], p.stop - p.start)
                    V.scalar_tensor_tensor(out=chosen[:, p, :], in0=rank[:, p, :], scalar=float(CHOSEN),
                                           in1=real[:, p, :], op0=ALU.is_lt, op1=ALU.mult).then_inc(chosen_ready, 1)
                    dve.wait_ge(chosen_ready, n + 1)

                def weigh():
                    done(V.tensor_tensor(scores[:, :, :], scores[:, :, :], chosen[:, :, :], ALU.mult))
                    done(V.tensor_reduce(total[:, :], scores[:, :, :], AX_X, ALU.add))
                    done(V.tensor_scalar(total[:, :], total[:, :], 1e-20, None, ALU.add))
                    done(V.reciprocal(total[:, :], total[:, :]))
                    done(V.scalar_tensor_tensor(out=scores[:, :, :], in0=scores[:, :, :], scalar=SCALE,
                                                in1=total[:, :].unsqueeze(2).to_broadcast([P, T, EXPERTS]),
                                                op0=ALU.mult, op1=ALU.mult))
                def number(n):
                    p = parts[n]
                    shape = [P, p.stop - p.start, EXPERTS, EXPERTS]
                    done(V.tensor_tensor(tied[:, p, :, :], chosen[:, p, :].unsqueeze(2).to_broadcast(shape),
                                         before[:, :, :].unsqueeze(1).to_broadcast(shape), ALU.mult))
                    done(V.tensor_reduce(nth[:, p, :], tied[:, p, :, :], AX_X, ALU.add))

                def count_tiles():
                    done(V.memset(earlier[:, 0, :], 0.0))
                    for t in range(T):
                        done(V.tensor_tensor(earlier[:, t + 1, :], tallies[:, 1, t, :], earlier[:, t, :], ALU.add))
                    done(V.tensor_tensor(filled[:, :, :], earlier[:, T, :].unsqueeze(2).to_broadcast([P, EXPERTS, T]),
                                         thresholds[:, :].unsqueeze(1).to_broadcast([P, EXPERTS, T]), ALU.is_gt))
                    done(V.tensor_reduce(n_tiles[:, :], filled[:, :, :], AX_X, ALU.add))
                    done(V.tensor_scalar(n_tiles[:, :], n_tiles[:, :], 1.0, None, ALU.max))
                    done(V.tensor_tensor(ahead[:, 0, :, :], n_tiles[:, :].unsqueeze(1).to_broadcast([P, EXPERTS, EXPERTS]),
                                         before[:, :, :], ALU.mult))
                    done(V.tensor_reduce(starts[:, :], ahead[:, 0, :, :], AX_X, ALU.add))

                def lay_out():
                    done(V.tensor_tensor(ends[:, :], starts[:, :], n_tiles[:, :], ALU.add))
                    V.tensor_copy(ends_i[:, :], ends[0:1, :])
                    done(V.tensor_tensor(passed[:, :, :], tile_ids[:, :].unsqueeze(2).to_broadcast([P, TILES + 1, EXPERTS]),
                                         ends[:, :].unsqueeze(1).to_broadcast([P, TILES + 1, EXPERTS]), ALU.is_ge))
                    done(V.tensor_reduce(tile_f[:, :], passed[:, :, :], AX_X, ALU.add))
                    done(V.tensor_scalar(tile_f[:, :], tile_f[:, :], float(EXPERTS - 1), None, ALU.min))
                    V.tensor_copy(tile_expert[:, :], tile_f[0:1, :]).then_inc(plan_ready, 1)
                    done(V.tensor_tensor(place[:, :, :], tallies[:, 0, :, :], earlier[:, 0:T, :], ALU.add))
                    done(V.scalar_tensor_tensor(out=place[:, :, :], in0=over_tiles(starts[:, :]), scalar=float(P),
                                                in1=place[:, :, :], op0=ALU.mult, op1=ALU.add))

                def pick(k):
                    done(V.scalar_tensor_tensor(out=mask[:, :, :], in0=nth[:, :, :], scalar=float(k),
                                                in1=chosen[:, :, :], op0=ALU.is_equal, op1=ALU.mult))
                    done(V.tensor_tensor(picked[:, :, :], mask[:, :, :], scores[:, :, :], ALU.mult))
                    done(V.tensor_reduce(mix[:, k, :], picked[:, :, :], AX_X, ALU.add))
                    done(V.tensor_tensor(picked[:, :, :], mask[:, :, :], place[:, :, :], ALU.mult))
                    done(V.tensor_reduce(place_k[:, k, :], picked[:, :, :], AX_X, ALU.add))

                def list_places():
                    wide_dump = dump[:, :, :]
                    wide_real = real[:, :, 0].unsqueeze(1).to_broadcast([P, CHOSEN, T])
                    done(V.tensor_tensor(list_k[:, :, :], place_k[:, :, :], wide_dump, ALU.subtract))
                    done(V.tensor_tensor(list_k[:, :, :], list_k[:, :, :], wide_real, ALU.mult))
                    done(V.tensor_tensor(list_k[:, :, :], list_k[:, :, :], wide_dump, ALU.add))
                    V.tensor_copy(place_i[:, :, :], place_k[:, :, :])
                    V.tensor_copy(list_i[:, :, :], list_k[:, :, :]).then_inc(list_ready, 1)

                def rest_of_rows(r, b, part):
                    dve.wait_ge(x_hi_ready, 2 * r + part + 1)
                    V.tensor_tensor(x_lo[b][:, 3 * part:3 * part + 3, :], ps_x[:, 0:I].rearrange("p (k n) -> p k n", k=3),
                                    x_hi[b][:, 3 * part:3 * part + 3, :].bitcast(F32), ALU.subtract)\
                        .then_inc(x_lo_ready, 1)

                def rest_of_inner(v):
                    dve.wait_ge(i_hi_ready, AHEAD + v + 1)
                    V.tensor_tensor(i_lo[:, :, :], ps_i[:, 0:I].rearrange("p (k n) -> p k n", k=KI),
                                    i_hi[:, :, :].bitcast(F32), ALU.subtract).then_inc(i_lo_ready, 1)

                def bias_of(rows, buffer, n):
                    return rows[:, ds(buffer * n, n)]

                def bias_gate(v, b, buffer):
                    dve.wait_ge(gate_ready, v + 1)
                    V.tensor_tensor(gate, ps_g[b][:, 0:I], bias_of(bg, buffer, I), ALU.add).then_inc(gate_biased, 1)

                def inside(v, b, buffer):
                    dve.wait_ge(up_ready, v + 1)
                    V.tensor_tensor(up, ps_u[b][:, 0:I], bias_of(bu, buffer, I), ALU.add).then_inc(up_biased, 1)
                    dve.wait_ge(silu_ready, v + 1)
                    dve.wait_ge(up_biased, v + 1)
                    V.tensor_tensor(inner[b][:, :], gate, up, ALU.mult).then_inc(inner_ready, 1)
                    dve.wait_ge(inner_ready, AHEAD + v + 1)

                def step(v, b, following, finish, widened=None):
                    rest_of_rows(v + 2, b, 0)
                    if widened is not None:
                        dve.wait_ge(piece_cut, widened)
                    bias_gate(v + 1, 1 - b, following)
                    rest_of_rows(v + 2, b, 1)
                    rest_of_inner(v)
                    inside(v + 1, 1 - b, following)
                    finish()

                def add_base(v, b, count, bias):
                    rows = y[b][:, :].rearrange("p (n c) -> p n c", n=2)
                    dve.wait_ge(base_in[b], 16 * count)
                    if bias:
                        done(V.tensor_tensor(rows, bias_of(bd, 0, D).rearrange("p (n c) -> p n c", n=2), rows, ALU.add))
                    dve.wait_ge(down_ready, AHEAD + v + 1)
                    V.tensor_tensor(rows, ps_y[:, :, 0:HALF], rows, ALU.add).then_inc(y_ready, 1)

                def add_bias(v, b, buffer, stores):
                    dve.wait_ge(down_ready, AHEAD + v + 1)
                    dve.wait_ge(y_stored[b], 16 * stores)
                    V.tensor_tensor(y[b][:, :].rearrange("p (n c) -> p n c", n=2), ps_y[:, :, 0:HALF],
                                    bias_of(bd, buffer, D).rearrange("p (n c) -> p n c", n=2), ALU.add)\
                        .then_inc(y_ready, 1)

                def plan(v):
                    if v == 0:
                        score_groups()
                        keep_groups()
                    elif v < COUNT_AT:
                        choose(v - 1)
                    elif v == COUNT_AT:
                        count_tiles()
                    elif v == COUNT_AT + 1:
                        lay_out()
                        weigh()
                    elif v == COUNT_AT + 2:
                        number(0)
                        number(1)
                    elif v == COUNT_AT + 3:
                        number(2)
                        pick(0)
                    elif v == COUNT_AT + 4:
                        for k in range(1, CHOSEN):
                            pick(k)
                        list_places()

                dve.wait_ge(exp_ready, 1)
                for r in range(2):
                    rest_of_rows(r, r, 0)
                    rest_of_rows(r, r, 1)
                dve.wait_ge(piece_cut, KD)
                bias_gate(0, 0, 0)
                inside(0, 0, 0)
                for v in range(T):
                    if v == COUNT_AT:
                        dve.wait_ge(counted, 1)
                        V.tensor_copy(tallies[:, :, :, :].rearrange("p w t e -> p (w t e)"), ps_plan)\
                            .then_inc(counts_taken, 1)
                        dve.wait_ge(counts_taken, 1)
                    last = v == T - 1
                    step(v, v % 2, int(last), lambda: add_base(v, v % 2, v // 2 + 1, True),
                         widened=PIECES + KD if last else None)
                    plan(v)
                with dve.Fori(T // 2, T - 1) as i:
                    for b in range(2):
                        step(2 * i + b, b, 1, lambda: add_base(2 * i + b, b, i + 1, False))
                step(V0 - 2, 0, 1, lambda: add_base(V0 - 2, 0, T, False))
                step(V0 - 1, 1, 0, lambda: add_base(V0 - 1, 1, T, False), widened=WIDENED)

                def expert_of(j):
                    return dve.value_load(tile_expert[0:1, ds(j, 1)], min_val=0, max_val=EXPERTS - 1)

                dve.wait_ge(plan_ready, 1)
                tiles = dve.value_load(ends_i[0:1, EXPERTS - 1:EXPERTS], min_val=EXPERTS, max_val=TILES)
                with dve.Fori(0, PAIRS) as i:
                    with dve.If(tiles > 2 * i):
                        for b in range(2):
                            j = 2 * i + b
                            e, e_next = expert_of(j), expert_of(j + 1)
                            step(j + V0, b, e_next % 2, lambda: add_bias(j + V0, b, e % 2, i + (T + AHEAD)),
                                 widened=e_next * PIECES + WIDENED)
                dve.wait_ge(added, EARLY)
                for m in range(CHOSEN * T - EARLY):
                    n, q = m + EARLY, m % len(late)
                    k, t = n // T, n % T
                    dve.wait_ge(late_in[q], 16 * (m // len(late) + 1))
                    if m >= T:
                        dve.wait_ge(summed, m - T + 1)
                    V.scalar_tensor_tensor(out=acc[:, t, :], in0=late[q], scalar=mix[:, k, t:t + 1],
                                           in1=acc[:, t, :], op0=ALU.mult, op1=ALU.add).then_inc(summed, 1)


def program(nc, a, out):
    ctx = ExitStack()
    with ctx:
        keep = {}

        def held(stack, name, shape, dt=F32):
            keep[name] = stack.enter_context(nc.sbuf_tensor(name, shape, dt))

        held(ctx, "ident", [P, P])
        held(ctx, "ones", [P, P])
        held(ctx, "eps", [P, 1])
        held(ctx, "place_i", [P, CHOSEN, T], I32)
        held(ctx, "mix", [P, CHOSEN, T])
        held(ctx, "tile_expert", [1, TILES + 1], I32)
        held(ctx, "ends_i", [1, EXPERTS], I32)
        for name, rows in (("xh_dram", NP), ("x1_dram", NP), ("base_dram", NP), ("y_dram", TILES * P),
                           ("list_dram", (TILES + CHOSEN) * P)):
            keep[name] = nc.dram_tensor(name, (rows, D), F32).ap()
        with ExitStack() as tokens:
            held(tokens, "acc", [P, T, D])
            held(tokens, "h2", [P, T, H2 * (C2 + 2)])
            with ExitStack() as graph:
                held(graph, "h1", [P, T, H1 * (C1 + 2)])
                held(graph, "counts", [P, T, NP], U16)
                for name, heads in (("s_src1", H1), ("s_dst1", H1), ("s_src2", H2), ("s_dst2", H2)):
                    held(graph, name, [P, heads * T])
                edges_and_projection(nc, a, keep)
                held(graph, "no_edge", [P, T, NP], BF16)
                held(graph, "w2", [P, KD, H2 * C2])
                held(graph, "a_src2", [P, H2 * C2])
                held(graph, "a_dst2", [P, H2 * C2])
                keep["w2_loaded"] = graph.enter_context(nc.semaphore("w2_loaded"))
                attention(nc, a, keep, 1, H1, C1)
                second_projection(nc, a, keep)
                attention(nc, a, keep, 2, H2, C2)
            network(nc, a, keep, out)


def kernel(**inputs):
    import numpy as _np
    import concourse.bacc as _bacc
    from concourse import mybir as _mybir
    from concourse.bass_utils import run_bass_kernel_spmd as _run

    given = {name.replace("L0_gnn_", "").replace("L0_ffn_", ""): _np.asarray(v) for name, v in inputs.items()}
    spare = LISTED * CHUNK * P - EDGES

    def grouped(edges, filler):
        padded = _np.concatenate([edges, _np.full(spare, filler, edges.dtype)])
        return padded.reshape(LISTED, P, CHUNK).transpose(1, 0, 2).reshape(P, LISTED * CHUNK)

    given["src"] = grouped(given["src"], PAD_SRC)
    given["dst"] = grouped(given["dst"], NODES - 1)
    given["x"] = _np.concatenate([given["x"], _np.zeros((NP + P - NODES, D), given["x"].dtype)])
    given["router_w"] = given["router_w"].T
    for name in ("a_src1", "a_dst1", "a_src2", "a_dst2"):
        given[name] = given[name].reshape(-1)

    nc = _bacc.Bacc("TRN2", target_bir_lowering=False, num_devices=1)
    arrays, a = {}, {}
    for name, value in given.items():
        value = _np.ascontiguousarray(value)
        arrays[f"in_{name}"] = value
        a[name] = nc.dram_tensor(f"in_{name}", value.shape, _mybir.dt.from_np(value.dtype), kind="ExternalInput").ap()
    out = nc.dram_tensor("out", (NP, D), F32, kind="ExternalOutput").ap()
    program(nc, a, out)
    r = _run(nc, [arrays], core_ids=[0])
    return r.results[0]["out"][:NODES]
```
